# Optimizing a Trainium2 kernel written in Bass

```python
import numpy as np
import jax
import jax.numpy as jnp

def _softmax(x, axis=-1):
    return jax.nn.softmax(x, axis=axis)

def _gelu(x):
    return jax.nn.gelu(x, approximate=True)

def _silu(x):
    return jax.nn.silu(x)

def _sigmoid(x):
    return jax.nn.sigmoid(x)

def _layernorm(x, axis=-1, eps=1e-05):
    m = jnp.mean(x, axis=axis, keepdims=True)
    v = jnp.var(x, axis=axis, keepdims=True)
    return (x - m) / jnp.sqrt(v + eps)

def _scatter_add(tgt, idx, src, axis=0):
    return tgt.at[idx].add(src)

def _segment_sum(src, seg, n):
    return jax.ops.segment_sum(src, seg, n)
kernel_name = 'mk_gnn_resnorm_d2_gnn_r8_ada28f'

def setup_inputs(seed: int=0):
    np.random.seed(seed)
    _w = jnp.asarray

    def _rec_inputs():
        import jax
        import jax.numpy as jnp
        _gk = jax.random.key(seed)
        x = -0.0005121 + 1.001 * jax.random.normal(jax.random.fold_in(_gk, 1), (6250, 160), jnp.float32)
        _s = jax.random.randint(jax.random.fold_in(_gk, 2), (100000,), 0, 6250, jnp.int32)
        _d = jax.random.randint(jax.random.fold_in(_gk, 3), (100000,), 0, 6250, jnp.int32)
        _loop = jnp.arange(6250, dtype=jnp.int32)
        src = jnp.concatenate([_s, _d, _loop])
        dst = jnp.concatenate([_d, _s, _loop])
        _o = jnp.argsort(dst, stable=True)
        src = src[_o]
        dst = dst[_o]
        edge_attr_16 = jax.random.uniform(jax.random.fold_in(_gk, 12), (206250, 16), jnp.float32, 0.0, 1)
        edge_attr_4 = 0.000898722 + 1.00012 * jax.random.normal(jax.random.fold_in(_gk, 13), (206250, 4), jnp.float32)
        edge_attr_64 = 0.000152336 + 1.00009 * jax.random.normal(jax.random.fold_in(_gk, 14), (206250, 64), jnp.float32)
        return (x, src, dst, edge_attr_16, edge_attr_4, edge_attr_64)
    x, src, dst, edge_attr_16, edge_attr_4, edge_attr_64 = _rec_inputs()

    def _L0_gnn_setup():
        import jax, jax.numpy as jnp
        import numpy as np
        N, E = (2500, 40000)
        CS, CV = (64, 32)
        AS_, AV, H = (16, 8, 4)
        NB = 16
        SQRT3 = 1.7320508075688772
        SQRT2 = 1.4142135623730951
        EPS = 1e-05

        def _cg_tp(s, v, y0, y1, w_ss, w_sv, w_vs, w_vv0, w_vv1):
            out_s = jnp.concatenate([w_ss * s * y0[:, None], w_vv0 * (jnp.einsum('eci,ei->ec', v, y1) / SQRT3)], axis=-1)
            out_v = jnp.concatenate([(w_sv * s)[:, :, None] * y1[:, None, :], (w_vs * jnp.ones_like(v[..., 0]))[..., None] * v * y0[:, None, None], (w_vv1 * jnp.ones_like(v[..., 0]))[..., None] * (jnp.cross(v, y1[:, None, :]) / SQRT2)], axis=1)
            return (out_s, out_v)

        def _equiv_layernorm(s, v, gamma_s, beta_s, gamma_v):
            mu = jnp.mean(s, axis=-1, keepdims=True)
            var = jnp.var(s, axis=-1, keepdims=True)
            s_n = (s - mu) * jax.lax.rsqrt(var + EPS) * gamma_s + beta_s
            rms = jnp.sqrt(jnp.mean(jnp.sum(v * v, axis=-1), axis=-1, keepdims=True) + EPS)
            v_n = v / rms[..., None] * gamma_v[None, :, None]
            return (s_n, v_n)
        key = jax.random.key(seed)
        ks = jax.random.split(key, 26)

        def rn(k, shape, fan):
            return jax.random.normal(k, shape, jnp.float32) / np.sqrt(fan)
        D1S, D1V = (CS + CV, CS + 2 * CV)
        WN = 2 * CS + 3 * CV
        inp = {'node': jax.random.normal(ks[0], (N, CS + 3 * CV), jnp.float32), 'edge_index': jax.random.randint(ks[1], (2, E), 0, N, jnp.int64 if jax.config.jax_enable_x64 else jnp.int32), 'rbf': jax.random.uniform(ks[2], (E, NB), jnp.float32), 'rsh': jax.random.normal(ks[3], (E, 4), jnp.float32), 'gamma_s': jnp.ones((CS,), jnp.float32), 'beta_s': jnp.zeros((CS,), jnp.float32), 'gamma_v': jnp.ones((CV,), jnp.float32), 'Ws_src': rn(ks[4], (CS, CS), CS), 'Wv_src': rn(ks[5], (CV, CV), CV), 'Ws_dst': rn(ks[6], (CS, CS), CS), 'Wv_dst': rn(ks[7], (CV, CV), CV), 'W_rbf': rn(ks[8], (NB, WN), NB), 'W_alpha': rn(ks[9], (D1S, H * AS_), D1S), 'alpha_dot': rn(ks[10], (1, H, AS_), AS_), 'Ws_val': rn(ks[11], (D1S, CS), D1S), 'Wv_val': rn(ks[12], (D1V, CV), D1V), 'Wg': rn(ks[13], (CS, CV), CS), 'w2_ss': rn(ks[14], (CS,), 1), 'w2_sv': rn(ks[15], (CS,), 1), 'w2_vs': rn(ks[16], (CV,), 1), 'w2_vv0': rn(ks[17], (CV,), 1), 'w2_vv1': rn(ks[18], (CV,), 1), 'Ws_vlin': rn(ks[19], (D1S, H * AS_), D1S), 'Wv_vlin': rn(ks[20], (D1V, H * AV), D1V), 'Wps': rn(ks[21], (H * AS_, CS), H * AS_), 'Wpv': rn(ks[22], (H * AV, CV), H * AV)}
        return inp
    _L0_gnn_all = _L0_gnn_setup()
    _L0_gnn_in = {k: v for k, v in _L0_gnn_all.items() if k in ('gamma_s', 'beta_s', 'gamma_v', 'Ws_src', 'Wv_src', 'Ws_dst', 'Wv_dst', 'W_rbf', 'W_alpha', 'alpha_dot', 'Ws_val', 'Wv_val', 'Wg', 'w2_ss', 'w2_sv', 'w2_vs', 'w2_vv0', 'w2_vv1', 'Ws_vlin', 'Wv_vlin', 'Wps', 'Wpv')}
    del _L0_gnn_all

    def _L1_gnn_setup():
        import jax, jax.numpy as jnp
        import numpy as np
        N = 6250
        E = 62500
        MUL0 = 64
        MUL1 = 32
        DIM_KEY = 64
        WEIGHT_NUMEL = 64 + 64 + 32 + 32 + 32

        def _irreps_linear(s, v, w0, w1):
            so = s @ w0 * w0.shape[0] ** (-0.5)
            vo = jnp.einsum('nui,uv->nvi', v, w1) * w1.shape[0] ** (-0.5)
            return (so, vo)
        key = jax.random.key(seed)
        ks = jax.random.split(key, 12)
        x = jax.random.normal(ks[0], (N, MUL0 + 3 * MUL1), dtype=jnp.float32)
        edge_src = jax.random.randint(ks[1], (E,), 0, N, dtype=jnp.int32)
        edge_dst = jax.random.randint(ks[2], (E,), 0, N, dtype=jnp.int32)
        edge_query = jax.random.normal(ks[3], (E, DIM_KEY), dtype=jnp.float32)
        edge_sh = jax.random.normal(ks[4], (E, 4), dtype=jnp.float32)
        si_w0 = jax.random.normal(ks[5], (MUL0, MUL0), dtype=jnp.float32)
        si_w1 = jax.random.normal(ks[6], (MUL1, MUL1), dtype=jnp.float32)
        lin1_w0 = jax.random.normal(ks[7], (MUL0, MUL0), dtype=jnp.float32)
        lin1_w1 = jax.random.normal(ks[8], (MUL1, MUL1), dtype=jnp.float32)
        tp_weight = jax.random.normal(ks[9], (DIM_KEY, WEIGHT_NUMEL), dtype=jnp.float32)
        lin2_w0 = jax.random.normal(ks[10], (MUL0 + MUL1, MUL0), dtype=jnp.float32)
        lin2_w1 = jax.random.normal(ks[11], (MUL0 + MUL1, MUL1), dtype=jnp.float32)
        return {'x': x, 'edge_src': edge_src, 'edge_dst': edge_dst, 'edge_query': edge_query, 'edge_sh': edge_sh, 'si_w0': si_w0, 'si_w1': si_w1, 'lin1_w0': lin1_w0, 'lin1_w1': lin1_w1, 'tp_weight': tp_weight, 'lin2_w0': lin2_w0, 'lin2_w1': lin2_w1}
    _L1_gnn_all = _L1_gnn_setup()
    _L1_gnn_in = {k: v for k, v in _L1_gnn_all.items() if k in ('si_w0', 'si_w1', 'lin1_w0', 'lin1_w1', 'tp_weight', 'lin2_w0', 'lin2_w1')}
    del _L1_gnn_all
    return {'x': x, 'src': src, 'dst': dst, 'edge_attr_16': edge_attr_16, 'edge_attr_4': edge_attr_4, 'edge_attr_64': edge_attr_64, 'L0_gnn_gamma_s': _L0_gnn_in['gamma_s'], 'L0_gnn_beta_s': _L0_gnn_in['beta_s'], 'L0_gnn_gamma_v': _L0_gnn_in['gamma_v'], 'L0_gnn_Ws_src': _L0_gnn_in['Ws_src'], 'L0_gnn_Wv_src': _L0_gnn_in['Wv_src'], 'L0_gnn_Ws_dst': _L0_gnn_in['Ws_dst'], 'L0_gnn_Wv_dst': _L0_gnn_in['Wv_dst'], 'L0_gnn_W_rbf': _L0_gnn_in['W_rbf'], 'L0_gnn_W_alpha': _L0_gnn_in['W_alpha'], 'L0_gnn_alpha_dot': _L0_gnn_in['alpha_dot'], 'L0_gnn_Ws_val': _L0_gnn_in['Ws_val'], 'L0_gnn_Wv_val': _L0_gnn_in['Wv_val'], 'L0_gnn_Wg': _L0_gnn_in['Wg'], 'L0_gnn_w2_ss': _L0_gnn_in['w2_ss'], 'L0_gnn_w2_sv': _L0_gnn_in['w2_sv'], 'L0_gnn_w2_vs': _L0_gnn_in['w2_vs'], 'L0_gnn_w2_vv0': _L0_gnn_in['w2_vv0'], 'L0_gnn_w2_vv1': _L0_gnn_in['w2_vv1'], 'L0_gnn_Ws_vlin': _L0_gnn_in['Ws_vlin'], 'L0_gnn_Wv_vlin': _L0_gnn_in['Wv_vlin'], 'L0_gnn_Wps': _L0_gnn_in['Wps'], 'L0_gnn_Wpv': _L0_gnn_in['Wpv'], 'L1_gnn_si_w0': _L1_gnn_in['si_w0'], 'L1_gnn_si_w1': _L1_gnn_in['si_w1'], 'L1_gnn_lin1_w0': _L1_gnn_in['lin1_w0'], 'L1_gnn_lin1_w1': _L1_gnn_in['lin1_w1'], 'L1_gnn_tp_weight': _L1_gnn_in['tp_weight'], 'L1_gnn_lin2_w0': _L1_gnn_in['lin2_w0'], 'L1_gnn_lin2_w1': _L1_gnn_in['lin2_w1']}

def reference(x, src, dst, edge_attr_16, edge_attr_4, edge_attr_64, L0_gnn_gamma_s, L0_gnn_beta_s, L0_gnn_gamma_v, L0_gnn_Ws_src, L0_gnn_Wv_src, L0_gnn_Ws_dst, L0_gnn_Wv_dst, L0_gnn_W_rbf, L0_gnn_W_alpha, L0_gnn_alpha_dot, L0_gnn_Ws_val, L0_gnn_Wv_val, L0_gnn_Wg, L0_gnn_w2_ss, L0_gnn_w2_sv, L0_gnn_w2_vs, L0_gnn_w2_vv0, L0_gnn_w2_vv1, L0_gnn_Ws_vlin, L0_gnn_Wv_vlin, L0_gnn_Wps, L0_gnn_Wpv, L1_gnn_si_w0, L1_gnn_si_w1, L1_gnn_lin1_w0, L1_gnn_lin1_w1, L1_gnn_tp_weight, L1_gnn_lin2_w0, L1_gnn_lin2_w1):
    import jax
    import jax.numpy as jnp

    def _L0_gnn_ref(node, rbf, rsh, gamma_s, beta_s, gamma_v, Ws_src, Wv_src, Ws_dst, Wv_dst, W_rbf, W_alpha, alpha_dot, Ws_val, Wv_val, Wg, w2_ss, w2_sv, w2_vs, w2_vv0, w2_vv1, Ws_vlin, Wv_vlin, Wps, Wpv, edge_index):
        import jax, jax.numpy as jnp
        import numpy as np
        N, E = (2500, 40000)
        CS, CV = (64, 32)
        AS_, AV, H = (16, 8, 4)
        NB = 16
        SQRT3 = 1.7320508075688772
        SQRT2 = 1.4142135623730951
        EPS = 1e-05

        def _cg_tp(s, v, y0, y1, w_ss, w_sv, w_vs, w_vv0, w_vv1):
            out_s = jnp.concatenate([w_ss * s * y0[:, None], w_vv0 * (jnp.einsum('eci,ei->ec', v, y1) / SQRT3)], axis=-1)
            out_v = jnp.concatenate([(w_sv * s)[:, :, None] * y1[:, None, :], (w_vs * jnp.ones_like(v[..., 0]))[..., None] * v * y0[:, None, None], (w_vv1 * jnp.ones_like(v[..., 0]))[..., None] * (jnp.cross(v, y1[:, None, :]) / SQRT2)], axis=1)
            return (out_s, out_v)

        def _equiv_layernorm(s, v, gamma_s, beta_s, gamma_v):
            mu = jnp.mean(s, axis=-1, keepdims=True)
            var = jnp.var(s, axis=-1, keepdims=True)
            s_n = (s - mu) * jax.lax.rsqrt(var + EPS) * gamma_s + beta_s
            rms = jnp.sqrt(jnp.mean(jnp.sum(v * v, axis=-1), axis=-1, keepdims=True) + EPS)
            v_n = v / rms[..., None] * gamma_v[None, :, None]
            return (s_n, v_n)
        n = node.shape[0]
        e = rsh.shape[0]
        s = node[:, :CS]
        v = node[:, CS:].reshape(n, CV, 3)
        s_n, v_n = _equiv_layernorm(s, v, gamma_s, beta_s, gamma_v)
        src, dst = (edge_index[0], edge_index[1])
        msg_s = (s_n @ Ws_src)[src] + (s_n @ Ws_dst)[dst]
        msg_v = jnp.einsum('ncx,cd->ndx', v_n, Wv_src)[src] + jnp.einsum('ncx,cd->ndx', v_n, Wv_dst)[dst]
        y0, y1 = (rsh[:, 0], rsh[:, 1:4])
        w1 = rbf @ W_rbf
        m1_s, m1_v = _cg_tp(msg_s, msg_v, y0, y1, w1[:, :CS], w1[:, CS:2 * CS], w1[:, 2 * CS:2 * CS + CV], w1[:, 2 * CS + CV:2 * CS + 2 * CV], w1[:, 2 * CS + 2 * CV:])
        a = (m1_s @ W_alpha).reshape(e, H, AS_)
        a = jnp.where(a > 0, a, 0.2 * a)
        a = jnp.sum(a * alpha_dot, axis=-1, keepdims=True)
        amax = jax.ops.segment_max(a, dst, num_segments=n)
        amax = jnp.where(jnp.isfinite(amax), amax, 0.0)
        ex = jnp.exp(a - amax[dst])
        den = jax.ops.segment_sum(ex, dst, num_segments=n)
        alpha = ex / (den[dst] + 1e-16)
        val_s = m1_s @ Ws_val
        val_v = jnp.einsum('ecx,cd->edx', m1_v, Wv_val)
        val_v = val_v * jax.nn.sigmoid(val_s @ Wg)[..., None]
        val_s = jax.nn.sigmoid(val_s)
        m2_s, m2_v = _cg_tp(val_s, val_v, y0, y1, w2_ss, w2_sv, w2_vs, w2_vv0, w2_vv1)
        hs = (m2_s @ Ws_vlin).reshape(e, H, AS_)
        hv = jnp.einsum('ecx,cd->edx', m2_v, Wv_vlin).reshape(e, H, AV, 3)
        h = jnp.concatenate([hs, hv.reshape(e, H, AV * 3)], axis=-1)
        agg = jax.ops.segment_sum(alpha * h, dst, num_segments=n)
        agg_s = agg[:, :, :AS_].reshape(n, H * AS_)
        agg_v = agg[:, :, AS_:].reshape(n, H * AV, 3)
        out = node + jnp.concatenate([agg_s @ Wps, jnp.einsum('ncx,cd->ndx', agg_v, Wpv).reshape(n, CV * 3)], axis=-1)
        return out

    def _L1_gnn_ref(x, edge_src, edge_dst, edge_query, edge_sh, si_w0, si_w1, lin1_w0, lin1_w1, tp_weight, lin2_w0, lin2_w1):
        import jax, jax.numpy as jnp
        import numpy as np
        N = 6250
        E = 62500
        MUL0 = 64
        MUL1 = 32
        DIM_KEY = 64
        WEIGHT_NUMEL = 64 + 64 + 32 + 32 + 32

        def _irreps_linear(s, v, w0, w1):
            so = s @ w0 * w0.shape[0] ** (-0.5)
            vo = jnp.einsum('nui,uv->nvi', v, w1) * w1.shape[0] ** (-0.5)
            return (so, vo)
        n = x.shape[0]
        s_in = x[:, :MUL0]
        v_in = x[:, MUL0:].reshape(n, MUL1, 3)
        si_s, si_v = _irreps_linear(s_in, v_in, si_w0, si_w1)
        s_skip = jnp.concatenate([si_s, si_v.reshape(n, 3 * MUL1)], axis=1)
        h_s, h_v = _irreps_linear(s_in, v_in, lin1_w0, lin1_w1)
        es = h_s[edge_src]
        ev = h_v[edge_src]
        w = edge_query @ tp_weight
        w0, w1, w2a, w2b, w3 = (w[:, :64], w[:, 64:128], w[:, 128:160], w[:, 160:192], w[:, 192:224])
        sh_s = edge_sh[:, 0:1]
        sh_v = edge_sh[:, 1:4]
        out0 = w0 * es * sh_s
        out1 = (w1 * es)[:, :, None] * sh_v[:, None, :]
        out2 = 2.0 ** (-0.5) * (w2a * sh_s)[:, :, None] * ev + 0.5 * w2b[:, :, None] * jnp.cross(ev, sh_v[:, None, :])
        out3 = 3.0 ** (-0.5) * w3 * jnp.sum(ev * sh_v[:, None, :], axis=-1)
        edge_x = jnp.concatenate([out0, out1.reshape(-1, 3 * MUL0), out2.reshape(-1, 3 * MUL1), out3], axis=1)
        agg = jax.ops.segment_sum(edge_x, edge_dst, num_segments=n)
        a0 = agg[:, :64]
        a1 = agg[:, 64:256].reshape(n, 64, 3)
        a2 = agg[:, 256:352].reshape(n, 32, 3)
        a3 = agg[:, 352:384]
        scal = jnp.concatenate([a0, a3], axis=1) @ lin2_w0 * (MUL0 + MUL1) ** (-0.5)
        vec = jnp.einsum('nui,uv->nvi', jnp.concatenate([a1, a2], axis=1), lin2_w1) * (MUL0 + MUL1) ** (-0.5)
        conv_out = jnp.concatenate([scal, vec.reshape(n, 3 * MUL1)], axis=1)
        return s_skip + conv_out / 10.0
    edge_index = jnp.stack([src, dst])
    x = _layernorm(x + _L0_gnn_ref(x, edge_attr_16, edge_attr_4, L0_gnn_gamma_s, L0_gnn_beta_s, L0_gnn_gamma_v, L0_gnn_Ws_src, L0_gnn_Wv_src, L0_gnn_Ws_dst, L0_gnn_Wv_dst, L0_gnn_W_rbf, L0_gnn_W_alpha, L0_gnn_alpha_dot, L0_gnn_Ws_val, L0_gnn_Wv_val, L0_gnn_Wg, L0_gnn_w2_ss, L0_gnn_w2_sv, L0_gnn_w2_vs, L0_gnn_w2_vv0, L0_gnn_w2_vv1, L0_gnn_Ws_vlin, L0_gnn_Wv_vlin, L0_gnn_Wps, L0_gnn_Wpv, edge_index), axis=-1)
    x = _layernorm(x + _L1_gnn_ref(x, src, dst, edge_attr_64, edge_attr_4, L1_gnn_si_w0, L1_gnn_si_w1, L1_gnn_lin1_w0, L1_gnn_lin1_w1, L1_gnn_tp_weight, L1_gnn_lin2_w0, L1_gnn_lin2_w1), axis=-1)
    return x

_drawn_inputs = setup_inputs


def setup_inputs(seed=0):
    import zlib

    import numpy as np

    out = dict(_drawn_inputs(seed))
    spreads = {'L0_gnn_gamma_s': (1.0, 0.6), 'L0_gnn_beta_s': (0.0, 0.8), 'L0_gnn_gamma_v': (1.0, 0.6)}
    factors = {'L0_gnn_Wv_src': 2.714, 'L0_gnn_w2_vv1': 4.418}
    for name, (base, spread) in spreads.items():
        noise = np.random.default_rng([zlib.crc32(name.encode()), seed]).standard_normal(out[name].shape)
        drawn = base * np.exp(spread * noise) if base else spread * noise
        out[name] = jnp.asarray(drawn.astype(out[name].dtype))
    for name, factor in factors.items():
        out[name] = (out[name] * factor).astype(out[name].dtype)
    return out
```

```python
from contextlib import ExitStack

import concourse.bass as bass
from concourse import mybir
import numpy as np

ALU = mybir.AluOpType
ACT = mybir.ActivationFunctionType
AX = mybir.AxisListType.X
F32 = mybir.dt.float32
I32 = mybir.dt.int32

P = 128
NODES = 6250
EDGES = 206250
CS, CV, H, AS, AV, NB = 64, 32, 4, 16, 8, 16
V3 = 3 * CV
C = CS + V3
BLOCKS = -(-NODES // P)
SUPER = -(-EDGES // 512) + (-(-EDGES // 512)) % 2
STEPS = SUPER + BLOCKS - 1
SCANG = -(-SUPER * 4 // P)
SCANT = SCANG * P
HEAD = AS + 3 * AV
BIG = 1.5e38
FAR = 1 << 20
EPS = 1e-5
STEPS += STEPS % 2

PACK = [
    ("ident", 128, 128), ("ones", 128, 128), ("iota", 128, 128), ("count", 128, STEPS), ("sidx", 128, 4),
    ("ts0", 64, 128), ("tv0", 96, 192), ("gamma_s", 64, 1), ("beta_s", 64, 1), ("gamma_v", 96, 1),
    ("wy0", 80, 128), ("wy1", 80, 96), ("wy2", 80, 96), ("wy3", 80, 96), ("wy4", 80, 96),
    ("m1a", 128, 128), ("m1b", 96, 128), ("p1", 128, 96), ("vb", 96, 96), ("vc1", 96, 96), ("vc2", 96, 96),
    ("wg", 128, 96), ("adot", 64, 4), ("mu1", 128, 96), ("mu2", 128, 64), ("mv1", 96, 64), ("mv0", 96, 96),
    ("mv2", 96, 96), ("mv3", 96, 96), ("r_mu1", 128, 1), ("r_mu2", 128, 1), ("r_vs", 96, 1), ("r_vv0", 96, 1),
    ("r_vv1", 96, 1), ("wp0", 80, 160), ("wp1", 80, 160), ("ts1", 64, 128), ("tv1", 96, 192), ("tp", 128, 224),
    ("l2s", 96, 64), ("l2v", 96, 32),
]
PLACE, PACKW = {}, 0
for _name, _rows, _cols in PACK:
    PLACE[_name] = (_rows, PACKW, _cols)
    PACKW += _cols


class At:

    def __init__(self, n, half, slot):
        self.n, self.half, self.slot = n, half, slot

    def __add__(self, d):
        return At(self.n + d, self.half + (self.slot + d) // 2, (self.slot + d) % 2)

    def inside(self, count):
        return not isinstance(self.n, int) or 0 <= self.n < count


def loop(eng, body, first, last, count):
    lo = 4
    hi = count - 4
    for m in range(first, lo):
        body(At(m, m // 2, m % 2))
    with eng.Fori(lo // 2, hi // 2) as i:
        for u in range(2):
            body(At(2 * i + u, i, u))
    for m in range(hi, last):
        body(At(m, m // 2, m % 2))


def blocks(eng, body):
    for m in range(3):
        body(At(m, m // 2, m % 2))
    with eng.Fori(1, (BLOCKS - 1) // 2) as i:
        for u in range(1, 3):
            body(At(2 * i + u, i + u // 2, u % 2))


def wait(eng, sem, value):
    if not isinstance(value, int) or value > 0:
        eng.wait_ge(sem, value)


def gnn(nc, io):
    tab_src = nc.dram_tensor("tab_src", [BLOCKS * P, C], F32).ap()
    tab_dst = nc.dram_tensor("tab_dst", [BLOCKS * P, C], F32).ap()
    tab_conv = nc.dram_tensor("tab_conv", [BLOCKS * P, C], F32).ap()
    h_dram = nc.dram_tensor("h_dram", [SUPER, P, 4 * C], F32).ap()
    ex_dram = nc.dram_tensor("ex_dram", [SCANT // 4, P, 16], F32).ap()

    with ExitStack() as top:
        pack = top.enter_context(nc.sbuf_tensor("pack_sb", [P, PACKW], F32))
        nodes = top.enter_context(nc.sbuf_tensor("nodes", [P, BLOCKS, C], F32))
        block128 = top.enter_context(nc.sbuf_tensor("block128", [P, STEPS], F32))
        step_s = top.enter_context(nc.sbuf_tensor("step_s", [P, STEPS], I32))
        step_b = top.enter_context(nc.sbuf_tensor("step_b", [P, STEPS], I32))
        banks = [top.enter_context(nc.psum_tensor(f"bank{i}", [P, 512], F32)) for i in range(8)]
        g = dict(pack=pack, nodes=nodes, block128=block128, step_s=step_s, step_b=step_b, banks=banks,
                 tab_src=tab_src, tab_dst=tab_dst, tab_conv=tab_conv, h_dram=h_dram, ex_dram=ex_dram, io=io)

        def w(name):
            rows, at, cols = PLACE[name]
            return pack[0:rows, at:at + cols]
        g["w"] = w

        constants(nc, g)
        attention_input(nc, g)
        with ExitStack() as mid:
            g["alpha"] = mid.enter_context(nc.sbuf_tensor("alpha", [P, SCANT, H], F32))
            attention_edges(nc, g)
            segment_softmax(nc, g)
        with ExitStack() as mid:
            g["agg"] = mid.enter_context(nc.sbuf_tensor("agg0", [P, BLOCKS, C + H], F32))
            attention_aggregate(nc, g)
            attention_output(nc, g)
        with ExitStack() as mid:
            g["agg"] = mid.enter_context(nc.sbuf_tensor("agg1", [P, BLOCKS, 384], F32))
            conv_edges(nc, g)
            conv_output(nc, g)


def constants(nc, g):
    w, io, pack = g["w"], g["io"], g["pack"]
    scaled = [("m1b", None, 3 ** -0.5), ("vc1", None, 2 ** -0.5), ("vc2", None, -(2 ** -0.5)),
              ("mu1", "r_mu1", 1.0), ("mu2", "r_mu2", 1.0), ("mv1", "r_vv0", 3 ** -0.5), ("mv0", "r_vs", 1.0),
              ("mv2", "r_vv1", 2 ** -0.5), ("mv3", "r_vv1", -(2 ** -0.5)),
              ("ts1", None, CS ** -0.5), ("tv1", None, CV ** -0.5),
              ("l2s", None, (CS + CV) ** -0.5 / 10.0), ("l2v", None, (CS + CV) ** -0.5 / 10.0)]
    with ExitStack() as ctx:
        sdst = ctx.enter_context(nc.sbuf_tensor("sdst", [P, 4], I32))
        sblk = ctx.enter_context(nc.sbuf_tensor("sblk", [P, 4], I32))
        start = ctx.enter_context(nc.sbuf_tensor("start", [P, 4], F32))
        start2 = ctx.enter_context(nc.sbuf_tensor("start2", [P, 4], F32))
        begun = ctx.enter_context(nc.sbuf_tensor("begun", [P, 4, STEPS], F32))
        s_f = ctx.enter_context(nc.sbuf_tensor("s_f", [P, STEPS], F32))
        b_f = ctx.enter_context(nc.sbuf_tensor("b_f", [P, STEPS], F32))
        loaded = ctx.enter_context(nc.semaphore("const_loaded"))
        chain = ctx.enter_context(nc.semaphore("const_chain"))
        summed = ctx.enter_context(nc.semaphore("const_summed"))
        with nc.Block() as block:
            @block.sync
            def _(sp):
                sp.dma_start(pack[:, :], io["pack"]).then_inc(loaded, 16)
                sp.dma_start(sdst[:, :], io["sdst"]).then_inc(loaded, 16)
                sp.dma_start(g["nodes"][:, :, :], io["x"]).then_inc(loaded, 16)

            @block.vector
            def _(dve):
                links = [0]

                def link(ins):
                    links[0] += 1
                    ins.then_inc(chain, 1)
                    dve.wait_ge(chain, links[0])

                dve.wait_ge(loaded, 48)
                link(dve.tensor_scalar(sblk[:, :], sdst[:, :], 7, None, ALU.logical_shift_right))
                link(dve.tensor_copy(start[:, :], sblk[:, :]))
                link(dve.tensor_tensor(start2[:, :], start[:, :], w("sidx"), ALU.add))
                for c in range(4):
                    ins = dve.tensor_scalar(begun[:, c, :], w("count"), start2[:, c:c + 1], None, ALU.is_ge)
                link(ins)
                for name, rows, const in scaled:
                    if rows:
                        ins = dve.tensor_scalar(w(name), w(name), w(rows), const, ALU.mult, ALU.mult)
                    else:
                        ins = dve.tensor_scalar(w(name), w(name), const, None, ALU.mult)
                at = PLACE["tp"][1]
                for a, b, const in ((128, 160, 2 ** -0.5), (160, 192, 0.5), (192, 224, 3 ** -0.5)):
                    ins = dve.tensor_scalar(pack[:, at + a:at + b], pack[:, at + a:at + b], const, None, ALU.mult)
                link(ins)
                dve.wait_ge(summed, 1)
                link(dve.tensor_copy(s_f[:, :], g["banks"][0][:, 0:STEPS]))
                link(dve.tensor_tensor(b_f[:, :], w("count"), s_f[:, :], ALU.subtract))
                dve.tensor_scalar(g["block128"][:, :], b_f[:, :], float(P), None, ALU.mult)
                dve.tensor_copy(g["step_s"][:, :], s_f[:, :])
                link(dve.tensor_scalar(g["step_b"][:, :], b_f[:, :], float(BLOCKS - 1), None, ALU.min))

            @block.tensor
            def _(pe):
                pe.wait_ge(chain, 4)
                for c in range(4):
                    ins = pe.matmul(g["banks"][0][:, 0:STEPS], w("ones"), begun[:, c, :], start=(c == 0), stop=(c == 3))
                ins.then_inc(summed, 1)


def node_tables(nc, g, tag, values, ts, tv, scales, outputs, base):
    w, banks = g["w"], g["banks"]
    with ExitStack() as ctx:
        def sb(name, shape):
            return ctx.enter_context(nc.sbuf_tensor(f"{tag}_{name}", shape, F32))

        def sem(name):
            return ctx.enter_context(nc.semaphore(f"{tag}_{name}"))
        row, feat = sb("row", [P, C]), sb("feat", [P, 2, P])
        out = sb("out", [P, 2, 2, C])
        picked, turned, kept, mapped, evacuated, summed = (sem(x) for x in (
            "picked", "turned", "kept", "mapped", "evacuated", "summed"))
        stored = [sem("stored0"), sem("stored1")]
        with nc.Block() as block:
            @block.vector
            def _(dve):
                def body(at):
                    wait(dve, turned, at.n)
                    if base is not None:
                        wait(dve, evacuated, at.n)
                    dve.tensor_copy(row[:, :], values[:, bass.ds(at.n, 1), :].rearrange("p a c -> p (a c)")).then_inc(picked, 1)
                    dve.wait_ge(mapped, at.n + 1)
                    wait(dve, stored[at.slot], at.half * (32 if base is None else 16))
                    for o in range(2 if base is None else 1):
                        dve.tensor_copy(out[:, at.slot, o, 0:CS], banks[2][:, o * CS:(o + 1) * CS])
                        ins = dve.tensor_copy(out[:, at.slot, o, CS:C], banks[3][:, o * V3:(o + 1) * V3])
                    ins.then_inc(summed, 1)
                    if base is not None:
                        there = base[:, bass.ds(at.n, 1), :].rearrange("p a c -> p (a c)")
                        dve.tensor_tensor(there[:, 0:CS], row[:, 0:CS], banks[2][:, CS:2 * CS], ALU.add)
                        dve.tensor_tensor(there[:, CS:C], row[:, CS:C], banks[3][:, V3:2 * V3], ALU.add).then_inc(evacuated, 1)
                blocks(dve, body)

            @block.tensor
            def _(pe):
                def body(at):
                    pe.wait_ge(picked, at.n + 1)
                    wait(pe, kept, at.n)
                    pe.transpose(banks[1][0:V3, 0:P], row[:, CS:C], w("ident"))
                    pe.transpose(banks[0][0:CS, 0:P], row[:, 0:CS], w("ident")).then_inc(turned, 1)
                    pe.wait_ge(kept, at.n + 1)
                    wait(pe, summed if base is None else evacuated, at.n)
                    pe.matmul(banks[2][:, 0:2 * CS], feat[0:CS, 0, :], w(ts), start=True, stop=True)
                    pe.matmul(banks[3][:, 0:2 * V3], feat[0:V3, 1, :], w(tv), start=True, stop=True).then_inc(mapped, 1)
                blocks(pe, body)

            @block.scalar
            def _(act):
                def body(at):
                    act.wait_ge(turned, at.n + 1)
                    wait(act, mapped, at.n)
                    if scales:
                        act.activation(feat[0:CS, 0, :], banks[0][0:CS, 0:P], ACT.Identity,
                                       bias=w(scales[1]), scale=w(scales[0]))
                        act.activation(feat[0:V3, 1, :], banks[1][0:V3, 0:P], ACT.Identity,
                                       scale=w(scales[2])).then_inc(kept, 1)
                    else:
                        act.activation(feat[0:CS, 0, :], banks[0][0:CS, 0:P], ACT.Copy)
                        act.activation(feat[0:V3, 1, :], banks[1][0:V3, 0:P], ACT.Copy).then_inc(kept, 1)
                blocks(act, body)

            @block.sync
            def _(sp):
                def body(at):
                    sp.wait_ge(summed, at.n + 1)
                    for o, table in enumerate(outputs):
                        sp.dma_start(table.rearrange("(b p) c -> b p c", p=P)[bass.ds(at.n, 1), :, :].rearrange("a p c -> (a p) c"),
                                     out[:, at.slot, o, :]).then_inc(stored[at.slot], 16)
                blocks(sp, body)
                sp.wait_ge(stored[0], 16 * len(outputs) * ((BLOCKS + 1) // 2))
                sp.wait_ge(stored[1], 16 * len(outputs) * (BLOCKS // 2))


def normalise(nc, g, tag, groups, out):
    with ExitStack() as ctx:
        square = ctx.enter_context(nc.sbuf_tensor(f"{tag}_square", [P, BLOCKS, C], F32))
        mean = ctx.enter_context(nc.sbuf_tensor(f"{tag}_mean", [P, BLOCKS], F32))
        mean1 = ctx.enter_context(nc.sbuf_tensor(f"{tag}_mean1", [P, BLOCKS], F32))
        var = ctx.enter_context(nc.sbuf_tensor(f"{tag}_var", [P, BLOCKS], F32))
        var1 = ctx.enter_context(nc.sbuf_tensor(f"{tag}_var1", [P, BLOCKS], F32))
        dev = ctx.enter_context(nc.sbuf_tensor(f"{tag}_dev", [P, BLOCKS], F32))
        inv = ctx.enter_context(nc.sbuf_tensor(f"{tag}_inv", [P, BLOCKS], F32))
        chain = ctx.enter_context(nc.semaphore(f"{tag}_chain"))
        rooted = ctx.enter_context(nc.semaphore(f"{tag}_rooted"))
        varied = ctx.enter_context(nc.semaphore(f"{tag}_varied"))
        with nc.Block() as block:
            @block.vector
            def _(dve):
                links = [0]

                def link(ins):
                    links[0] += 1
                    ins.then_inc(chain, 1)
                    dve.wait_ge(chain, links[0])

                for n, (src, lo, hi, divisor, centre) in enumerate(groups):
                    width = hi - lo
                    spread = [P, BLOCKS, width]
                    if centre:
                        link(dve.tensor_reduce(mean[:, :], src[:, :, lo:hi], AX, ALU.add))
                        link(dve.tensor_scalar(mean1[:, :], mean[:, :], 1.0 / width, None, ALU.mult))
                        link(dve.tensor_tensor(out[:, :, lo:hi], src[:, :, lo:hi],
                                               mean1[:, :].unsqueeze(2).to_broadcast(spread), ALU.subtract))
                        src = out
                    link(dve.tensor_tensor(square[:, :, lo:hi], src[:, :, lo:hi], src[:, :, lo:hi], ALU.mult))
                    link(dve.tensor_reduce(var[:, :], square[:, :, lo:hi], AX, ALU.add))
                    link(dve.tensor_scalar(var1[:, :], var[:, :], 1.0 / divisor, EPS, ALU.mult, ALU.add))
                    dve.sem_inc(varied, 1)
                    dve.wait_ge(rooted, n + 1)
                    link(dve.reciprocal(inv[:, :], dev[:, :]))
                    link(dve.tensor_tensor(out[:, :, lo:hi], src[:, :, lo:hi],
                                           inv[:, :].unsqueeze(2).to_broadcast(spread), ALU.mult))

            @block.scalar
            def _(act):
                for n in range(len(groups)):
                    act.wait_ge(varied, n + 1)
                    act.activation(dev[:, :], var1[:, :], ACT.Sqrt).then_inc(rooted, 1)


def attention_input(nc, g):
    with ExitStack() as ctx:
        normed = ctx.enter_context(nc.sbuf_tensor("normed", [P, BLOCKS, C], F32))
        normalise(nc, g, "ln0", [(g["nodes"], 0, CS, CS, True), (g["nodes"], CS, C, CV, False)], normed)
        node_tables(nc, g, "tab0", normed, "ts0", "tv0", ("gamma_s", "beta_s", "gamma_v"),
                    [g["tab_src"], g["tab_dst"]], None)


def attention_edges(nc, g):
    w, banks, io = g["w"], g["banks"], g["io"]
    with ExitStack() as ctx:
        def sb(name, shape, dt=F32):
            return ctx.enter_context(nc.sbuf_tensor(f"ae_{name}", shape, dt))

        def sem(name):
            return ctx.enter_context(nc.semaphore(f"ae_{name}"))
        idx = [sb(f"idx{u}", [P, 8], I32) for u in range(2)]
        gsrc = [sb(f"gsrc{u}", [P, 4, C]) for u in range(2)]
        gdst = [sb(f"gdst{u}", [P, 4, C]) for u in range(2)]
        rbf = [sb(f"rbf{u}", [80, 512]) for u in range(2)]
        y16 = [sb(f"y16_{u}", [80, 512]) for u in range(2)]
        rbfy = [sb(f"rbfy{u}", [80, 512]) for u in range(2)]
        ys = [sb(f"ys{u}", [P, 2, 512]) for u in range(2)]
        yv = [sb(f"yv{u}", [V3, 4, 512]) for u in range(2)]
        hsb = [sb(f"hsb{u}", [P, 4, C]) for u in range(2)]
        msg = sb("msg", [P, 4, C + CS])
        sT, vT = sb("sT", [P, 512]), sb("vT", [V3, 512])
        q = sb("q", [P, 5, 512])
        av = sb("av", [P, 512])
        leaky = sb("leaky", [CS, 512])
        sig = sb("sig", [P, 512])
        gate = sb("gate", [V3, 512])
        vy, vsum, vval = sb("vy", [V3, 512]), sb("vsum", [V3, 512]), sb("vval", [V3, 512])
        uy = sb("uy", [P, 2, 512])
        vvy = sb("vvy", [V3, 4, 512])
        filled, may_gather = sem("filled"), sem("may_gather")
        idx_in = [sem(f"idx_in{u}") for u in range(2)]
        rbf_in = [sem(f"rbf_in{u}") for u in range(2)]
        y_in = [sem(f"y_in{u}") for u in range(2)]
        gathered = [sem(f"gathered{u}") for u in range(2)]
        stored = [sem(f"stored{u}") for u in range(2)]
        summed, spread, multiplied, vy_done, vsum_done, leaky_done, vval_done, uy_done, vvy_done = (sem(x) for x in (
            "summed", "spread", "multiplied", "vy_done", "vsum_done", "leaky_done", "vval_done", "uy_done", "vvy_done"))
        pe_turned, pe_w, pe_av, pe_p1, pe_vv, pe_h, pe_gate, pe_alpha = (sem(x) for x in (
            "pe_turned", "pe_w", "pe_av", "pe_p1", "pe_vv", "pe_h", "pe_gate", "pe_alpha"))
        av_kept, sig_done, h_kept, gate_done, turned_kept, alpha_kept = (sem(x) for x in (
            "av_kept", "sig_done", "h_kept", "gate_done", "turned_kept", "alpha_kept"))
        b_w, b_s, b_v, b_av, b_p1, b_vv, b_h = banks[0:2], banks[2], banks[3], banks[4], banks[5], banks[6], banks[7]
        MS = (P, V3, V3, V3, V3)

        with nc.Block() as block:
            @block.sync
            def _(sp):
                def body(m):
                    t = m + 2
                    if t.inside(SUPER):
                        wait(sp, summed, t.n - 1)
                        wait(sp, spread, t.n - 1)
                        sp.dma_start(idx[t.slot][:, :], io["eidx"][t.n]).then_inc(idx_in[t.slot], 16)
                        sp.dma_start(rbf[t.slot][:, :], io["rbf5"][t.n]).then_inc(rbf_in[t.slot], 16)
                        sp.dma_start(y16[t.slot][0:CS, :], io["y16"][t.n]).then_inc(rbf_in[t.slot], 16)
                    t = m + -2
                    if t.inside(SUPER):
                        sp.wait_ge(h_kept, 2 * t.n + 2)
                        sp.dma_start(g["h_dram"][t.n], hsb[t.slot][:, :, :].rearrange("p k c -> p (k c)"))\
                            .then_inc(stored[t.slot], 16)
                    t = m + 1
                    if t.inside(SUPER):
                        wait(sp, vvy_done, t.n - 1)
                        for j in range(2):
                            sp.dma_start(ys[t.slot][CS * j:CS * j + CS, :, :].rearrange("p a e -> p (a e)"),
                                         io["ys"][t.n, j:j + 1, :].to_broadcast([CS, 1024])).then_inc(y_in[t.slot], 16)
                        for j in range(3):
                            sp.dma_start(yv[t.slot][CV * j:CV * j + CV, :, :].rearrange("p a e -> p (a e)"),
                                         io["yv"][t.n, j:j + 1, :].to_broadcast([CV, 2048])).then_inc(y_in[t.slot], 16)
                loop(sp, body, -2, SUPER + 2, SUPER)
                for u in range(2):
                    sp.wait_ge(stored[u], 16 * (SUPER // 2))

            @block.gpsimd
            def _(pool):
                def body(t):
                    pool.wait_ge(idx_in[t.slot], 16 * (t.half + 1))
                    wait(pool, summed, t.n - 1)
                    pool.sem_inc(may_gather, 1)
                    for k in range(4):
                        pool.indirect_dma_start(gsrc[t.slot][:, k, :], None, g["tab_src"],
                                                bass.IndirectOffsetOnAxis(ap=idx[t.slot][:, k:k + 1], axis=0))\
                            .then_inc(gathered[t.slot], 16)
                        pool.indirect_dma_start(gdst[t.slot][:, k, :], None, g["tab_dst"],
                                                bass.IndirectOffsetOnAxis(ap=idx[t.slot][:, 4 + k:5 + k], axis=0))\
                            .then_inc(gathered[t.slot], 16)
                loop(pool, body, 0, SUPER, SUPER)

            @block.vector
            def _(dve):
                dve.memset(y16[0][CS:80, :], 1.0)
                dve.memset(y16[1][CS:80, :], 1.0)
                dve.memset(g["alpha"][:, 4 * SUPER:SCANT, :], 0.0).then_inc(filled, 1)
                dve.wait_ge(filled, 1)

                def body(m):
                    t = m + -1
                    if t.inside(SUPER):
                        dve.wait_ge(pe_p1, t.n + 1)
                        dve.wait_ge(y_in[t.slot], 80 * (t.half + 1))
                        wait(dve, vsum_done, t.n)
                        dve.tensor_tensor(vy[:, :], b_p1[0:V3, :], yv[t.slot][:, 0, :], ALU.mult).then_inc(vy_done, 1)
                        dve.wait_ge(pe_vv, t.n + 1)
                        dve.wait_ge(vy_done, t.n + 1)
                        wait(dve, vval_done, t.n)
                        dve.tensor_tensor(vsum[:, :], b_vv[0:V3, :], vy[:, :], ALU.add).then_inc(vsum_done, 1)
                        dve.wait_ge(av_kept, t.n + 1)
                        wait(dve, pe_alpha, t.n)
                        dve.scalar_tensor_tensor(leaky[:, :], av[0:CS, :], 0.2, av[0:CS, :], ALU.mult, ALU.max)\
                            .then_inc(leaky_done, 1)
                    t = m + 1
                    if t.inside(SUPER):
                        dve.wait_ge(gathered[t.slot], 128 * (t.half + 1))
                        wait(dve, pe_turned, t.n)
                        dve.tensor_tensor(msg[:, :, 0:CS], gsrc[t.slot][:, :, 0:CS], gdst[t.slot][:, :, 0:CS], ALU.add)
                        dve.tensor_tensor(msg[:, :, CS:CS + C], gsrc[t.slot][:, :, :], gdst[t.slot][:, :, :], ALU.add)\
                            .then_inc(summed, 1)
                        dve.wait_ge(rbf_in[t.slot], 32 * (t.half + 1))
                        wait(dve, pe_w, 5 * t.n - 5)
                        dve.tensor_tensor(rbfy[t.slot][:, :], rbf[t.slot][:, :], y16[t.slot][:, :], ALU.mult)\
                            .then_inc(spread, 1)
                    t = m
                    if t.inside(SUPER):
                        dve.wait_ge(turned_kept, t.n + 1)
                        wait(dve, pe_vv, t.n)
                        for c in range(5):
                            dve.wait_ge(pe_w, 5 * t.n + c + 1)
                            dve.tensor_tensor(q[0:MS[c], c, :], b_w[(t.slot + c) % 2][0:MS[c], :],
                                              (sT if c == 0 else vT)[:, :], ALU.mult).then_inc(multiplied, 1)
                    t = m + -1
                    if t.inside(SUPER):
                        dve.wait_ge(gate_done, t.n + 1)
                        dve.wait_ge(vsum_done, t.n + 1)
                        wait(dve, vvy_done, t.n)
                        dve.tensor_tensor(vval[:, :], vsum[:, :], gate[:, :], ALU.mult).then_inc(vval_done, 1)
                        dve.wait_ge(sig_done, t.n + 1)
                        wait(dve, pe_h, 2 * t.n)
                        dve.tensor_tensor(uy[:, :, :], sig[:, :].unsqueeze(1).to_broadcast([P, 2, 512]),
                                          ys[t.slot][:, :, :], ALU.mult).then_inc(uy_done, 1)
                        dve.wait_ge(vval_done, t.n + 1)
                        dve.tensor_tensor(vvy[:, :, :], vval[:, :].unsqueeze(1).to_broadcast([V3, 4, 512]),
                                          yv[t.slot][:, :, :], ALU.mult).then_inc(vvy_done, 1)
                loop(dve, body, -1, SUPER + 1, SUPER)

            @block.tensor
            def _(pe):
                def values(t, half, bank):
                    for k in (0, 1):
                        e = slice(P * (2 * half + k), P * (2 * half + k) + P)
                        o = bank[:, C * k:C * k + C].rearrange("p (h c) -> p h c", h=H)
                        pe.matmul(o[:, :, 0:24], uy[:, 0, e], w("mu1"), start=True, stop=False)
                        pe.matmul(o[:, :, 24:40], uy[:, 1, e], w("mu2"), start=False, stop=False)
                        pe.matmul(o[:, :, 0:16], vvy[:, 0, e], w("mv1"), start=False, stop=False)
                        pe.matmul(o[:, :, 16:40], vvy[:, 3, e], w("mv0"), start=False, stop=False)
                        pe.matmul(o[:, :, 16:40], vvy[:, 1, e], w("mv2"), start=False, stop=False)
                        ins = pe.matmul(o[:, :, 16:40], vvy[:, 2, e], w("mv3"), start=False, stop=True)
                    ins.then_inc(pe_h, 1)

                def body(m):
                    t = m + -1
                    if t.inside(SUPER):
                        pe.wait_ge(multiplied, 5 * t.n + 5)
                        wait(pe, av_kept, t.n)
                        pe.matmul(b_av[:, :], w("m1a"), q[:, 0, :], start=True, stop=False)
                        pe.matmul(b_av[:, :], w("m1b"), q[0:V3, 1, :], start=False, stop=True).then_inc(pe_av, 1)
                        wait(pe, gate_done, t.n)
                        pe.matmul(b_p1[0:V3, :], w("p1"), q[:, 0, :], start=True, stop=True).then_inc(pe_p1, 1)
                        wait(pe, vsum_done, t.n)
                        pe.matmul(b_vv[0:V3, :], w("vb"), q[0:V3, 2, :], start=True, stop=False)
                        pe.matmul(b_vv[0:V3, :], w("vc1"), q[0:V3, 3, :], start=False, stop=False)
                        pe.matmul(b_vv[0:V3, :], w("vc2"), q[0:V3, 4, :], start=False, stop=True).then_inc(pe_vv, 1)
                    t = m + -2
                    if t.inside(SUPER):
                        pe.wait_ge(vvy_done, t.n + 1)
                        wait(pe, h_kept, 2 * t.n)
                        values(t, 0, b_h)
                        wait(pe, turned_kept, min(t.n + 3, SUPER) if isinstance(t.n, int) else t.n + 3)
                        values(t, 1, b_s)
                    t = m + -1
                    if t.inside(SUPER):
                        pe.wait_ge(av_kept, t.n + 1)
                        pe.wait_ge(vy_done, t.n + 1)
                        pe.matmul(b_p1[0:V3, :], w("wg"), av[:, :], start=True, stop=True).then_inc(pe_gate, 1)
                    t = m
                    if t.inside(SUPER):
                        pe.wait_ge(spread, t.n + 1)
                        for c in range(5):
                            wait(pe, multiplied, 5 * t.n + c - 1)
                            pe.matmul(b_w[(t.slot + c) % 2][0:MS[c], :], w(f"wy{c}"), rbfy[t.slot][:, :],
                                      start=True, stop=True).then_inc(pe_w, 1)
                    t = m + 1
                    if t.inside(SUPER):
                        pe.wait_ge(summed, t.n + 1)
                        wait(pe, h_kept, 2 * t.n - 4)
                        wait(pe, turned_kept, t.n)
                        for k in range(4):
                            pe.transpose(b_s[:, P * k:P * k + P], msg[:, k, 0:P], w("ident"))
                        for k in range(4):
                            ins = pe.transpose(b_v[0:V3, P * k:P * k + P], msg[:, k, P:P + V3], w("ident"))
                        ins.then_inc(pe_turned, 1)
                    t = m + -1
                    if t.inside(SUPER):
                        pe.wait_ge(leaky_done, t.n + 1)
                        wait(pe, alpha_kept, t.n)
                        wait(pe, h_kept, 2 * t.n - 1)
                        for k in range(4):
                            ins = pe.matmul(b_h[:, 320 + 4 * k:324 + 4 * k], leaky[:, P * k:P * k + P], w("adot"),
                                            start=True, stop=True)
                        ins.then_inc(pe_alpha, 1)
                loop(pe, body, -1, SUPER + 2, SUPER)

            @block.scalar
            def _(act):
                def body(m):
                    t = m + -1
                    if t.inside(SUPER):
                        act.wait_ge(pe_av, t.n + 1)
                        wait(act, pe_gate, t.n)
                        wait(act, leaky_done, t.n)
                        wait(act, sig_done, t.n)
                        act.activation(av[:, :], b_av[:, :], ACT.Copy).then_inc(av_kept, 1)
                        act.wait_ge(av_kept, t.n + 1)
                        wait(act, uy_done, t.n)
                        act.activation(sig[0:CS, :], av[CS:P, :], ACT.Sigmoid)
                        act.activation(sig[CS:P, :], av[CS:P, :], ACT.Sigmoid).then_inc(sig_done, 1)
                    t = m + -2
                    if t.inside(SUPER):
                        wait(act, stored[t.slot], 16 * t.half)
                        for half, bank in ((0, b_h), (1, b_s)):
                            act.wait_ge(pe_h, 2 * t.n + half + 1)
                            act.activation(hsb[t.slot][:, 2 * half:2 * half + 2, :].rearrange("p k c -> p (k c)"),
                                           bank[:, 0:2 * C], ACT.Copy).then_inc(h_kept, 1)
                        act.wait_ge(pe_alpha, t.n + 1)
                        act.activation(g["alpha"][:, bass.ds(4 * t.n, 4), :].rearrange("p k h -> p (k h)"),
                                       b_h[:, 320:336], ACT.Copy).then_inc(alpha_kept, 1)
                    t = m + -1
                    if t.inside(SUPER):
                        act.wait_ge(pe_gate, t.n + 1)
                        wait(act, vval_done, t.n)
                        act.activation(gate[:, :], b_p1[0:V3, :], ACT.Sigmoid).then_inc(gate_done, 1)
                    t = m + 1
                    if t.inside(SUPER):
                        act.wait_ge(pe_turned, t.n + 1)
                        wait(act, multiplied, 5 * t.n)
                        act.activation(sT[:, :], b_s[:, :], ACT.Copy)
                        act.activation(vT[:, :], b_v[0:V3, :], ACT.Copy).then_inc(turned_kept, 1)
                loop(act, body, -1, SUPER + 2, SUPER)


def segment_softmax(nc, g):
    w, banks, io, alpha = g["w"], g["banks"], g["io"], g["alpha"]
    with ExitStack() as ctx:
        def sb(name, shape, dt=F32):
            return ctx.enter_context(nc.sbuf_tensor(f"sm_{name}", shape, dt))

        def sem(name):
            return ctx.enter_context(nc.semaphore(f"sm_{name}"))
        logit = sb("logit", [P, H, SCANT])
        forward = sb("forward", [P, H, SCANT])
        backward = alpha[:, :, :].rearrange("p t h -> p (t h)").rearrange("p (h t) -> p h t", h=H)
        dst = [sb(f"dst{i}", [P, SCANT], I32) for i in range(3)]
        gate = sb("gate", [P, 2, SCANT])
        whole, whole4 = sb("whole", [P, 2]), sb("whole4", [P, 2, H])
        ends = sb("ends", [P, 2, H])
        rows = sb("rows", [H, 2, 2, P])
        carry = sb("carry", [H, 2, P + 2])
        first = sb("first", [P, 2, H])
        loaded, turned, kept, chain, ended, swapped, carried, returned, shifted, exped, back, back_kept, stored = (
            sem(x) for x in ("loaded", "turned", "kept", "chain", "ended", "swapped", "carried", "returned",
                             "shifted", "exped", "back", "back_kept", "stored"))
        groups = [(h, j, min(4, SCANG - 4 * j)) for h in range(H) for j in range(-(-SCANG // 4))]
        by_group = alpha[:, :, :].rearrange("p (q g) h -> p h g q", g=SCANG)

        with nc.Block() as block:
            @block.sync
            def _(sp):
                for i in range(3):
                    sp.dma_start(dst[i][:, :], io["dst3"][i]).then_inc(loaded, 16)
                sp.wait_ge(back_kept, len(groups))
                sp.dma_start(g["ex_dram"].rearrange("s p c -> p s c"),
                             alpha[:, :, :].rearrange("p (s k) h -> p s (k h)", k=4)).then_inc(stored, 16)
                sp.wait_ge(stored, 16)

            @block.tensor
            def _(pe):
                for n, (h, j, cnt) in enumerate(groups):
                    wait(pe, kept, n - 3)
                    for i in range(cnt):
                        ins = pe.transpose(banks[n % 4][:, P * i:P * i + P], by_group[:, h, 4 * j + i, :], w("ident"))
                    ins.then_inc(turned, 1)
                for d in range(2):
                    pe.wait_ge(ended, d + 1)
                    pe.transpose(banks[4][0:H, 0:P], ends[:, d, :], w("ident"))
                    pe.transpose(banks[4][0:H, P:2 * P], whole4[:, d, :], w("ident")).then_inc(swapped, 1)
                    pe.wait_ge(carried, d + 1)
                    pe.transpose(banks[5][:, 0:H], carry[0:H, d, 2 * d:2 * d + P], w("ident")[0:H, 0:H]).then_inc(returned, 1)
                for n, (h, j, cnt) in enumerate(groups):
                    pe.wait_ge(exped, h + 1)
                    wait(pe, back_kept, n - 3)
                    for i in range(cnt):
                        at = P * (4 * j + i)
                        ins = pe.transpose(banks[n % 4][:, P * i:P * i + P], logit[:, h, at:at + P], w("ident"))
                    ins.then_inc(back, 1)

            @block.scalar
            def _(act):
                for n, (h, j, cnt) in enumerate(groups):
                    act.wait_ge(turned, n + 1)
                    act.activation(logit[:, h, 512 * j:512 * j + P * cnt], banks[n % 4][:, 0:P * cnt], ACT.Copy).then_inc(kept, 1)
                act.wait_ge(shifted, 1)
                for h in range(H):
                    act.activation(logit[:, h, :], logit[:, h, :], ACT.Exp).then_inc(exped, 1)
                for n, (h, j, cnt) in enumerate(groups):
                    act.wait_ge(back, n + 1)
                    act.activation(by_group[:, h, 4 * j:4 * j + cnt, :],
                                   banks[n % 4][:, 0:P * cnt].rearrange("p (g q) -> p g q", q=P), ACT.Copy).then_inc(back_kept, 1)

            @block.vector
            def _(dve):
                links = [0]

                def link(ins):
                    links[0] += 1
                    ins.then_inc(chain, 1)
                    dve.wait_ge(chain, links[0])

                dve.memset(carry[:, :, :], -BIG)
                dve.wait_ge(loaded, 48)
                for d in range(2):
                    ins = dve.tensor_tensor(gate[:, d, :], dst[0][:, :], dst[1 + d][:, :], ALU.is_equal)
                link(ins)
                link(dve.tensor_scalar(gate[:, :, :], gate[:, :, :], 2 * BIG, -BIG, ALU.mult, ALU.add))
                link(dve.tensor_reduce(whole[:, :], gate[:, :, :], AX, ALU.min))
                link(dve.tensor_copy(whole4[:, :, :], whole[:, :].unsqueeze(2).to_broadcast([P, 2, H])))
                dve.wait_ge(kept, len(groups))
                for d, (out, data) in enumerate(((forward, logit), (backward, forward))):
                    def flip(x):
                        return x[:, ::-1] if d else x

                    def scans(initial):
                        for h in range(H):
                            ins = dve.tensor_tensor_scan(flip(out[:, h, :]), flip(gate[:, d, :]), flip(data[:, h, :]),
                                                         initial(h), ALU.min, ALU.max)
                        return ins
                    link(scans(lambda h: -BIG))
                    dve.tensor_copy(ends[:, d, :], out[:, :, 0 if d else SCANT - 1]).then_inc(ended, 1)
                    dve.wait_ge(swapped, d + 1)
                    link(dve.tensor_copy(rows[:, d, :, :], banks[4][0:H, 0:2 * P].rearrange("p (a q) -> p a q", a=2)))
                    dve.tensor_tensor_scan(flip(carry[:, d, 1:P + 1]), flip(rows[:, d, 1, :]), flip(rows[:, d, 0, :]),
                                           -BIG, ALU.min, ALU.max).then_inc(carried, 1)
                    dve.wait_ge(returned, d + 1)
                    link(dve.tensor_copy(first[:, d, :], banks[5][:, 0:H]))
                    link(scans(lambda h: first[:, d, h:h + 1]))
                dve.tensor_tensor(logit[:, :, :], logit[:, :, :], backward, ALU.subtract).then_inc(shifted, 1)


def step_loads(sp, at, table, free, loads):
    s = sp.value_load(table[0:1, bass.ds(at.n, 1)], min_val=0, max_val=SUPER - 1)
    for sem, value in free:
        wait(sp, sem, value)
    for out, src, sem in loads:
        sp.dma_start(out, src[bass.ds(s, 1)].rearrange("a p c -> (a p) c")).then_inc(sem, 16)


def attention_aggregate(nc, g):
    w, banks, io, agg = g["w"], g["banks"], g["io"], g["agg"]
    W = C + H
    with ExitStack() as ctx:
        def sb(name, shape, dt=F32):
            return ctx.enter_context(nc.sbuf_tensor(f"ag_{name}", shape, dt))

        def sem(name):
            return ctx.enter_context(nc.semaphore(f"ag_{name}"))
        idx = [sb(f"idx{u}", [P, 8], I32) for u in range(2)]
        ex = [sb(f"ex{u}", [P, 16]) for u in range(2)]
        val = [sb(f"val{u}", [P, 4, C]) for u in range(2)]
        exval = [sb(f"exval{u}", [P, 4, W]) for u in range(2)]
        rel = [sb(f"rel{u}", [P, 4]) for u in range(2)]
        hot = [sb(f"hot{u}", [P, 4, P]) for u in range(2)]
        loaded = [sem(f"loaded{u}") for u in range(2)]
        zeroed, rel_done, ready, weighted, summed, added = (sem(x) for x in (
            "zeroed", "rel_done", "ready", "weighted", "summed", "added"))
        with nc.Block() as block:
            @block.sync
            def _(sp):
                def body(t):
                    step_loads(sp, t, g["step_s"], ((weighted, t.n - 1),), ((idx[t.slot][:, :], io["eidx"], loaded[t.slot]),
                                                    (ex[t.slot][:, :], g["ex_dram"], loaded[t.slot]),
                                                    (val[t.slot][:, :, :].rearrange("p k c -> p (k c)"), g["h_dram"], loaded[t.slot])))
                loop(sp, body, 0, STEPS, STEPS)

            @block.vector
            def _(dve):
                dve.memset(agg[:, :, :], 0.0).then_inc(zeroed, 1)
                dve.wait_ge(zeroed, 1)

                def body(m):
                    t = m
                    if t.inside(STEPS):
                        dve.wait_ge(loaded[t.slot], 48 * (t.half + 1))
                        wait(dve, summed, t.n - 1)
                        wait(dve, ready, t.n - 1)
                        dve.tensor_scalar(rel[t.slot][:, :], idx[t.slot][:, 4:8], g["block128"][:, bass.ds(t.n, 1)], None,
                                          ALU.subtract).then_inc(rel_done, 1)
                        dve.tensor_tensor(exval[t.slot][:, :, 0:C].rearrange("p k (h c) -> p k h c", h=H),
                                          val[t.slot][:, :, :].rearrange("p k (h c) -> p k h c", h=H),
                                          ex[t.slot][:, :].rearrange("p (k h) -> p k h", k=4).unsqueeze(3).to_broadcast([P, 4, H, HEAD]),
                                          ALU.mult)
                        dve.tensor_copy(exval[t.slot][:, :, C:W], ex[t.slot][:, :].rearrange("p (k h) -> p k h", k=4))\
                            .then_inc(weighted, 1)
                        dve.wait_ge(rel_done, t.n + 1)
                        for k in range(4):
                            ins = dve.tensor_scalar(hot[t.slot][:, k, :], w("iota"), rel[t.slot][:, k:k + 1], None, ALU.is_equal)
                        ins.then_inc(ready, 1)
                    t = m + -1
                    if t.inside(STEPS):
                        b = dve.value_load(g["step_b"][0:1, bass.ds(t.n, 1)], min_val=0, max_val=BLOCKS - 1)
                        there = agg[:, bass.ds(b, 1), :].rearrange("p a c -> p (a c)")
                        dve.wait_ge(summed, t.n + 1)
                        wait(dve, added, t.n)
                        dve.tensor_tensor(there, there, banks[t.slot][:, 0:W], ALU.add).then_inc(added, 1)
                loop(dve, body, 0, STEPS + 1, STEPS)

            @block.tensor
            def _(pe):
                def body(t):
                    pe.wait_ge(ready, t.n + 1)
                    wait(pe, added, t.n - 1)
                    for k in range(4):
                        ins = pe.matmul(banks[t.slot][:, 0:W], hot[t.slot][:, k, :], exval[t.slot][:, k, :],
                                        start=(k == 0), stop=(k == 3))
                    ins.then_inc(summed, 1)
                loop(pe, body, 0, STEPS, STEPS)


def node_update(nc, g, tag, source, chunks, base, factor):
    w, banks = g["w"], g["banks"]
    with ExitStack() as ctx:
        row = ctx.enter_context(nc.sbuf_tensor(f"{tag}_row", [P, source.shape[2]], F32))
        feat = ctx.enter_context(nc.sbuf_tensor(f"{tag}_feat", [P, len(chunks), P], F32))
        picked, turned, kept, mapped, added = (ctx.enter_context(nc.semaphore(f"{tag}_{x}")) for x in (
            "picked", "turned", "kept", "mapped", "added"))
        tall = max(cols for _, cols, *_ in chunks)
        with nc.Block() as block:
            @block.vector
            def _(dve):
                def body(at):
                    b = at.n
                    wait(dve, turned, b)
                    dve.tensor_copy(row[:, :], source[:, bass.ds(b, 1), :].rearrange("p a c -> p (a c)")).then_inc(picked, 1)
                    there = base[:, bass.ds(b, 1), :].rearrange("p a c -> p (a c)")
                    dve.wait_ge(mapped, b + 1)
                    dve.scalar_tensor_tensor(there, there, factor, banks[1][:, 0:C], ALU.mult, ALU.add).then_inc(added, 1)
                blocks(dve, body)

            @block.tensor
            def _(pe):
                def body(at):
                    b = at.n
                    pe.wait_ge(picked, b + 1)
                    wait(pe, kept, b)
                    for i, (at, cols, _, _, _) in enumerate(chunks):
                        ins = pe.transpose(banks[0][0:cols, P * i:P * i + P], row[:, at:at + cols], w("ident"))
                    ins.then_inc(turned, 1)
                    pe.wait_ge(kept, b + 1)
                    wait(pe, added, b)
                    wrote = set()
                    for i, (_, cols, weights, lo, width) in enumerate(chunks):
                        ins = pe.matmul(banks[1][:, lo:lo + width], feat[0:cols, i, :], w(weights),
                                        start=(lo not in wrote), stop=(i == len(chunks) - 1 or width != C))
                        wrote.add(lo)
                    ins.then_inc(mapped, 1)
                blocks(pe, body)

            @block.scalar
            def _(act):
                def body(at):
                    b = at.n
                    act.wait_ge(turned, b + 1)
                    wait(act, mapped, b)
                    act.activation(feat[0:tall, :, :].rearrange("p i q -> p (i q)"), banks[0][0:tall, 0:P * len(chunks)],
                                   ACT.Copy).then_inc(kept, 1)
                blocks(act, body)


def attention_output(nc, g):
    agg, nodes = g["agg"], g["nodes"]
    with ExitStack() as ctx:
        den = ctx.enter_context(nc.sbuf_tensor("den", [P, BLOCKS, H], F32))
        rden = ctx.enter_context(nc.sbuf_tensor("rden", [P, BLOCKS, H], F32))
        chain = ctx.enter_context(nc.semaphore("den_chain"))
        with nc.Block() as block:
            @block.vector
            def _(dve):
                dve.tensor_scalar(den[:, :, :], agg[:, :, C:C + H], 1e-16, None, ALU.add).then_inc(chain, 1)
                dve.wait_ge(chain, 1)
                dve.reciprocal(rden[:, :, :], den[:, :, :]).then_inc(chain, 1)
                dve.wait_ge(chain, 2)
                heads = agg[:, :, 0:C].rearrange("p b (h c) -> p b h c", h=H)
                dve.tensor_tensor(heads, heads, rden[:, :, :].unsqueeze(3).to_broadcast([P, BLOCKS, H, HEAD]),
                                  ALU.mult).then_inc(chain, 1)
    node_update(nc, g, "upd0", agg, [(0, 80, "wp0", 0, C), (80, 80, "wp1", 0, C)], nodes, 2.0)
    normalise(nc, g, "ln1", [(nodes, 0, C, C, True)], nodes)
    node_tables(nc, g, "tab1", nodes, "ts1", "tv1", None, [g["tab_conv"]], nodes)


def conv_edges(nc, g):
    w, banks, io, agg = g["w"], g["banks"], g["io"], g["agg"]
    PW, WW = 2 * CS + 3 * V3, 2 * CS + 3 * CV
    with ExitStack() as ctx:
        def sb(name, shape, dt=F32):
            return ctx.enter_context(nc.sbuf_tensor(f"ce_{name}", shape, dt))

        def sem(name):
            return ctx.enter_context(nc.semaphore(f"ce_{name}"))
        idx = [sb(f"idx{u}", [P, 8], I32) for u in range(2)]
        y = [sb(f"y{u}", [P, 16]) for u in range(2)]
        query = [sb(f"query{u}", [P, 512]) for u in range(2)]
        node = [sb(f"node{u}", [P, 4, C]) for u in range(2)]
        rel = [sb(f"rel{u}", [P, 4]) for u in range(2)]
        prod = [sb("prod0", [P, 4, PW])] * 2
        hot = [sb("hot0", [P, 4, 4, P])] * 2
        idx_in, query_in, gathered = ([sem(f"{x}{u}") for u in range(2)] for x in ("idx_in", "query_in", "gathered"))
        may_gather = sem("may_gather")
        zeroed, rel_done, ready, hot_done, prod_done, weights, summed, added, taken = (sem(x) for x in (
            "zeroed", "rel_done", "ready", "hot_done", "prod_done", "weights", "summed", "added", "taken"))
        with nc.Block() as block:
            @block.sync
            def _(sp):
                def body(t):
                    step_loads(sp, t, g["step_s"], ((hot_done, t.n - 1),), ((idx[t.slot][:, :], io["eidx"], idx_in[t.slot]),
                                                    (y[t.slot][:, :], io["ey"], query_in[t.slot]),
                                                    (query[t.slot][0:CS, :], io["query"], query_in[t.slot])))
                loop(sp, body, 0, STEPS, STEPS)

            @block.gpsimd
            def _(pool):
                def body(t):
                    pool.wait_ge(idx_in[t.slot], 16 * (t.half + 1))
                    wait(pool, prod_done, 4 * t.n - 4)
                    pool.sem_inc(may_gather, 1)
                    for k in range(4):
                        pool.indirect_dma_start(node[t.slot][:, k, :], None, g["tab_conv"],
                                                bass.IndirectOffsetOnAxis(ap=idx[t.slot][:, k:k + 1], axis=0))\
                            .then_inc(gathered[t.slot], 16)
                loop(pool, body, 0, STEPS, STEPS)

            @block.vector
            def _(dve):
                dve.memset(agg[:, :, :], 0.0)
                for u in range(2):
                    ins = dve.memset(query[u][CS:P, :], 0.0)
                ins.then_inc(zeroed, 1)
                dve.wait_ge(zeroed, 1)

                def body(m):
                    t = m
                    if t.inside(STEPS):
                        dve.wait_ge(idx_in[t.slot], 16 * (t.half + 1))
                        dve.wait_ge(query_in[t.slot], 32 * (t.half + 1))
                        wait(dve, hot_done, t.n - 1)
                        dve.tensor_scalar(rel[t.slot][:, :], idx[t.slot][:, 4:8], g["block128"][:, bass.ds(t.n, 1)], None,
                                          ALU.subtract).then_inc(rel_done, 1)
                        dve.wait_ge(gathered[t.slot], 64 * (t.half + 1))
                        wait(dve, summed, t.n)
                        for k in range(4):
                            dve.wait_ge(weights, 4 * t.n + k + 1)
                            bank = banks[2 + k]
                            there, here = prod[0][:, k, :], node[t.slot][:, k, :]
                            dve.tensor_tensor(there[:, 0:2 * CS].rearrange("p (a c) -> p a c", a=2),
                                              bank[:, 0:2 * CS].rearrange("p (a c) -> p a c", a=2),
                                              here[:, 0:CS].unsqueeze(1).to_broadcast([P, 2, CS]), ALU.mult)
                            dve.tensor_tensor(there[:, 2 * CS:PW].rearrange("p (a x c) -> p a x c", a=3, x=3),
                                              bank[:, 2 * CS:WW].rearrange("p (a c) -> p a c", a=3).unsqueeze(2).to_broadcast([P, 3, 3, CV]),
                                              here[:, CS:C].rearrange("p (x c) -> p x c", x=3).unsqueeze(1).to_broadcast([P, 3, 3, CV]),
                                              ALU.mult).then_inc(prod_done, 1)
                        dve.wait_ge(rel_done, t.n + 1)
                        for j in range(4):
                            for k in range(4):
                                ins = dve.tensor_scalar(hot[0][:, j, k, :], w("iota"), rel[t.slot][:, k:k + 1],
                                                        y[t.slot][:, 4 * k + j:4 * k + j + 1], ALU.is_equal, ALU.mult)
                        ins.then_inc(hot_done, 1)
                    t = m + -1
                    if t.inside(STEPS):
                        b = dve.value_load(g["step_b"][0:1, bass.ds(t.n, 1)], min_val=0, max_val=BLOCKS - 1)
                        there = agg[:, bass.ds(b, 1), :].rearrange("p a c -> p (a c)")
                        dve.wait_ge(summed, t.n + 1)
                        wait(dve, added, t.n)
                        dve.tensor_tensor(there, there, banks[t.slot][:, 0:384], ALU.add).then_inc(taken, 1)
                        dve.wait_ge(taken, t.n + 1)
                        a2 = there.rearrange("p (x c) -> p x c", c=96)[:, 1:4, CS:96]
                        dve.tensor_tensor(a2, a2, banks[t.slot][:, 384:480].rearrange("p (x c) -> p x c", x=3),
                                          ALU.subtract).then_inc(added, 1)
                loop(dve, body, 0, STEPS + 1, STEPS)

            @block.tensor
            def _(pe):
                def mm(out, k, j, lo, width, start=False, stop=False):
                    return pe.matmul(out, hot[0][:, j, k, :], prod[0][:, k, lo:lo + width],
                                     start=start, stop=stop, skip_group_check=True)

                def body(m):
                    t = m
                    if t.inside(STEPS):
                        pe.wait_ge(zeroed, 1)
                        pe.wait_ge(query_in[t.slot], 32 * (t.half + 1))
                        for k in range(4):
                            wait(pe, prod_done, 4 * t.n - 3 + k)
                            pe.matmul(banks[2 + k][:, 0:WW], query[t.slot][:, P * k:P * k + P], w("tp"),
                                      start=True, stop=True).then_inc(weights, 1)
                        pe.wait_ge(hot_done, t.n + 1)
                        wait(pe, added, t.n - 1)
                        out = banks[t.slot]
                        for k in range(4):
                            mm(out[:, 0:CS], k, 0, 0, CS, start=(k == 0))
                            mm(out[:, 96:384].rearrange("p (x c) -> p x c", c=96)[:, :, CS:96], k, 0, 128, V3)
                            for j in range(3):
                                up, down = (j + 1) % 3, (j + 2) % 3
                                mm(out[:, 96 + 96 * j:96 + 96 * j + CS], k, j + 1, CS, CS)
                                mm(out[:, CS:96], k, j + 1, 320 + CV * j, CV)
                                mm(out[:, 96 + 96 * up + CS:192 + 96 * up], k, j + 1, 224 + CV * down, CV)
                                ins = mm(out[:, 384 + CV * down:416 + CV * down], k, j + 1, 224 + CV * up, CV,
                                         stop=(k == 3 and j == 2))
                        ins.then_inc(summed, 1)
                loop(pe, body, 0, STEPS, STEPS)


def conv_output(nc, g):
    nodes = g["nodes"]
    node_update(nc, g, "upd1", g["agg"], [(0, 96, "l2s", 0, CS)] + [(96 + 96 * x, 96, "l2v", CS + CV * x, CV) for x in range(3)],
                nodes, 1.0)
    normalise(nc, g, "ln2", [(nodes, 0, C, C, True)], nodes)
    with nc.semaphore("out_stored") as stored:
        with nc.Block() as block:
            @block.sync
            def _(sp):
                sp.dma_start(g["io"]["out"], nodes[:, :, :]).then_inc(stored, 16)
                sp.wait_ge(stored, 16)


def component_major(a):
    return np.concatenate([a[..., :CS], a[..., CS:].reshape(*a.shape[:-1], CV, 3).swapaxes(-1, -2).reshape(*a.shape[:-1], V3)], -1)


def lay_pack(i):
    W = {name: np.zeros((rows, cols), np.float32) for name, rows, cols in PACK}
    L0 = {k[7:]: np.asarray(v) for k, v in i.items() if k.startswith("L0_gnn_")}
    L1 = {k[7:]: np.asarray(v) for k, v in i.items() if k.startswith("L1_gnn_")}
    W["ident"][:] = np.eye(P)
    W["ones"][:] = 1
    W["iota"][:] = np.arange(P)
    W["count"][:] = np.arange(STEPS)
    W["sidx"][:] = np.arange(4 * P).reshape(4, P).T
    W["ts0"][:, :CS], W["ts0"][:, CS:] = L0["Ws_src"], L0["Ws_dst"]
    W["ts1"][:, :CS], W["ts1"][:, CS:] = L1["lin1_w0"], L1["si_w0"]
    rbf = L0["W_rbf"]
    ss, sv, vs, vv0, vv1 = rbf[:, :64], rbf[:, 64:128], rbf[:, 128:160], rbf[:, 160:192], rbf[:, 192:224]
    W["wy0"][0:16, 0:64], W["wy0"][64:80, 64:128] = ss, sv
    for name in ("gamma_s", "beta_s"):
        W[name][:, 0] = L0[name]
    W["m1a"][0:64, 0:64], W["m1a"][0:64, 64:128] = L0["W_alpha"][0:64], L0["Ws_val"][0:64]
    for h in range(H):
        W["adot"][AS * h:AS * h + AS, h] = L0["alpha_dot"][0, h]
    Wsv = L0["Ws_vlin"].reshape(CS + CV, H, AS)
    Wvv = L0["Wv_vlin"].reshape(CS + 2 * CV, H, AV)
    mu1, mu2, mv1 = (W[n].reshape(-1, H, c) for n, c in (("mu1", 24), ("mu2", 16), ("mv1", 16)))
    mv = {n: W[n].reshape(V3, H, 3, AV) for n in ("mv0", "mv2", "mv3")}
    mu1[0:64, :, 0:16], mu1[64:128, :, 16:24] = Wsv[0:64], Wvv[0:64]
    mu2[0:64, :, 0:8], mu2[64:128, :, 8:16] = Wvv[0:64], Wvv[0:64]
    W["r_mu1"][0:64, 0], W["r_mu1"][64:128, 0] = L0["w2_ss"], L0["w2_sv"]
    W["r_mu2"][0:64, 0], W["r_mu2"][64:128, 0] = L0["w2_sv"], L0["w2_sv"]
    for x in range(3):
        r, up, down = slice(CV * x, CV * x + CV), (x + 1) % 3, (x + 2) % 3
        W["tv0"][r, CV * x:CV * x + CV], W["tv0"][r, V3 + CV * x:V3 + CV * x + CV] = L0["Wv_src"], L0["Wv_dst"]
        W["tv1"][r, CV * x:CV * x + CV], W["tv1"][r, V3 + CV * x:V3 + CV * x + CV] = L1["lin1_w1"], L1["si_w1"]
        W["gamma_v"][r, 0] = L0["gamma_v"]
        W["wy1"][16 + 16 * x:32 + 16 * x, r] = vv0
        W["wy2"][0:16, r] = vs
        W["wy3"][16 + 16 * up:32 + 16 * up, r] = vv1
        W["wy4"][16 + 16 * down:32 + 16 * down, r] = vv1
        W["m1b"][r, 0:64], W["m1b"][r, 64:128] = L0["W_alpha"][64:96], L0["Ws_val"][64:96]
        W["p1"][64:128, r] = L0["Wv_val"][0:64]
        W["vb"][r, r] = L0["Wv_val"][64:96]
        W["vc1"][r, CV * down:CV * down + CV] = L0["Wv_val"][96:128]
        W["vc2"][r, CV * up:CV * up + CV] = L0["Wv_val"][96:128]
        W["wg"][64:128, r] = L0["Wg"]
        mv1[r] = Wsv[64:96]
        mv["mv0"][r, :, x] = Wvv[64:96]
        mv["mv2"][r, :, down] = Wvv[96:128]
        mv["mv3"][r, :, up] = Wvv[96:128]
        for n, s in (("r_vs", "w2_vs"), ("r_vv0", "w2_vv0"), ("r_vv1", "w2_vv1")):
            W[n][r, 0] = L0[s]
    for h in range(H):
        part, at = W[f"wp{h // 2}"], HEAD * (h % 2)
        part[at:at + AS, 0:CS] = L0["Wps"][AS * h:AS * h + AS]
        for x in range(3):
            part[at + AS + AV * x:at + AS + AV * x + AV, CS + CV * x:CS + CV * x + CV] = L0["Wpv"][AV * h:AV * h + AV]
    W["tp"][0:64] = L1["tp_weight"]
    W["l2s"][:], W["l2v"][:] = L1["lin2_w0"], L1["lin2_w1"]
    out = np.zeros((P, PACKW), np.float32)
    for name, (rows, at, cols) in PLACE.items():
        out[0:rows, at:at + cols] = W[name].reshape(rows, cols)
    return out


def lay_inputs(i):
    E = SUPER * 512
    x = component_major(np.asarray(i["x"]))
    x = np.pad(x, ((0, BLOCKS * P - NODES), (0, 0))).reshape(BLOCKS, P, C).transpose(1, 0, 2)
    src = np.pad(np.asarray(i["src"]), (0, E - EDGES))
    dst_all = np.pad(np.asarray(i["dst"]), (0, SCANT * P - EDGES), constant_values=NODES)
    dst = dst_all[:E]
    both = np.stack([src.reshape(SUPER, 4, P), dst.reshape(SUPER, 4, P)], 1)
    eidx = both.transpose(0, 3, 1, 2).reshape(SUPER, P, 8)
    far = np.array([FAR], dst.dtype)
    sdst = np.concatenate([far, dst[512::512], np.repeat(far, 512 - SUPER)]).reshape(4, P).T
    no = np.array([-1], dst.dtype)
    dst3 = np.stack([dst_all, np.concatenate([no, dst_all[:-1]]), np.concatenate([dst_all[1:], no])]).reshape(3, P, SCANT)
    y = np.pad(np.asarray(i["edge_attr_4"]), ((0, E - EDGES), (0, 0))).reshape(SUPER, 512, 4)
    ey = y.reshape(SUPER, 4, P, 4).transpose(0, 2, 1, 3).reshape(SUPER, P, 16)
    yt = y.transpose(0, 2, 1)
    rbf = np.pad(np.asarray(i["edge_attr_16"]), ((0, E - EDGES), (0, 0))).reshape(SUPER, 512, 16).transpose(0, 2, 1)
    query = np.pad(np.asarray(i["edge_attr_64"]), ((0, E - EDGES), (0, 0))).reshape(SUPER, 512, 64).transpose(0, 2, 1)
    return dict(
        pack=lay_pack(i), x=x, eidx=eidx, sdst=sdst, dst3=dst3, ey=ey,
        rbf5=np.tile(rbf, (1, 5, 1)), y16=np.repeat(yt, 16, axis=1),
        ys=yt[:, [0, 2, 1, 3]].reshape(SUPER, 2, 1024),
        yv=yt[:, [1, 2, 3, 0, 2, 3, 1, 0, 3, 1, 2, 0]].reshape(SUPER, 3, 2048),
        query=query)


def kernel(**inputs):
    import numpy as _np
    import concourse.bacc as _bacc
    from concourse import mybir as _mybir
    from concourse.bass_utils import run_bass_kernel_spmd as _run

    nc = _bacc.Bacc("TRN2", target_bir_lowering=False, num_devices=1)
    arrays, io = {}, {}
    for name, a in lay_inputs(inputs).items():
        a = _np.ascontiguousarray(a)
        arrays[f"in_{name}"] = a
        io[name] = nc.dram_tensor(f"in_{name}", a.shape, _mybir.dt.from_np(a.dtype), kind="ExternalInput").ap()
    io["out"] = nc.dram_tensor("out_nodes", (P, BLOCKS, C), F32, kind="ExternalOutput").ap()
    gnn(nc, io)
    r = _run(nc, [arrays], core_ids=[0])
    got = r.results[0]["out_nodes"]
    got = got.transpose(1, 0, 2).reshape(BLOCKS * P, C)[:NODES]
    return _np.concatenate([got[:, :CS], got[:, CS:].reshape(NODES, 3, CV).swapaxes(1, 2).reshape(NODES, V3)], 1)
```

```python
from contextlib import ExitStack

import concourse.bass as bass
from concourse import mybir
import numpy as np

ALU = mybir.AluOpType
ACT = mybir.ActivationFunctionType
AX = mybir.AxisListType.X
F32 = mybir.dt.float32
I32 = mybir.dt.int32

P = 128
NODES = 6250
EDGES = 206250
CS, CV, H, AS, AV, NB = 64, 32, 4, 16, 8, 16
V3 = 3 * CV
C = CS + V3
C5 = CS + 5 * CV
BLOCKS = -(-NODES // P)
SUPER = -(-EDGES // 512) + (-(-EDGES // 512)) % 2
STEPS = SUPER + BLOCKS - 1
SCANG = -(-SUPER * 4 // P)
SCANT = SCANG * P
HEAD = AS + 3 * AV
BIG = 1.5e38
FAR = 1 << 20
EPS = 1e-5
STEPS += STEPS % 2

PACK = [
    ("ident", 128, 128), ("ones", 128, 128), ("iota", 128, 128), ("count", 128, STEPS), ("sidx", 128, 4),
    ("ts0", 64, 128), ("tv0", 96, 192), ("gamma_s", 64, 1), ("beta_s", 64, 1), ("gamma_v", 96, 1),
    ("wy0", 80, 128), ("wy1", 80, 96), ("wy2", 80, 96), ("wy3", 80, 96), ("wy4", 80, 96),
    ("m1a", 128, 128), ("m1b", 96, 128), ("p1", 128, 96), ("vb", 96, 96), ("vc1", 96, 96), ("vc2", 96, 96),
    ("wg", 128, 96), ("adot", 64, 4), ("mu1", 128, 96), ("mu2", 128, 64), ("mv1", 96, 64), ("mv0", 96, 96),
    ("mv2", 96, 96), ("mv3", 96, 96), ("r_mu1", 128, 1), ("r_mu2", 128, 1), ("r_vs", 96, 1), ("r_vv0", 96, 1),
    ("r_vv1", 96, 1), ("wp0", 80, 160), ("wp1", 80, 160), ("ts1", 64, 128), ("tv1", 96, 256), ("tp", 128, 256),
    ("l2s", 96, 64), ("l2v", 96, 32),
]
PLACE, PACKW = {}, 0
for _name, _rows, _cols in PACK:
    PLACE[_name] = (_rows, PACKW, _cols)
    PACKW += _cols


class At:

    def __init__(self, n, quarter, slot4):
        self.n, self.quarter, self.slot4 = n, quarter, slot4
        self.half, self.slot = 2 * quarter + slot4 // 2, slot4 % 2

    def __add__(self, d):
        return At(self.n + d, self.quarter + (self.slot4 + d) // 4, (self.slot4 + d) % 4)

    def inside(self, count):
        return not isinstance(self.n, int) or 0 <= self.n < count


def loop(eng, body, first, last, count):
    lo = 4
    hi = count - 4
    for m in range(first, lo):
        body(At(m, m // 4, m % 4))
    with eng.Fori(lo // 4, hi // 4) as i:
        for u in range(4):
            body(At(4 * i + u, i, u))
    for m in range(hi, last):
        body(At(m, m // 4, m % 4))


def blocks(eng, body):
    for m in range(5):
        body(At(m, m // 4, m % 4))
    with eng.Fori(1, BLOCKS // 4) as i:
        for u in range(1, 5):
            body(At(4 * i + u, i + u // 4, u % 4))


def wait(eng, sem, value):
    if not isinstance(value, int) or value > 0:
        eng.wait_ge(sem, value)


def gnn(nc, io):
    tab_src = nc.dram_tensor("tab_src", [BLOCKS * P, C], F32).ap()
    tab_dst = nc.dram_tensor("tab_dst", [BLOCKS * P, C], F32).ap()
    tab_conv = nc.dram_tensor("tab_conv", [BLOCKS * P, C5], F32).ap()
    h_dram = nc.dram_tensor("h_dram", [SUPER, P, 4 * C], F32).ap()
    ex_dram = nc.dram_tensor("ex_dram", [SCANT // 4, P, 16], F32).ap()

    with ExitStack() as top:
        pack = top.enter_context(nc.sbuf_tensor("pack_sb", [P, PACKW], F32))
        nodes = top.enter_context(nc.sbuf_tensor("nodes", [P, BLOCKS, C], F32))
        block128 = top.enter_context(nc.sbuf_tensor("block128", [P, STEPS], F32))
        step_s = top.enter_context(nc.sbuf_tensor("step_s", [P, STEPS], I32))
        step_b = top.enter_context(nc.sbuf_tensor("step_b", [P, STEPS], I32))
        psum = top.enter_context(nc.psum_tensor("psum", [P, 8, 512], F32))
        banks = [psum[:, i, :] for i in range(8)]
        g = dict(psum=psum, pack=pack, nodes=nodes, block128=block128, step_s=step_s, step_b=step_b, banks=banks,
                 tab_src=tab_src, tab_dst=tab_dst, tab_conv=tab_conv, h_dram=h_dram, ex_dram=ex_dram, io=io)

        def w(name):
            rows, at, cols = PLACE[name]
            return pack[0:rows, at:at + cols]
        g["w"] = w

        constants(nc, g)
        attention_input(nc, g)
        with ExitStack() as mid:
            g["alpha"] = mid.enter_context(nc.sbuf_tensor("alpha", [P, SCANT, H], F32))
            attention_edges(nc, g)
            segment_softmax(nc, g)
        with ExitStack() as mid:
            g["agg"] = mid.enter_context(nc.sbuf_tensor("agg0", [P, BLOCKS, C + H], F32))
            attention_aggregate(nc, g)
            attention_output(nc, g)
        with ExitStack() as mid:
            g["agg"] = mid.enter_context(nc.sbuf_tensor("agg1", [P, BLOCKS, 512], F32))
            conv_edges(nc, g)
            conv_output(nc, g)


def constants(nc, g):
    w, io, pack = g["w"], g["io"], g["pack"]
    scaled = [("m1b", None, 3 ** -0.5), ("vc1", None, 2 ** -0.5), ("vc2", None, -(2 ** -0.5)),
              ("mu1", "r_mu1", 1.0), ("mu2", "r_mu2", 1.0), ("mv1", "r_vv0", 3 ** -0.5), ("mv0", "r_vs", 1.0),
              ("mv2", "r_vv1", 2 ** -0.5), ("mv3", "r_vv1", -(2 ** -0.5)),
              ("ts1", None, CS ** -0.5), ("tv1", None, CV ** -0.5),
              ("l2s", None, (CS + CV) ** -0.5 / 10.0), ("l2v", None, (CS + CV) ** -0.5 / 10.0)]
    with ExitStack() as ctx:
        sdst = ctx.enter_context(nc.sbuf_tensor("sdst", [P, 4], I32))
        sblk = ctx.enter_context(nc.sbuf_tensor("sblk", [P, 4], I32))
        start = ctx.enter_context(nc.sbuf_tensor("start", [P, 4], F32))
        start2 = ctx.enter_context(nc.sbuf_tensor("start2", [P, 4], F32))
        begun = ctx.enter_context(nc.sbuf_tensor("begun", [P, 4, STEPS], F32))
        s_f = ctx.enter_context(nc.sbuf_tensor("s_f", [P, STEPS], F32))
        b_f = ctx.enter_context(nc.sbuf_tensor("b_f", [P, STEPS], F32))
        loaded = ctx.enter_context(nc.semaphore("const_loaded"))
        chain = ctx.enter_context(nc.semaphore("const_chain"))
        summed = ctx.enter_context(nc.semaphore("const_summed"))
        with nc.Block() as block:
            @block.sync
            def _(sp):
                sp.dma_start(pack[:, :], io["pack"]).then_inc(loaded, 16)
                sp.dma_start(sdst[:, :], io["sdst"]).then_inc(loaded, 16)
                sp.dma_start(g["nodes"][:, :, :], io["x"]).then_inc(loaded, 16)

            @block.vector
            def _(dve):
                links = [0]

                def link(ins):
                    links[0] += 1
                    ins.then_inc(chain, 1)
                    dve.wait_ge(chain, links[0])

                dve.wait_ge(loaded, 48)
                link(dve.tensor_scalar(sblk[:, :], sdst[:, :], 7, None, ALU.logical_shift_right))
                link(dve.tensor_copy(start[:, :], sblk[:, :]))
                link(dve.tensor_tensor(start2[:, :], start[:, :], w("sidx"), ALU.add))
                for c in range(4):
                    ins = dve.tensor_scalar(begun[:, c, :], w("count"), start2[:, c:c + 1], None, ALU.is_ge)
                link(ins)
                for name, rows, const in scaled:
                    if rows:
                        ins = dve.tensor_scalar(w(name), w(name), w(rows), const, ALU.mult, ALU.mult)
                    else:
                        ins = dve.tensor_scalar(w(name), w(name), const, None, ALU.mult)
                at = PLACE["tp"][1]
                for a, b, const in ((128, 160, 2 ** -0.5), (160, 192, 3 ** -0.5), (192, 256, 0.5)):
                    ins = dve.tensor_scalar(pack[:, at + a:at + b], pack[:, at + a:at + b], const, None, ALU.mult)
                link(ins)
                dve.wait_ge(summed, 1)
                link(dve.tensor_copy(s_f[:, :], g["banks"][0][:, 0:STEPS]))
                link(dve.tensor_tensor(b_f[:, :], w("count"), s_f[:, :], ALU.subtract))
                dve.tensor_scalar(g["block128"][:, :], b_f[:, :], float(P), None, ALU.mult)
                dve.tensor_copy(g["step_s"][:, :], s_f[:, :])
                link(dve.tensor_scalar(g["step_b"][:, :], b_f[:, :], float(BLOCKS - 1), None, ALU.min))

            @block.tensor
            def _(pe):
                pe.wait_ge(chain, 4)
                for c in range(4):
                    ins = pe.matmul(g["banks"][0][:, 0:STEPS], w("ones"), begun[:, c, :], start=(c == 0), stop=(c == 3))
                ins.then_inc(summed, 1)


def node_tables(nc, g, tag, values, ts, tv, scales, outputs, base):
    w, banks = g["w"], g["banks"]
    with ExitStack() as ctx:
        def sb(name, shape):
            return ctx.enter_context(nc.sbuf_tensor(f"{tag}_{name}", shape, F32))

        def sem(name):
            return ctx.enter_context(nc.semaphore(f"{tag}_{name}"))
        row, feat = sb("row", [P, C]), sb("feat", [P, 2, P])
        width = outputs[0].shape[1]
        turn = width - CS
        out = sb("out", [P, 2, 2, width])
        picked, turned, kept, mapped, evacuated, summed = (sem(x) for x in (
            "picked", "turned", "kept", "mapped", "evacuated", "summed"))
        stored = [sem("stored0"), sem("stored1")]
        with nc.Block() as block:
            @block.vector
            def _(dve):
                def body(at):
                    wait(dve, turned, at.n)
                    if base is not None:
                        wait(dve, evacuated, at.n)
                    dve.tensor_copy(row[:, :], values[:, bass.ds(at.n, 1), :].rearrange("p a c -> p (a c)")).then_inc(picked, 1)
                    dve.wait_ge(mapped, at.n + 1)
                    wait(dve, stored[at.slot], at.half * (32 if base is None else 16))
                    for o in range(2 if base is None else 1):
                        dve.tensor_copy(out[:, at.slot, o, 0:CS], banks[2][:, o * CS:(o + 1) * CS])
                        ins = dve.tensor_copy(out[:, at.slot, o, CS:width], banks[3][:, o * turn:(o + 1) * turn])
                    ins.then_inc(summed, 1)
                    if base is not None:
                        there = base[:, bass.ds(at.n, 1), :].rearrange("p a c -> p (a c)")
                        dve.tensor_tensor(there[:, 0:CS], row[:, 0:CS], banks[2][:, CS:2 * CS], ALU.add)
                        dve.tensor_tensor(there[:, CS:C], row[:, CS:C], banks[3][:, turn:turn + V3], ALU.add).then_inc(evacuated, 1)
                blocks(dve, body)

            @block.tensor
            def _(pe):
                def body(at):
                    pe.wait_ge(picked, at.n + 1)
                    wait(pe, kept, at.n)
                    pe.transpose(banks[1][0:V3, 0:P], row[:, CS:C], w("ident"))
                    pe.transpose(banks[0][0:CS, 0:P], row[:, 0:CS], w("ident")).then_inc(turned, 1)
                    pe.wait_ge(kept, at.n + 1)
                    wait(pe, summed if base is None else evacuated, at.n)
                    pe.matmul(banks[2][:, 0:2 * CS], feat[0:CS, 0, :], w(ts), start=True, stop=True)
                    pe.matmul(banks[3][:, 0:turn + V3], feat[0:V3, 1, :], w(tv), start=True, stop=True).then_inc(mapped, 1)
                blocks(pe, body)

            @block.scalar
            def _(act):
                def body(at):
                    act.wait_ge(turned, at.n + 1)
                    wait(act, mapped, at.n)
                    if scales:
                        act.activation(feat[0:CS, 0, :], banks[0][0:CS, 0:P], ACT.Identity,
                                       bias=w(scales[1]), scale=w(scales[0]))
                        act.activation(feat[0:V3, 1, :], banks[1][0:V3, 0:P], ACT.Identity,
                                       scale=w(scales[2])).then_inc(kept, 1)
                    else:
                        act.activation(feat[0:CS, 0, :], banks[0][0:CS, 0:P], ACT.Copy)
                        act.activation(feat[0:V3, 1, :], banks[1][0:V3, 0:P], ACT.Copy).then_inc(kept, 1)
                blocks(act, body)

            @block.sync
            def _(sp):
                def body(at):
                    sp.wait_ge(summed, at.n + 1)
                    for o, table in enumerate(outputs):
                        sp.dma_start(table.rearrange("(b p) c -> b p c", p=P)[bass.ds(at.n, 1), :, :].rearrange("a p c -> (a p) c"),
                                     out[:, at.slot, o, :]).then_inc(stored[at.slot], 16)
                blocks(sp, body)
                sp.wait_ge(stored[0], 16 * len(outputs) * ((BLOCKS + 1) // 2))
                sp.wait_ge(stored[1], 16 * len(outputs) * (BLOCKS // 2))


def normalise(nc, g, tag, groups, out):
    with ExitStack() as ctx:
        square = ctx.enter_context(nc.sbuf_tensor(f"{tag}_square", [P, BLOCKS, C], F32))
        mean = ctx.enter_context(nc.sbuf_tensor(f"{tag}_mean", [P, BLOCKS], F32))
        mean1 = ctx.enter_context(nc.sbuf_tensor(f"{tag}_mean1", [P, BLOCKS], F32))
        var = ctx.enter_context(nc.sbuf_tensor(f"{tag}_var", [P, BLOCKS], F32))
        var1 = ctx.enter_context(nc.sbuf_tensor(f"{tag}_var1", [P, BLOCKS], F32))
        dev = ctx.enter_context(nc.sbuf_tensor(f"{tag}_dev", [P, BLOCKS], F32))
        inv = ctx.enter_context(nc.sbuf_tensor(f"{tag}_inv", [P, BLOCKS], F32))
        chain = ctx.enter_context(nc.semaphore(f"{tag}_chain"))
        rooted = ctx.enter_context(nc.semaphore(f"{tag}_rooted"))
        varied = ctx.enter_context(nc.semaphore(f"{tag}_varied"))
        with nc.Block() as block:
            @block.vector
            def _(dve):
                links = [0]

                def link(ins):
                    links[0] += 1
                    ins.then_inc(chain, 1)
                    dve.wait_ge(chain, links[0])

                for n, (src, lo, hi, divisor, centre) in enumerate(groups):
                    width = hi - lo
                    spread = [P, BLOCKS, width]
                    if centre:
                        link(dve.tensor_reduce(mean[:, :], src[:, :, lo:hi], AX, ALU.add))
                        link(dve.tensor_scalar(mean1[:, :], mean[:, :], 1.0 / width, None, ALU.mult))
                        link(dve.tensor_tensor(out[:, :, lo:hi], src[:, :, lo:hi],
                                               mean1[:, :].unsqueeze(2).to_broadcast(spread), ALU.subtract))
                        src = out
                    link(dve.tensor_tensor(square[:, :, lo:hi], src[:, :, lo:hi], src[:, :, lo:hi], ALU.mult))
                    link(dve.tensor_reduce(var[:, :], square[:, :, lo:hi], AX, ALU.add))
                    link(dve.tensor_scalar(var1[:, :], var[:, :], 1.0 / divisor, EPS, ALU.mult, ALU.add))
                    dve.sem_inc(varied, 1)
                    dve.wait_ge(rooted, n + 1)
                    link(dve.reciprocal(inv[:, :], dev[:, :]))
                    link(dve.tensor_tensor(out[:, :, lo:hi], src[:, :, lo:hi],
                                           inv[:, :].unsqueeze(2).to_broadcast(spread), ALU.mult))

            @block.scalar
            def _(act):
                for n in range(len(groups)):
                    act.wait_ge(varied, n + 1)
                    act.activation(dev[:, :], var1[:, :], ACT.Sqrt).then_inc(rooted, 1)


def attention_input(nc, g):
    with ExitStack() as ctx:
        normed = ctx.enter_context(nc.sbuf_tensor("normed", [P, BLOCKS, C], F32))
        normalise(nc, g, "ln0", [(g["nodes"], 0, CS, CS, True), (g["nodes"], CS, C, CV, False)], normed)
        node_tables(nc, g, "tab0", normed, "ts0", "tv0", ("gamma_s", "beta_s", "gamma_v"),
                    [g["tab_src"], g["tab_dst"]], None)


def attention_edges(nc, g):
    w, banks, io = g["w"], g["banks"], g["io"]
    with ExitStack() as ctx:
        def sb(name, shape, dt=F32):
            return ctx.enter_context(nc.sbuf_tensor(f"ae_{name}", shape, dt))

        def sem(name):
            return ctx.enter_context(nc.semaphore(f"ae_{name}"))
        idx = [sb(f"idx{u}", [P, 8], I32) for u in range(2)]
        gsrc = [sb(f"gsrc{u}", [P, 4, C]) for u in range(2)]
        gdst = [sb(f"gdst{u}", [P, 4, C]) for u in range(2)]
        rbf = [sb(f"rbf{u}", [80, 512]) for u in range(2)]
        y16 = [sb(f"y16_{u}", [80, 512]) for u in range(2)]
        rbfy = [sb(f"rbfy{u}", [80, 512]) for u in range(2)]
        ys = [sb(f"ys{u}", [P, 2, 512]) for u in range(2)]
        yv = [sb(f"yv{u}", [V3, 4, 512]) for u in range(2)]
        hsb = [sb(f"hsb{u}", [P, 4, C]) for u in range(2)]
        msg = sb("msg", [P, 4, C + CS])
        sT, vT = sb("sT", [P, 512]), sb("vT", [V3, 512])
        q = sb("q", [P, 5, 512])
        av = sb("av", [P, 512])
        leaky = sb("leaky", [CS, 512])
        sig = sb("sig", [P, 512])
        gate = sb("gate", [V3, 512])
        vy, vsum, vval = sb("vy", [V3, 512]), sb("vsum", [V3, 512]), sb("vval", [V3, 512])
        uy = sb("uy", [P, 2, 512])
        vvy = sb("vvy", [V3, 4, 512])
        filled, may_gather = sem("filled"), sem("may_gather")
        idx_in = [sem(f"idx_in{u}") for u in range(2)]
        rbf_in = [sem(f"rbf_in{u}") for u in range(2)]
        y_in = [sem(f"y_in{u}") for u in range(2)]
        gathered = [sem(f"gathered{u}") for u in range(2)]
        stored = [sem(f"stored{u}") for u in range(2)]
        summed, spread, multiplied, vy_done, vsum_done, leaky_done, vval_done, uy_done, vvy_done = (sem(x) for x in (
            "summed", "spread", "multiplied", "vy_done", "vsum_done", "leaky_done", "vval_done", "uy_done", "vvy_done"))
        pe_turned, pe_w, pe_av, pe_p1, pe_vv, pe_h, pe_gate, pe_alpha = (sem(x) for x in (
            "pe_turned", "pe_w", "pe_av", "pe_p1", "pe_vv", "pe_h", "pe_gate", "pe_alpha"))
        av_kept, sig_done, h_kept, gate_done, turned_kept, alpha_kept = (sem(x) for x in (
            "av_kept", "sig_done", "h_kept", "gate_done", "turned_kept", "alpha_kept"))
        b_w, b_s, b_v, b_av, b_p1, b_vv, b_h = banks[0:2], banks[2], banks[3], banks[4], banks[5], banks[6], banks[7]
        MS = (P, V3, V3, V3, V3)

        with nc.Block() as block:
            @block.sync
            def _(sp):
                def body(m):
                    t = m + 2
                    if t.inside(SUPER):
                        wait(sp, summed, t.n - 1)
                        wait(sp, spread, t.n - 1)
                        sp.dma_start(idx[t.slot][:, :], io["eidx"][t.n]).then_inc(idx_in[t.slot], 16)
                        sp.dma_start(rbf[t.slot][:, :], io["rbf5"][t.n]).then_inc(rbf_in[t.slot], 16)
                        sp.dma_start(y16[t.slot][0:CS, :], io["y16"][t.n]).then_inc(rbf_in[t.slot], 16)
                    t = m + -2
                    if t.inside(SUPER):
                        sp.wait_ge(h_kept, 2 * t.n + 2)
                        sp.dma_start(g["h_dram"][t.n], hsb[t.slot][:, :, :].rearrange("p k c -> p (k c)"))\
                            .then_inc(stored[t.slot], 16)
                    t = m + 1
                    if t.inside(SUPER):
                        wait(sp, vvy_done, t.n - 1)
                        for j in range(2):
                            sp.dma_start(ys[t.slot][CS * j:CS * j + CS, :, :].rearrange("p a e -> p (a e)"),
                                         io["ys"][t.n, j:j + 1, :].to_broadcast([CS, 1024])).then_inc(y_in[t.slot], 16)
                        for j in range(3):
                            sp.dma_start(yv[t.slot][CV * j:CV * j + CV, :, :].rearrange("p a e -> p (a e)"),
                                         io["yv"][t.n, j:j + 1, :].to_broadcast([CV, 2048])).then_inc(y_in[t.slot], 16)
                loop(sp, body, -2, SUPER + 2, SUPER)
                for u in range(2):
                    sp.wait_ge(stored[u], 16 * (SUPER // 2))

            @block.gpsimd
            def _(pool):
                def body(t):
                    pool.wait_ge(idx_in[t.slot], 16 * (t.half + 1))
                    wait(pool, summed, t.n - 1)
                    pool.sem_inc(may_gather, 1)
                    for k in range(4):
                        pool.indirect_dma_start(gsrc[t.slot][:, k, :], None, g["tab_src"],
                                                bass.IndirectOffsetOnAxis(ap=idx[t.slot][:, k:k + 1], axis=0))\
                            .then_inc(gathered[t.slot], 16)
                        pool.indirect_dma_start(gdst[t.slot][:, k, :], None, g["tab_dst"],
                                                bass.IndirectOffsetOnAxis(ap=idx[t.slot][:, 4 + k:5 + k], axis=0))\
                            .then_inc(gathered[t.slot], 16)
                loop(pool, body, 0, SUPER, SUPER)

            @block.vector
            def _(dve):
                dve.memset(y16[0][CS:80, :], 1.0)
                dve.memset(y16[1][CS:80, :], 1.0)
                dve.memset(g["alpha"][:, 4 * SUPER:SCANT, :], 0.0).then_inc(filled, 1)
                dve.wait_ge(filled, 1)

                def body(m):
                    t = m + -1
                    if t.inside(SUPER):
                        dve.wait_ge(pe_p1, t.n + 1)
                        dve.wait_ge(y_in[t.slot], 80 * (t.half + 1))
                        wait(dve, vsum_done, t.n)
                        dve.tensor_tensor(vy[:, :], b_p1[0:V3, :], yv[t.slot][:, 0, :], ALU.mult).then_inc(vy_done, 1)
                        dve.wait_ge(pe_vv, t.n + 1)
                        dve.wait_ge(vy_done, t.n + 1)
                        wait(dve, vval_done, t.n)
                        dve.tensor_tensor(vsum[:, :], b_vv[0:V3, :], vy[:, :], ALU.add).then_inc(vsum_done, 1)
                        dve.wait_ge(av_kept, t.n + 1)
                        wait(dve, pe_alpha, t.n)
                        dve.scalar_tensor_tensor(leaky[:, :], av[0:CS, :], 0.2, av[0:CS, :], ALU.mult, ALU.max)\
                            .then_inc(leaky_done, 1)
                    t = m + 1
                    if t.inside(SUPER):
                        dve.wait_ge(gathered[t.slot], 128 * (t.half + 1))
                        wait(dve, pe_turned, t.n)
                        dve.tensor_tensor(msg[:, :, 0:CS], gsrc[t.slot][:, :, 0:CS], gdst[t.slot][:, :, 0:CS], ALU.add)
                        dve.tensor_tensor(msg[:, :, CS:CS + C], gsrc[t.slot][:, :, :], gdst[t.slot][:, :, :], ALU.add)\
                            .then_inc(summed, 1)
                        dve.wait_ge(rbf_in[t.slot], 32 * (t.half + 1))
                        wait(dve, pe_w, 5 * t.n - 5)
                        dve.tensor_tensor(rbfy[t.slot][:, :], rbf[t.slot][:, :], y16[t.slot][:, :], ALU.mult)\
                            .then_inc(spread, 1)
                    t = m
                    if t.inside(SUPER):
                        dve.wait_ge(turned_kept, t.n + 1)
                        wait(dve, pe_vv, t.n)
                        for c in range(5):
                            dve.wait_ge(pe_w, 5 * t.n + c + 1)
                            dve.tensor_tensor(q[0:MS[c], c, :], b_w[(t.slot + c) % 2][0:MS[c], :],
                                              (sT if c == 0 else vT)[:, :], ALU.mult).then_inc(multiplied, 1)
                    t = m + -1
                    if t.inside(SUPER):
                        dve.wait_ge(gate_done, t.n + 1)
                        dve.wait_ge(vsum_done, t.n + 1)
                        wait(dve, vvy_done, t.n)
                        dve.tensor_tensor(vval[:, :], vsum[:, :], gate[:, :], ALU.mult).then_inc(vval_done, 1)
                        dve.wait_ge(sig_done, t.n + 1)
                        wait(dve, pe_h, 2 * t.n)
                        dve.tensor_tensor(uy[:, :, :], sig[:, :].unsqueeze(1).to_broadcast([P, 2, 512]),
                                          ys[t.slot][:, :, :], ALU.mult).then_inc(uy_done, 1)
                        dve.wait_ge(vval_done, t.n + 1)
                        dve.tensor_tensor(vvy[:, :, :], vval[:, :].unsqueeze(1).to_broadcast([V3, 4, 512]),
                                          yv[t.slot][:, :, :], ALU.mult).then_inc(vvy_done, 1)
                loop(dve, body, -1, SUPER + 1, SUPER)

            @block.tensor
            def _(pe):
                def values(t, half, bank):
                    for k in (0, 1):
                        e = slice(P * (2 * half + k), P * (2 * half + k) + P)
                        o = bank[:, C * k:C * k + C].rearrange("p (h c) -> p h c", h=H)
                        pe.matmul(o[:, :, 0:24], uy[:, 0, e], w("mu1"), start=True, stop=False)
                        pe.matmul(o[:, :, 24:40], uy[:, 1, e], w("mu2"), start=False, stop=False)
                        pe.matmul(o[:, :, 0:16], vvy[:, 0, e], w("mv1"), start=False, stop=False)
                        pe.matmul(o[:, :, 16:40], vvy[:, 3, e], w("mv0"), start=False, stop=False)
                        pe.matmul(o[:, :, 16:40], vvy[:, 1, e], w("mv2"), start=False, stop=False)
                        ins = pe.matmul(o[:, :, 16:40], vvy[:, 2, e], w("mv3"), start=False, stop=True)
                    ins.then_inc(pe_h, 1)

                def body(m):
                    t = m + -1
                    if t.inside(SUPER):
                        pe.wait_ge(multiplied, 5 * t.n + 5)
                        wait(pe, av_kept, t.n)
                        pe.matmul(b_av[:, :], w("m1a"), q[:, 0, :], start=True, stop=False)
                        pe.matmul(b_av[:, :], w("m1b"), q[0:V3, 1, :], start=False, stop=True).then_inc(pe_av, 1)
                        wait(pe, gate_done, t.n)
                        pe.matmul(b_p1[0:V3, :], w("p1"), q[:, 0, :], start=True, stop=True).then_inc(pe_p1, 1)
                        wait(pe, vsum_done, t.n)
                        pe.matmul(b_vv[0:V3, :], w("vb"), q[0:V3, 2, :], start=True, stop=False)
                        pe.matmul(b_vv[0:V3, :], w("vc1"), q[0:V3, 3, :], start=False, stop=False)
                        pe.matmul(b_vv[0:V3, :], w("vc2"), q[0:V3, 4, :], start=False, stop=True).then_inc(pe_vv, 1)
                    t = m + -2
                    if t.inside(SUPER):
                        pe.wait_ge(vvy_done, t.n + 1)
                        wait(pe, h_kept, 2 * t.n)
                        values(t, 0, b_h)
                        wait(pe, turned_kept, min(t.n + 3, SUPER) if isinstance(t.n, int) else t.n + 3)
                        values(t, 1, b_s)
                    t = m + -1
                    if t.inside(SUPER):
                        pe.wait_ge(av_kept, t.n + 1)
                        pe.wait_ge(vy_done, t.n + 1)
                        pe.matmul(b_p1[0:V3, :], w("wg"), av[:, :], start=True, stop=True).then_inc(pe_gate, 1)
                    t = m
                    if t.inside(SUPER):
                        pe.wait_ge(spread, t.n + 1)
                        for c in range(5):
                            wait(pe, multiplied, 5 * t.n + c - 1)
                            pe.matmul(b_w[(t.slot + c) % 2][0:MS[c], :], w(f"wy{c}"), rbfy[t.slot][:, :],
                                      start=True, stop=True).then_inc(pe_w, 1)
                    t = m + 1
                    if t.inside(SUPER):
                        pe.wait_ge(summed, t.n + 1)
                        wait(pe, h_kept, 2 * t.n - 4)
                        wait(pe, turned_kept, t.n)
                        for k in range(4):
                            pe.transpose(b_s[:, P * k:P * k + P], msg[:, k, 0:P], w("ident"))
                        for k in range(4):
                            ins = pe.transpose(b_v[0:V3, P * k:P * k + P], msg[:, k, P:P + V3], w("ident"))
                        ins.then_inc(pe_turned, 1)
                    t = m + -1
                    if t.inside(SUPER):
                        pe.wait_ge(leaky_done, t.n + 1)
                        wait(pe, alpha_kept, t.n)
                        wait(pe, h_kept, 2 * t.n - 1)
                        for k in range(4):
                            ins = pe.matmul(b_h[:, 320 + 4 * k:324 + 4 * k], leaky[:, P * k:P * k + P], w("adot"),
                                            start=True, stop=True)
                        ins.then_inc(pe_alpha, 1)
                loop(pe, body, -1, SUPER + 2, SUPER)

            @block.scalar
            def _(act):
                def body(m):
                    t = m + -1
                    if t.inside(SUPER):
                        act.wait_ge(pe_av, t.n + 1)
                        wait(act, pe_gate, t.n)
                        wait(act, leaky_done, t.n)
                        wait(act, sig_done, t.n)
                        act.activation(av[:, :], b_av[:, :], ACT.Copy).then_inc(av_kept, 1)
                        act.wait_ge(av_kept, t.n + 1)
                        wait(act, uy_done, t.n)
                        act.activation(sig[0:CS, :], av[CS:P, :], ACT.Sigmoid)
                        act.activation(sig[CS:P, :], av[CS:P, :], ACT.Sigmoid).then_inc(sig_done, 1)
                    t = m + -2
                    if t.inside(SUPER):
                        wait(act, stored[t.slot], 16 * t.half)
                        for half, bank in ((0, b_h), (1, b_s)):
                            act.wait_ge(pe_h, 2 * t.n + half + 1)
                            act.activation(hsb[t.slot][:, 2 * half:2 * half + 2, :].rearrange("p k c -> p (k c)"),
                                           bank[:, 0:2 * C], ACT.Copy).then_inc(h_kept, 1)
                        act.wait_ge(pe_alpha, t.n + 1)
                        act.activation(g["alpha"][:, bass.ds(4 * t.n, 4), :].rearrange("p k h -> p (k h)"),
                                       b_h[:, 320:336], ACT.Copy).then_inc(alpha_kept, 1)
                    t = m + -1
                    if t.inside(SUPER):
                        act.wait_ge(pe_gate, t.n + 1)
                        wait(act, vval_done, t.n)
                        act.activation(gate[:, :], b_p1[0:V3, :], ACT.Sigmoid).then_inc(gate_done, 1)
                    t = m + 1
                    if t.inside(SUPER):
                        act.wait_ge(pe_turned, t.n + 1)
                        wait(act, multiplied, 5 * t.n)
                        act.activation(sT[:, :], b_s[:, :], ACT.Copy)
                        act.activation(vT[:, :], b_v[0:V3, :], ACT.Copy).then_inc(turned_kept, 1)
                loop(act, body, -1, SUPER + 2, SUPER)


def segment_softmax(nc, g):
    w, banks, io, alpha = g["w"], g["banks"], g["io"], g["alpha"]
    with ExitStack() as ctx:
        def sb(name, shape, dt=F32):
            return ctx.enter_context(nc.sbuf_tensor(f"sm_{name}", shape, dt))

        def sem(name):
            return ctx.enter_context(nc.semaphore(f"sm_{name}"))
        logit = sb("logit", [P, H, SCANT])
        forward = sb("forward", [P, H, SCANT])
        backward = alpha[:, :, :].rearrange("p t h -> p (t h)").rearrange("p (h t) -> p h t", h=H)
        dst = [sb(f"dst{i}", [P, SCANT], I32) for i in range(3)]
        gate = sb("gate", [P, 2, SCANT])
        whole, whole4 = sb("whole", [P, 2]), sb("whole4", [P, 2, H])
        ends = sb("ends", [P, 2, H])
        rows = sb("rows", [H, 2, 2, P])
        carry = sb("carry", [H, 2, P + 2])
        first = sb("first", [P, 2, H])
        loaded, turned, kept, chain, ended, swapped, carried, returned, shifted, exped, back, back_kept, stored = (
            sem(x) for x in ("loaded", "turned", "kept", "chain", "ended", "swapped", "carried", "returned",
                             "shifted", "exped", "back", "back_kept", "stored"))
        groups = [(h, j, min(4, SCANG - 4 * j)) for h in range(H) for j in range(-(-SCANG // 4))]
        by_group = alpha[:, :, :].rearrange("p (q g) h -> p h g q", g=SCANG)

        with nc.Block() as block:
            @block.sync
            def _(sp):
                for i in range(3):
                    sp.dma_start(dst[i][:, :], io["dst3"][i]).then_inc(loaded, 16)
                sp.wait_ge(back_kept, len(groups))
                sp.dma_start(g["ex_dram"].rearrange("s p c -> p s c"),
                             alpha[:, :, :].rearrange("p (s k) h -> p s (k h)", k=4)).then_inc(stored, 16)
                sp.wait_ge(stored, 16)

            @block.tensor
            def _(pe):
                for n, (h, j, cnt) in enumerate(groups):
                    wait(pe, kept, n - 3)
                    for i in range(cnt):
                        ins = pe.transpose(banks[n % 4][:, P * i:P * i + P], by_group[:, h, 4 * j + i, :], w("ident"))
                    ins.then_inc(turned, 1)
                for d in range(2):
                    pe.wait_ge(ended, d + 1)
                    pe.transpose(banks[4][0:H, 0:P], ends[:, d, :], w("ident"))
                    pe.transpose(banks[4][0:H, P:2 * P], whole4[:, d, :], w("ident")).then_inc(swapped, 1)
                    pe.wait_ge(carried, d + 1)
                    pe.transpose(banks[5][:, 0:H], carry[0:H, d, 2 * d:2 * d + P], w("ident")[0:H, 0:H]).then_inc(returned, 1)
                for n, (h, j, cnt) in enumerate(groups):
                    pe.wait_ge(exped, h + 1)
                    wait(pe, back_kept, n - 3)
                    for i in range(cnt):
                        at = P * (4 * j + i)
                        ins = pe.transpose(banks[n % 4][:, P * i:P * i + P], logit[:, h, at:at + P], w("ident"))
                    ins.then_inc(back, 1)

            @block.scalar
            def _(act):
                for n, (h, j, cnt) in enumerate(groups):
                    act.wait_ge(turned, n + 1)
                    act.activation(logit[:, h, 512 * j:512 * j + P * cnt], banks[n % 4][:, 0:P * cnt], ACT.Copy).then_inc(kept, 1)
                act.wait_ge(shifted, 1)
                for h in range(H):
                    act.activation(logit[:, h, :], logit[:, h, :], ACT.Exp).then_inc(exped, 1)
                for n, (h, j, cnt) in enumerate(groups):
                    act.wait_ge(back, n + 1)
                    act.activation(by_group[:, h, 4 * j:4 * j + cnt, :],
                                   banks[n % 4][:, 0:P * cnt].rearrange("p (g q) -> p g q", q=P), ACT.Copy).then_inc(back_kept, 1)

            @block.vector
            def _(dve):
                links = [0]

                def link(ins):
                    links[0] += 1
                    ins.then_inc(chain, 1)
                    dve.wait_ge(chain, links[0])

                dve.memset(carry[:, :, :], -BIG)
                dve.wait_ge(loaded, 48)
                for d in range(2):
                    ins = dve.tensor_tensor(gate[:, d, :], dst[0][:, :], dst[1 + d][:, :], ALU.is_equal)
                link(ins)
                link(dve.tensor_scalar(gate[:, :, :], gate[:, :, :], 2 * BIG, -BIG, ALU.mult, ALU.add))
                link(dve.tensor_reduce(whole[:, :], gate[:, :, :], AX, ALU.min))
                link(dve.tensor_copy(whole4[:, :, :], whole[:, :].unsqueeze(2).to_broadcast([P, 2, H])))
                dve.wait_ge(kept, len(groups))
                for d, (out, data) in enumerate(((forward, logit), (backward, forward))):
                    def flip(x):
                        return x[:, ::-1] if d else x

                    def scans(initial):
                        for h in range(H):
                            ins = dve.tensor_tensor_scan(flip(out[:, h, :]), flip(gate[:, d, :]), flip(data[:, h, :]),
                                                         initial(h), ALU.min, ALU.max)
                        return ins
                    link(scans(lambda h: -BIG))
                    dve.tensor_copy(ends[:, d, :], out[:, :, 0 if d else SCANT - 1]).then_inc(ended, 1)
                    dve.wait_ge(swapped, d + 1)
                    link(dve.tensor_copy(rows[:, d, :, :], banks[4][0:H, 0:2 * P].rearrange("p (a q) -> p a q", a=2)))
                    dve.tensor_tensor_scan(flip(carry[:, d, 1:P + 1]), flip(rows[:, d, 1, :]), flip(rows[:, d, 0, :]),
                                           -BIG, ALU.min, ALU.max).then_inc(carried, 1)
                    dve.wait_ge(returned, d + 1)
                    link(dve.tensor_copy(first[:, d, :], banks[5][:, 0:H]))
                    link(scans(lambda h: first[:, d, h:h + 1]))
                dve.tensor_tensor(logit[:, :, :], logit[:, :, :], backward, ALU.subtract).then_inc(shifted, 1)


def step_loads(sp, at, table, free, loads):
    s = sp.value_load(table[0:1, bass.ds(at.n, 1)], min_val=0, max_val=SUPER - 1)
    for sem, value in free:
        wait(sp, sem, value)
    for out, src, sem in loads:
        sp.dma_start(out, src[bass.ds(s, 1)].rearrange("a p c -> (a p) c")).then_inc(sem, 16)


def attention_aggregate(nc, g):
    w, banks, io, agg = g["w"], g["banks"], g["io"], g["agg"]
    W = C + H
    with ExitStack() as ctx:
        def sb(name, shape, dt=F32):
            return ctx.enter_context(nc.sbuf_tensor(f"ag_{name}", shape, dt))

        def sem(name):
            return ctx.enter_context(nc.semaphore(f"ag_{name}"))
        idx = [sb(f"idx{u}", [P, 8], I32) for u in range(2)]
        ex = [sb(f"ex{u}", [P, 16]) for u in range(2)]
        val = [sb(f"val{u}", [P, 4, C]) for u in range(2)]
        exval = [sb(f"exval{u}", [P, 4, W]) for u in range(2)]
        rel = [sb(f"rel{u}", [P, 4]) for u in range(2)]
        hot = [sb(f"hot{u}", [P, 4, P]) for u in range(2)]
        loaded = [sem(f"loaded{u}") for u in range(2)]
        zeroed, rel_done, ready, weighted, summed, added = (sem(x) for x in (
            "zeroed", "rel_done", "ready", "weighted", "summed", "added"))
        with nc.Block() as block:
            @block.sync
            def _(sp):
                def body(t):
                    step_loads(sp, t, g["step_s"], ((weighted, t.n - 1),), ((idx[t.slot][:, :], io["eidx"], loaded[t.slot]),
                                                    (ex[t.slot][:, :], g["ex_dram"], loaded[t.slot]),
                                                    (val[t.slot][:, :, :].rearrange("p k c -> p (k c)"), g["h_dram"], loaded[t.slot])))
                loop(sp, body, 0, STEPS, STEPS)

            @block.vector
            def _(dve):
                dve.memset(agg[:, :, :], 0.0).then_inc(zeroed, 1)
                dve.wait_ge(zeroed, 1)

                def body(m):
                    t = m
                    if t.inside(STEPS):
                        dve.wait_ge(loaded[t.slot], 48 * (t.half + 1))
                        wait(dve, summed, t.n - 1)
                        wait(dve, ready, t.n - 1)
                        dve.tensor_scalar(rel[t.slot][:, :], idx[t.slot][:, 4:8], g["block128"][:, bass.ds(t.n, 1)], None,
                                          ALU.subtract).then_inc(rel_done, 1)
                        dve.tensor_tensor(exval[t.slot][:, :, 0:C].rearrange("p k (h c) -> p k h c", h=H),
                                          val[t.slot][:, :, :].rearrange("p k (h c) -> p k h c", h=H),
                                          ex[t.slot][:, :].rearrange("p (k h) -> p k h", k=4).unsqueeze(3).to_broadcast([P, 4, H, HEAD]),
                                          ALU.mult)
                        dve.tensor_copy(exval[t.slot][:, :, C:W], ex[t.slot][:, :].rearrange("p (k h) -> p k h", k=4))\
                            .then_inc(weighted, 1)
                        dve.wait_ge(rel_done, t.n + 1)
                        for k in range(4):
                            ins = dve.tensor_scalar(hot[t.slot][:, k, :], w("iota"), rel[t.slot][:, k:k + 1], None, ALU.is_equal)
                        ins.then_inc(ready, 1)
                    t = m + -1
                    if t.inside(STEPS):
                        b = dve.value_load(g["step_b"][0:1, bass.ds(t.n, 1)], min_val=0, max_val=BLOCKS - 1)
                        there = agg[:, bass.ds(b, 1), :].rearrange("p a c -> p (a c)")
                        dve.wait_ge(summed, t.n + 1)
                        wait(dve, added, t.n)
                        dve.tensor_tensor(there, there, banks[t.slot][:, 0:W], ALU.add).then_inc(added, 1)
                loop(dve, body, 0, STEPS + 1, STEPS)

            @block.tensor
            def _(pe):
                def body(t):
                    pe.wait_ge(ready, t.n + 1)
                    wait(pe, added, t.n - 1)
                    for k in range(4):
                        ins = pe.matmul(banks[t.slot][:, 0:W], hot[t.slot][:, k, :], exval[t.slot][:, k, :],
                                        start=(k == 0), stop=(k == 3))
                    ins.then_inc(summed, 1)
                loop(pe, body, 0, STEPS, STEPS)


def node_update(nc, g, tag, columns, pick, chunks, base, factor):
    w, banks = g["w"], g["banks"]
    with ExitStack() as ctx:
        row = ctx.enter_context(nc.sbuf_tensor(f"{tag}_row", [P, columns], F32))
        feat = ctx.enter_context(nc.sbuf_tensor(f"{tag}_feat", [P, len(chunks), P], F32))
        picked, turned, kept, mapped, added = (ctx.enter_context(nc.semaphore(f"{tag}_{x}")) for x in (
            "picked", "turned", "kept", "mapped", "added"))
        tall = max(cols for _, cols, *_ in chunks)
        with nc.Block() as block:
            @block.vector
            def _(dve):
                def body(at):
                    b = at.n
                    wait(dve, turned, b)
                    pick(dve, row, b).then_inc(picked, 1)
                    there = base[:, bass.ds(b, 1), :].rearrange("p a c -> p (a c)")
                    dve.wait_ge(mapped, b + 1)
                    dve.scalar_tensor_tensor(there, there, factor, banks[1][:, 0:C], ALU.mult, ALU.add).then_inc(added, 1)
                blocks(dve, body)

            @block.tensor
            def _(pe):
                def body(at):
                    b = at.n
                    pe.wait_ge(picked, b + 1)
                    wait(pe, kept, b)
                    for i, (at, cols, _, _, _) in enumerate(chunks):
                        ins = pe.transpose(banks[0][0:cols, P * i:P * i + P], row[:, at:at + cols], w("ident"))
                    ins.then_inc(turned, 1)
                    pe.wait_ge(kept, b + 1)
                    wait(pe, added, b)
                    wrote = set()
                    for i, (_, cols, weights, lo, width) in enumerate(chunks):
                        ins = pe.matmul(banks[1][:, lo:lo + width], feat[0:cols, i, :], w(weights),
                                        start=(lo not in wrote), stop=(i == len(chunks) - 1 or width != C))
                        wrote.add(lo)
                    ins.then_inc(mapped, 1)
                blocks(pe, body)

            @block.scalar
            def _(act):
                def body(at):
                    b = at.n
                    act.wait_ge(turned, b + 1)
                    wait(act, mapped, b)
                    act.activation(feat[0:tall, :, :].rearrange("p i q -> p (i q)"), banks[0][0:tall, 0:P * len(chunks)],
                                   ACT.Copy).then_inc(kept, 1)
                blocks(act, body)


def attention_output(nc, g):
    agg, nodes = g["agg"], g["nodes"]
    with ExitStack() as ctx:
        den = ctx.enter_context(nc.sbuf_tensor("den", [P, BLOCKS, H], F32))
        rden = ctx.enter_context(nc.sbuf_tensor("rden", [P, BLOCKS, H], F32))
        chain = ctx.enter_context(nc.semaphore("den_chain"))
        with nc.Block() as block:
            @block.vector
            def _(dve):
                dve.tensor_scalar(den[:, :, :], agg[:, :, C:C + H], 1e-16, None, ALU.add).then_inc(chain, 1)
                dve.wait_ge(chain, 1)
                dve.reciprocal(rden[:, :, :], den[:, :, :]).then_inc(chain, 1)
                dve.wait_ge(chain, 2)
                heads = agg[:, :, 0:C].rearrange("p b (h c) -> p b h c", h=H)
                dve.tensor_tensor(heads, heads, rden[:, :, :].unsqueeze(3).to_broadcast([P, BLOCKS, H, HEAD]),
                                  ALU.mult).then_inc(chain, 1)

    def pick(dve, row, b):
        return dve.tensor_copy(row[:, :], agg[:, bass.ds(b, 1), 0:C].rearrange("p a c -> p (a c)"))
    node_update(nc, g, "upd0", C, pick, [(0, 80, "wp0", 0, C), (80, 80, "wp1", 0, C)], nodes, 2.0)
    normalise(nc, g, "ln1", [(nodes, 0, C, C, True)], nodes)
    node_tables(nc, g, "tab1", nodes, "ts1", "tv1", None, [g["tab_conv"]], nodes)


def conv_edges(nc, g):
    w, psum, io, agg = g["w"], g["psum"], g["io"], g["agg"]
    WW = 256
    with ExitStack() as ctx:
        def sb(name, shape, dt=F32):
            return ctx.enter_context(nc.sbuf_tensor(f"ce_{name}", shape, dt))

        def sem(name):
            return ctx.enter_context(nc.semaphore(f"ce_{name}"))
        idx = [sb(f"idx{u}", [P, 8], I32) for u in range(4)]
        y = [sb(f"y{u}", [P, 16]) for u in range(4)]
        query = [sb(f"query{u}", [P, 512]) for u in range(4)]
        node = [sb(f"node{u}", [P, 4, C5]) for u in range(2)]
        rel = [sb(f"rel{u}", [P, 4]) for u in range(2)]
        prod = [sb(f"prod{u}", [P, 4, 4 * C]) for u in range(2)]
        plain = [sb(f"plain{u}", [P, 4, P]) for u in range(2)]
        hot = [sb(f"hot{j}", [P, 4, P]) for j in range(4)]
        idx_in, loaded = ([sem(f"{x}{u}") for u in range(4)] for x in ("idx_in", "loaded"))
        gathered = [sem(f"gathered{u}") for u in range(2)]
        may_gather, zeroed, rel_done, plain_done, hot_done, prod_done, weights, summed, added = (sem(x) for x in (
            "may_gather", "zeroed", "rel_done", "plain_done", "hot_done", "prod_done", "weights", "summed", "added"))
        b_w = [psum[:, 2 * u:2 * u + 2, :].rearrange("p b (k c) -> p (b k) c", k=2) for u in range(2)]
        b_0 = [psum[:, 4 + 2 * u, 0:C] for u in range(2)]
        b_y = [psum[:, 5 + 2 * u, 0:3 * C].rearrange("p (x c) -> p x c", x=3) for u in range(2)]
        with nc.Block() as block:
            @block.sync
            def _(sp):
                def body(t):
                    step_loads(sp, t, g["step_s"], ((summed, 4 * t.n - 12),),
                               ((idx[t.slot4][:, :], io["eidx"], idx_in[t.slot4]), (y[t.slot4][:, :], io["ey"], loaded[t.slot4]),
                                (query[t.slot4][0:CS, :], io["query"], loaded[t.slot4])))
                loop(sp, body, 0, STEPS, STEPS)

            @block.gpsimd
            def _(pool):
                def body(t):
                    pool.wait_ge(idx_in[t.slot4], 16 * (t.quarter + 1))
                    wait(pool, prod_done, t.n - 1)
                    pool.sem_inc(may_gather, 1)
                    for k in range(4):
                        pool.indirect_dma_start(node[t.slot][:, k, :], None, g["tab_conv"],
                                                bass.IndirectOffsetOnAxis(ap=idx[t.slot4][:, k:k + 1], axis=0))\
                            .then_inc(gathered[t.slot], 16)
                loop(pool, body, 0, STEPS, STEPS)

            @block.vector
            def _(dve):
                dve.memset(agg[:, :, :], 0.0)
                for u in range(4):
                    ins = dve.memset(query[u][CS:P, :], 0.0)
                ins.then_inc(zeroed, 1)
                dve.wait_ge(zeroed, 1)

                def body(m):
                    t = m + 1
                    if t.inside(STEPS):
                        dve.wait_ge(idx_in[t.slot4], 16 * (t.quarter + 1))
                        wait(dve, plain_done, t.n - 1)
                        dve.tensor_scalar(rel[t.slot][:, :], idx[t.slot4][:, 4:8], g["block128"][:, bass.ds(t.n, 1)], None,
                                          ALU.subtract).then_inc(rel_done, 1)
                        dve.wait_ge(rel_done, t.n + 1)
                        wait(dve, hot_done, 4 * t.n - 4)
                        dve.tensor_tensor(plain[t.slot][:, :, :], w("iota").unsqueeze(1).to_broadcast([P, 4, P]),
                                          rel[t.slot][:, :].unsqueeze(2).to_broadcast([P, 4, P]), ALU.is_equal)\
                            .then_inc(plain_done, 1)
                    t = m
                    if t.inside(STEPS):
                        dve.wait_ge(gathered[t.slot], 64 * (t.half + 1))
                        dve.wait_ge(weights, t.n + 1)
                        wait(dve, summed, 4 * t.n - 4)
                        bank, here, there = b_w[t.slot], node[t.slot], prod[t.slot]
                        scalars, vectors = here[:, :, 0:CS], here[:, :, CS:C].rearrange("p k (x c) -> p k x c", x=3)
                        dve.tensor_tensor(there[:, :, 0:CS], bank[:, :, 0:CS], scalars, ALU.mult)
                        dve.tensor_tensor(there[:, :, CS:C].rearrange("p k (x c) -> p k x c", x=3), vectors,
                                          bank[:, :, 128:160].unsqueeze(2).to_broadcast([P, 4, 3, CV]), ALU.mult)
                        dve.tensor_tensor(there[:, :, C:4 * C].rearrange("p k (x c) -> p k x c", x=3)[:, :, :, 0:CS],
                                          bank[:, :, CS:128].unsqueeze(2).to_broadcast([P, 4, 3, CS]),
                                          scalars.unsqueeze(2).to_broadcast([P, 4, 3, CS]), ALU.mult)
                        for x in range(3):
                            ins = dve.tensor_tensor(there[:, :, C * x + C + CS:C * x + 2 * C], bank[:, :, 160:WW],
                                                    here[:, :, CS + CV * x:CS + CV * x + V3], ALU.mult)
                        ins.then_inc(prod_done, 1)
                    t = m + -1
                    if t.inside(STEPS):
                        b = dve.value_load(g["step_b"][0:1, bass.ds(t.n, 1)], min_val=0, max_val=BLOCKS - 1)
                        there = agg[:, bass.ds(b, 1), :].rearrange("p a c -> p (a c)")
                        dve.wait_ge(summed, 4 * t.n + 4)
                        wait(dve, added, 3 * t.n)
                        dve.tensor_tensor(there[:, 0:C], there[:, 0:C], b_0[t.slot], ALU.add).then_inc(added, 1)
                        a13 = there[:, C5:512].rearrange("p (x c) -> p x c", x=3)
                        dve.tensor_tensor(a13, a13, b_y[t.slot][:, :, 0:96], ALU.add)
                        dve.wait_ge(added, 3 * t.n + 1)
                        plus = there[:, 96:192].rearrange("p (x c) -> p x c", x=3)
                        dve.tensor_tensor(plus, plus, b_y[t.slot][:, :, 128:C], ALU.add).then_inc(added, 1)
                        dve.wait_ge(added, 3 * t.n + 2)
                        minus = there[:, 128:224].rearrange("p (x c) -> p x c", x=3)
                        dve.tensor_tensor(minus, minus, b_y[t.slot][:, :, 96:128], ALU.subtract).then_inc(added, 1)
                loop(dve, body, -1, STEPS + 1, STEPS)

            @block.scalar
            def _(act):
                def body(t):
                    act.wait_ge(plain_done, t.n + 1)
                    act.wait_ge(loaded[t.slot4], 32 * (t.quarter + 1))
                    for j in range(4):
                        wait(act, summed, 4 * t.n - 3 + j)
                        for k in range(4):
                            ins = act.activation(hot[j][:, k, :], plain[t.slot][:, k, :], ACT.Identity,
                                                 scale=y[t.slot4][:, 4 * k + j:4 * k + j + 1])
                        ins.then_inc(hot_done, 1)
                loop(act, body, 0, STEPS, STEPS)

            @block.tensor
            def _(pe):
                pe.wait_ge(zeroed, 1)

                def body(m):
                    t = m + 1
                    if t.inside(STEPS):
                        pe.wait_ge(loaded[t.slot4], 32 * (t.quarter + 1))
                        wait(pe, prod_done, t.n - 1)
                        for k in range(4):
                            ins = pe.matmul(b_w[t.slot][:, k, :], query[t.slot4][:, P * k:P * k + P], w("tp"),
                                            start=True, stop=True)
                        ins.then_inc(weights, 1)
                    t = m
                    if t.inside(STEPS):
                        pe.wait_ge(prod_done, t.n + 1)
                        wait(pe, added, 3 * t.n - 3)
                        for j in range(4):
                            pe.wait_ge(hot_done, 4 * t.n + j + 1)
                            for k in range(4):
                                ins = pe.matmul(b_y[t.slot][:, j - 1, :] if j else b_0[t.slot], hot[j][:, k, :],
                                                prod[t.slot][:, k, C * j:C * j + C], start=(k == 0), stop=(k == 3),
                                                skip_group_check=True)
                            ins.then_inc(summed, 1)
                loop(pe, body, -1, STEPS, STEPS)


def conv_output(nc, g):
    nodes, agg = g["nodes"], g["agg"]
    with nc.semaphore("folded") as folded:
        with nc.Block() as block:
            @block.vector
            def _(dve):
                dve.tensor_tensor(agg[:, :, 64:128], agg[:, :, 64:128], agg[:, :, 160:224], ALU.add)
                dve.tensor_tensor(agg[:, :, 288:320], agg[:, :, 288:320], agg[:, :, 384:416], ALU.add).then_inc(folded, 1)
                dve.wait_ge(folded, 1)
                dve.tensor_tensor(agg[:, :, 288:320], agg[:, :, 288:320], agg[:, :, 480:512], ALU.add).then_inc(folded, 1)
                dve.wait_ge(folded, 2)

    def pick(dve, row, b):
        there = agg[:, bass.ds(b, 1), :].rearrange("p a c -> p (a c)")
        vectors = row[:, 96:384].rearrange("p (x c) -> p x c", x=3)
        dve.tensor_copy(row[:, 0:CS], there[:, 0:CS])
        dve.tensor_copy(row[:, CS:96], there[:, 288:320])
        dve.tensor_copy(vectors[:, :, 0:CS], there[:, C5:512].rearrange("p (x c) -> p x c", x=3)[:, :, 0:CS])
        return dve.tensor_copy(vectors[:, :, CS:96], there[:, CS:C].rearrange("p (x c) -> p x c", x=3))
    node_update(nc, g, "upd1", 384, pick, [(0, 96, "l2s", 0, CS)] + [(96 + 96 * x, 96, "l2v", CS + CV * x, CV) for x in range(3)],
                nodes, 1.0)
    normalise(nc, g, "ln2", [(nodes, 0, C, C, True)], nodes)
    with nc.semaphore("out_stored") as stored:
        with nc.Block() as block:
            @block.sync
            def _(sp):
                sp.dma_start(g["io"]["out"], nodes[:, :, :]).then_inc(stored, 16)
                sp.wait_ge(stored, 16)


def component_major(a):
    return np.concatenate([a[..., :CS], a[..., CS:].reshape(*a.shape[:-1], CV, 3).swapaxes(-1, -2).reshape(*a.shape[:-1], V3)], -1)


def lay_pack(i):
    W = {name: np.zeros((rows, cols), np.float32) for name, rows, cols in PACK}
    L0 = {k[7:]: np.asarray(v) for k, v in i.items() if k.startswith("L0_gnn_")}
    L1 = {k[7:]: np.asarray(v) for k, v in i.items() if k.startswith("L1_gnn_")}
    W["ident"][:] = np.eye(P)
    W["ones"][:] = 1
    W["iota"][:] = np.arange(P)
    W["count"][:] = np.arange(STEPS)
    W["sidx"][:] = np.arange(4 * P).reshape(4, P).T
    W["ts0"][:, :CS], W["ts0"][:, CS:] = L0["Ws_src"], L0["Ws_dst"]
    W["ts1"][:, :CS], W["ts1"][:, CS:] = L1["lin1_w0"], L1["si_w0"]
    rbf = L0["W_rbf"]
    ss, sv, vs, vv0, vv1 = rbf[:, :64], rbf[:, 64:128], rbf[:, 128:160], rbf[:, 160:192], rbf[:, 192:224]
    W["wy0"][0:16, 0:64], W["wy0"][64:80, 64:128] = ss, sv
    for name in ("gamma_s", "beta_s"):
        W[name][:, 0] = L0[name]
    W["m1a"][0:64, 0:64], W["m1a"][0:64, 64:128] = L0["W_alpha"][0:64], L0["Ws_val"][0:64]
    for h in range(H):
        W["adot"][AS * h:AS * h + AS, h] = L0["alpha_dot"][0, h]
    Wsv = L0["Ws_vlin"].reshape(CS + CV, H, AS)
    Wvv = L0["Wv_vlin"].reshape(CS + 2 * CV, H, AV)
    mu1, mu2, mv1 = (W[n].reshape(-1, H, c) for n, c in (("mu1", 24), ("mu2", 16), ("mv1", 16)))
    mv = {n: W[n].reshape(V3, H, 3, AV) for n in ("mv0", "mv2", "mv3")}
    mu1[0:64, :, 0:16], mu1[64:128, :, 16:24] = Wsv[0:64], Wvv[0:64]
    mu2[0:64, :, 0:8], mu2[64:128, :, 8:16] = Wvv[0:64], Wvv[0:64]
    W["r_mu1"][0:64, 0], W["r_mu1"][64:128, 0] = L0["w2_ss"], L0["w2_sv"]
    W["r_mu2"][0:64, 0], W["r_mu2"][64:128, 0] = L0["w2_sv"], L0["w2_sv"]
    for x in range(3):
        r, up, down = slice(CV * x, CV * x + CV), (x + 1) % 3, (x + 2) % 3
        W["tv0"][r, CV * x:CV * x + CV], W["tv0"][r, V3 + CV * x:V3 + CV * x + CV] = L0["Wv_src"], L0["Wv_dst"]
        for at in (x, x + 3)[:2 if x < 2 else 1]:
            W["tv1"][r, CV * at:CV * at + CV] = L1["lin1_w1"]
        W["tv1"][r, 5 * CV + CV * x:5 * CV + CV * x + CV] = L1["si_w1"]
        W["gamma_v"][r, 0] = L0["gamma_v"]
        W["wy1"][16 + 16 * x:32 + 16 * x, r] = vv0
        W["wy2"][0:16, r] = vs
        W["wy3"][16 + 16 * up:32 + 16 * up, r] = vv1
        W["wy4"][16 + 16 * down:32 + 16 * down, r] = vv1
        W["m1b"][r, 0:64], W["m1b"][r, 64:128] = L0["W_alpha"][64:96], L0["Ws_val"][64:96]
        W["p1"][64:128, r] = L0["Wv_val"][0:64]
        W["vb"][r, r] = L0["Wv_val"][64:96]
        W["vc1"][r, CV * down:CV * down + CV] = L0["Wv_val"][96:128]
        W["vc2"][r, CV * up:CV * up + CV] = L0["Wv_val"][96:128]
        W["wg"][64:128, r] = L0["Wg"]
        mv1[r] = Wsv[64:96]
        mv["mv0"][r, :, x] = Wvv[64:96]
        mv["mv2"][r, :, down] = Wvv[96:128]
        mv["mv3"][r, :, up] = Wvv[96:128]
        for n, s in (("r_vs", "w2_vs"), ("r_vv0", "w2_vv0"), ("r_vv1", "w2_vv1")):
            W[n][r, 0] = L0[s]
    for h in range(H):
        part, at = W[f"wp{h // 2}"], HEAD * (h % 2)
        part[at:at + AS, 0:CS] = L0["Wps"][AS * h:AS * h + AS]
        for x in range(3):
            part[at + AS + AV * x:at + AS + AV * x + AV, CS + CV * x:CS + CV * x + CV] = L0["Wpv"][AV * h:AV * h + AV]
    tp = L1["tp_weight"]
    W["tp"][0:64] = np.concatenate([tp[:, 0:160], tp[:, 192:224], tp[:, 160:192], tp[:, 160:192]], 1)
    W["l2s"][:], W["l2v"][:] = L1["lin2_w0"], L1["lin2_w1"]
    out = np.zeros((P, PACKW), np.float32)
    for name, (rows, at, cols) in PLACE.items():
        out[0:rows, at:at + cols] = W[name].reshape(rows, cols)
    return out


def lay_inputs(i):
    E = SUPER * 512
    x = component_major(np.asarray(i["x"]))
    x = np.pad(x, ((0, BLOCKS * P - NODES), (0, 0))).reshape(BLOCKS, P, C).transpose(1, 0, 2)
    src = np.pad(np.asarray(i["src"]), (0, E - EDGES))
    dst_all = np.pad(np.asarray(i["dst"]), (0, SCANT * P - EDGES), constant_values=NODES)
    dst = dst_all[:E]
    both = np.stack([src.reshape(SUPER, 4, P), dst.reshape(SUPER, 4, P)], 1)
    eidx = both.transpose(0, 3, 1, 2).reshape(SUPER, P, 8)
    far = np.array([FAR], dst.dtype)
    sdst = np.concatenate([far, dst[512::512], np.repeat(far, 512 - SUPER)]).reshape(4, P).T
    no = np.array([-1], dst.dtype)
    dst3 = np.stack([dst_all, np.concatenate([no, dst_all[:-1]]), np.concatenate([dst_all[1:], no])]).reshape(3, P, SCANT)
    y = np.pad(np.asarray(i["edge_attr_4"]), ((0, E - EDGES), (0, 0))).reshape(SUPER, 512, 4)
    ey = y.reshape(SUPER, 4, P, 4).transpose(0, 2, 1, 3).reshape(SUPER, P, 16)
    yt = y.transpose(0, 2, 1)
    rbf = np.pad(np.asarray(i["edge_attr_16"]), ((0, E - EDGES), (0, 0))).reshape(SUPER, 512, 16).transpose(0, 2, 1)
    query = np.pad(np.asarray(i["edge_attr_64"]), ((0, E - EDGES), (0, 0))).reshape(SUPER, 512, 64).transpose(0, 2, 1)
    return dict(
        pack=lay_pack(i), x=x, eidx=eidx, sdst=sdst, dst3=dst3, ey=ey,
        rbf5=np.tile(rbf, (1, 5, 1)), y16=np.repeat(yt, 16, axis=1),
        ys=yt[:, [0, 2, 1, 3]].reshape(SUPER, 2, 1024),
        yv=yt[:, [1, 2, 3, 0, 2, 3, 1, 0, 3, 1, 2, 0]].reshape(SUPER, 3, 2048),
        query=query)


def kernel(**inputs):
    import numpy as _np
    import concourse.bacc as _bacc
    from concourse import mybir as _mybir
    from concourse.bass_utils import run_bass_kernel_spmd as _run

    nc = _bacc.Bacc("TRN2", target_bir_lowering=False, num_devices=1)
    arrays, io = {}, {}
    for name, a in lay_inputs(inputs).items():
        a = _np.ascontiguousarray(a)
        arrays[f"in_{name}"] = a
        io[name] = nc.dram_tensor(f"in_{name}", a.shape, _mybir.dt.from_np(a.dtype), kind="ExternalInput").ap()
    io["out"] = nc.dram_tensor("out_nodes", (P, BLOCKS, C), F32, kind="ExternalOutput").ap()
    gnn(nc, io)
    r = _run(nc, [arrays], core_ids=[0])
    got = r.results[0]["out_nodes"]
    got = got.transpose(1, 0, 2).reshape(BLOCKS * P, C)[:NODES]
    return _np.concatenate([got[:, :CS], got[:, CS:].reshape(NODES, 3, CV).swapaxes(1, 2).reshape(NODES, V3)], 1)
```

```python
from contextlib import ExitStack

import concourse.bass as bass
from concourse import mybir
import numpy as np

ALU = mybir.AluOpType
ACT = mybir.ActivationFunctionType
AX = mybir.AxisListType.X
F32 = mybir.dt.float32
I32 = mybir.dt.int32

P = 128
NODES = 6250
EDGES = 206250
CS, CV, H, AS, AV, NB = 64, 32, 4, 16, 8, 16
V3 = 3 * CV
C = CS + V3
C5 = CS + 5 * CV
BLOCKS = -(-NODES // P)
SUPER = -(-EDGES // 512) + (-(-EDGES // 512)) % 2
STEPS = SUPER + BLOCKS - 1
SCANG = -(-SUPER * 4 // P)
SCANT = SCANG * P
VH = 3 * AV
BIG = 1.5e38
FAR = 1 << 20
EPS = 1e-5
STEPS += STEPS % 2

PACK = [
    ("ident", 128, 128), ("ones", 128, 128), ("iota", 128, 128), ("count", 128, STEPS), ("sidx", 128, 4),
    ("ts0", 64, 128), ("tv0", 96, 192), ("gamma_s", 64, 1), ("beta_s", 64, 1), ("gamma_v", 96, 1),
    ("wy", 80, 352), ("m1_0", 128, 192), ("m1_1", 128, 288), ("m1_2", 96, 96), ("val_0", 64, 128), ("val_1", 64, 128),
    ("wg", 64, 32), ("adot", 128, 64), ("m2_0", 128, 96), ("m2_1", 128, 192), ("m2_2", 96, 96),
    ("r2_0", 128, 1), ("r2_1", 128, 1), ("r2_2", 96, 1), ("wps", 64, 64), ("wpv", 96, 96),
    ("ts1", 64, 128), ("tv1", 96, 256), ("tp", 128, 224),
    ("l2s", 96, 64), ("l2v", 96, 32),
]
PLACE, PACKW = {}, 0
for _name, _rows, _cols in PACK:
    PLACE[_name] = (_rows, PACKW, _cols)
    PACKW += _cols


class At:

    def __init__(self, n, quarter, slot4):
        self.n, self.quarter, self.slot4 = n, quarter, slot4
        self.half, self.slot = 2 * quarter + slot4 // 2, slot4 % 2

    def __add__(self, d):
        return At(self.n + d, self.quarter + (self.slot4 + d) // 4, (self.slot4 + d) % 4)

    def inside(self, count):
        return not isinstance(self.n, int) or 0 <= self.n < count


def loop(eng, body, first, last, count):
    lo = 4
    hi = (count - 4) // 4 * 4
    for m in range(first, lo):
        body(At(m, m // 4, m % 4))
    with eng.Fori(lo // 4, hi // 4) as i:
        for u in range(4):
            body(At(4 * i + u, i, u))
    for m in range(hi, last):
        body(At(m, m // 4, m % 4))


def wait(eng, sem, value):
    if not isinstance(value, int) or value > 0:
        eng.wait_ge(sem, value)


def gnn(nc, io):
    tab_src = nc.dram_tensor("tab_src", [BLOCKS * P, C], F32).ap()
    tab_dst = nc.dram_tensor("tab_dst", [BLOCKS * P, C], F32).ap()
    tab_conv = nc.dram_tensor("tab_conv", [BLOCKS * P, C5], F32).ap()
    h_dram = nc.dram_tensor("h_dram", [SUPER, P, 4 * C], F32).ap()

    with ExitStack() as top:
        pack = top.enter_context(nc.sbuf_tensor("pack_sb", [P, PACKW], F32))
        nodes = top.enter_context(nc.sbuf_tensor("nodes", [P, BLOCKS, C], F32))
        block128 = top.enter_context(nc.sbuf_tensor("block128", [P, STEPS], F32))
        step_s = top.enter_context(nc.sbuf_tensor("step_s", [P, STEPS], I32))
        step_b = top.enter_context(nc.sbuf_tensor("step_b", [P, STEPS], I32))
        psum = top.enter_context(nc.psum_tensor("psum", [P, 8, 512], F32))
        banks = [psum[:, i, :] for i in range(8)]
        g = dict(psum=psum, pack=pack, nodes=nodes, block128=block128, step_s=step_s, step_b=step_b, banks=banks,
                 tab_src=tab_src, tab_dst=tab_dst, tab_conv=tab_conv, h_dram=h_dram, io=io)

        def w(name):
            rows, at, cols = PLACE[name]
            return pack[0:rows, at:at + cols]
        g["w"] = w

        constants(nc, g)
        attention_input(nc, g)
        with ExitStack() as mid:
            g["alpha"] = mid.enter_context(nc.sbuf_tensor("alpha", [P, SCANT, H], F32))
            attention_edges(nc, g)
            segment_softmax(nc, g)
            g["agg"] = mid.enter_context(nc.sbuf_tensor("agg0", [P, BLOCKS, C + H], F32))
            attention_aggregate(nc, g)
            attention_output(nc, g)
        with ExitStack() as mid:
            g["agg"] = mid.enter_context(nc.sbuf_tensor("agg1", [P, BLOCKS, 512], F32))
            conv_edges(nc, g)
            conv_output(nc, g)


def constants(nc, g):
    w, io, pack = g["w"], g["io"], g["pack"]
    scaled = [("m1_1", 0, 96, None, 2 ** -0.5), ("m1_1", 96, P, None, 3 ** -0.5), ("m2_0", 0, P, "r2_0", 1.0),
              ("m2_1", 0, 96, "r2_1", 2 ** -0.5), ("m2_1", 96, P, "r2_1", 3 ** -0.5), ("m2_2", 0, 96, "r2_2", 1.0),
              ("ts1", 0, CS, None, CS ** -0.5), ("tv1", 0, V3, None, CV ** -0.5),
              ("l2s", 0, 96, None, (CS + CV) ** -0.5 / 10.0), ("l2v", 0, 96, None, (CS + CV) ** -0.5 / 10.0)]
    with ExitStack() as ctx:
        sdst = ctx.enter_context(nc.sbuf_tensor("sdst", [P, 4], I32))
        sblk = ctx.enter_context(nc.sbuf_tensor("sblk", [P, 4], I32))
        start = ctx.enter_context(nc.sbuf_tensor("start", [P, 4], F32))
        start2 = ctx.enter_context(nc.sbuf_tensor("start2", [P, 4], F32))
        begun = ctx.enter_context(nc.sbuf_tensor("begun", [P, 4, STEPS], F32))
        s_f = ctx.enter_context(nc.sbuf_tensor("s_f", [P, STEPS], F32))
        b_f = ctx.enter_context(nc.sbuf_tensor("b_f", [P, STEPS], F32))
        loaded = ctx.enter_context(nc.semaphore("const_loaded"))
        chain = ctx.enter_context(nc.semaphore("const_chain"))
        summed = ctx.enter_context(nc.semaphore("const_summed"))
        with nc.Block() as block:
            @block.sync
            def _(sp):
                sp.dma_start(pack[:, :], io["pack"]).then_inc(loaded, 16)
                sp.dma_start(sdst[:, :], io["sdst"]).then_inc(loaded, 16)
                sp.dma_start(g["nodes"][:, :, :], io["x"]).then_inc(loaded, 16)

            @block.vector
            def _(dve):
                links = [0]

                def link(ins):
                    links[0] += 1
                    ins.then_inc(chain, 1)
                    dve.wait_ge(chain, links[0])

                dve.wait_ge(loaded, 48)
                link(dve.tensor_scalar(sblk[:, :], sdst[:, :], 7, None, ALU.logical_shift_right))
                link(dve.tensor_copy(start[:, :], sblk[:, :]))
                link(dve.tensor_tensor(start2[:, :], start[:, :], w("sidx"), ALU.add))
                for c in range(4):
                    ins = dve.tensor_scalar(begun[:, c, :], w("count"), start2[:, c:c + 1], None, ALU.is_ge)
                link(ins)
                for name, lo, hi, factor, const in scaled:
                    part = w(name)[lo:hi, :]
                    if factor:
                        ins = dve.tensor_scalar(part, part, w(factor)[lo:hi, :], const, ALU.mult, ALU.mult)
                    else:
                        ins = dve.tensor_scalar(part, part, const, None, ALU.mult)
                at = PLACE["tp"][1]
                for a, b, const in ((128, 160, 2 ** -0.5), (160, 192, 3 ** -0.5), (192, 224, 0.5)):
                    ins = dve.tensor_scalar(pack[:, at + a:at + b], pack[:, at + a:at + b], const, None, ALU.mult)
                link(ins)
                dve.wait_ge(summed, 1)
                dve.tensor_copy(w("m1_0")[:, 160:192], g["banks"][1][:, 0:32])
                dve.tensor_scalar(w("m1_1")[96:P, 160:192], g["banks"][1][96:P, 32:64], 3 ** -0.5, None, ALU.mult)
                link(dve.tensor_copy(s_f[:, :], g["banks"][0][:, 0:STEPS]))
                link(dve.tensor_tensor(b_f[:, :], w("count"), s_f[:, :], ALU.subtract))
                dve.tensor_scalar(g["block128"][:, :], b_f[:, :], float(P), None, ALU.mult)
                dve.tensor_copy(g["step_s"][:, :], s_f[:, :])
                link(dve.tensor_scalar(g["step_b"][:, :], b_f[:, :], float(BLOCKS - 1), None, ALU.min))

            @block.tensor
            def _(pe):
                pe.wait_ge(chain, 4)
                for i in range(2):
                    pe.matmul(g["banks"][1][:, 32 * i:32 * i + 32], w(f"val_{i}"), w("wg"), start=True, stop=True)
                for c in range(4):
                    ins = pe.matmul(g["banks"][0][:, 0:STEPS], w("ones"), begun[:, c, :], start=(c == 0), stop=(c == 3))
                ins.then_inc(summed, 1)


def node_tables(nc, g, tag, values, ts, tv, scales, outputs, base):
    w, banks = g["w"], g["banks"]
    with ExitStack() as ctx:
        def sb(name, shape):
            return ctx.enter_context(nc.sbuf_tensor(f"{tag}_{name}", shape, F32))

        def sem(name):
            return ctx.enter_context(nc.semaphore(f"{tag}_{name}"))
        width = outputs[0].shape[1]
        turn = width - CS
        row = [sb(f"row{u}", [P, C]) for u in range(2)]
        feat = [sb(f"feat{u}", [P, 2, P]) for u in range(2)]
        out = [sb(f"out{u}", [P, 2, width]) for u in range(2)]
        picked, turned, kept, mapped, summed, added = (sem(x) for x in ("picked", "turned", "kept", "mapped", "summed", "added"))
        stored = [sem("stored0"), sem("stored1")]
        b_t, b_s, b_v = banks[0:2], banks[2:4], banks[4:6]
        with nc.Block() as block:
            @block.vector
            def _(dve):
                def body(m):
                    t = m + 1
                    if t.inside(BLOCKS):
                        wait(dve, turned, t.n - 1)
                        if base is not None:
                            wait(dve, added, t.n - 1)
                        dve.tensor_copy(row[t.slot][:, :], values[:, bass.ds(t.n, 1), :].rearrange("p a c -> p (a c)"))\
                            .then_inc(picked, 1)
                    t = m
                    if t.inside(BLOCKS):
                        dve.wait_ge(mapped, t.n + 1)
                        wait(dve, stored[t.slot], t.half * 16 * len(outputs))
                        for o in range(len(outputs)):
                            dve.tensor_copy(out[t.slot][:, o, 0:CS], b_s[t.slot][:, o * CS:(o + 1) * CS])
                            ins = dve.tensor_copy(out[t.slot][:, o, CS:width], b_v[t.slot][:, o * turn:(o + 1) * turn])
                        ins.then_inc(summed, 1)
                        if base is not None:
                            there = base[:, bass.ds(t.n, 1), :].rearrange("p a c -> p (a c)")
                            dve.tensor_tensor(there[:, 0:CS], row[t.slot][:, 0:CS], b_s[t.slot][:, CS:2 * CS], ALU.add)
                            dve.tensor_tensor(there[:, CS:C], row[t.slot][:, CS:C], b_v[t.slot][:, turn:turn + V3], ALU.add)\
                                .then_inc(added, 1)
                loop(dve, body, -1, BLOCKS, BLOCKS)

            @block.tensor
            def _(pe):
                def body(m):
                    t = m + 1
                    if t.inside(BLOCKS):
                        pe.wait_ge(picked, t.n + 1)
                        wait(pe, kept, t.n - 1)
                        pe.transpose(b_t[t.slot][0:V3, P:2 * P], row[t.slot][:, CS:C], w("ident"))
                        pe.transpose(b_t[t.slot][0:CS, 0:P], row[t.slot][:, 0:CS], w("ident")).then_inc(turned, 1)
                    t = m
                    if t.inside(BLOCKS):
                        pe.wait_ge(kept, t.n + 1)
                        wait(pe, summed if base is None else added, t.n - 1)
                        pe.matmul(b_s[t.slot][:, 0:2 * CS], feat[t.slot][0:CS, 0, :], w(ts), start=True, stop=True)
                        pe.matmul(b_v[t.slot][:, 0:turn + V3], feat[t.slot][0:V3, 1, :], w(tv), start=True, stop=True)\
                            .then_inc(mapped, 1)
                loop(pe, body, -1, BLOCKS, BLOCKS)

            @block.scalar
            def _(act):
                def body(t):
                    act.wait_ge(turned, t.n + 1)
                    wait(act, mapped, t.n - 1)
                    if scales:
                        act.activation(feat[t.slot][0:CS, 0, :], b_t[t.slot][0:CS, 0:P], ACT.Identity,
                                       bias=w(scales[1]), scale=w(scales[0]))
                        act.activation(feat[t.slot][0:V3, 1, :], b_t[t.slot][0:V3, P:2 * P], ACT.Identity,
                                       scale=w(scales[2])).then_inc(kept, 1)
                    else:
                        act.activation(feat[t.slot][0:CS, 0, :], b_t[t.slot][0:CS, 0:P], ACT.Copy)
                        act.activation(feat[t.slot][0:V3, 1, :], b_t[t.slot][0:V3, P:2 * P], ACT.Copy).then_inc(kept, 1)
                loop(act, body, 0, BLOCKS, BLOCKS)

            @block.sync
            def _(sp):
                def body(t):
                    sp.wait_ge(summed, t.n + 1)
                    for o, table in enumerate(outputs):
                        sp.dma_start(table.rearrange("(b p) c -> b p c", p=P)[bass.ds(t.n, 1), :, :].rearrange("a p c -> (a p) c"),
                                     out[t.slot][:, o, :]).then_inc(stored[t.slot], 16)
                loop(sp, body, 0, BLOCKS, BLOCKS)
                sp.wait_ge(stored[0], 16 * len(outputs) * ((BLOCKS + 1) // 2))
                sp.wait_ge(stored[1], 16 * len(outputs) * (BLOCKS // 2))


def normalise(nc, g, tag, groups, out):
    with ExitStack() as ctx:
        square = ctx.enter_context(nc.sbuf_tensor(f"{tag}_square", [P, BLOCKS, C], F32))
        mean = ctx.enter_context(nc.sbuf_tensor(f"{tag}_mean", [P, BLOCKS], F32))
        mean1 = ctx.enter_context(nc.sbuf_tensor(f"{tag}_mean1", [P, BLOCKS], F32))
        var = ctx.enter_context(nc.sbuf_tensor(f"{tag}_var", [P, BLOCKS], F32))
        var1 = ctx.enter_context(nc.sbuf_tensor(f"{tag}_var1", [P, BLOCKS], F32))
        dev = ctx.enter_context(nc.sbuf_tensor(f"{tag}_dev", [P, BLOCKS], F32))
        inv = ctx.enter_context(nc.sbuf_tensor(f"{tag}_inv", [P, BLOCKS], F32))
        chain = ctx.enter_context(nc.semaphore(f"{tag}_chain"))
        rooted = ctx.enter_context(nc.semaphore(f"{tag}_rooted"))
        varied = ctx.enter_context(nc.semaphore(f"{tag}_varied"))
        with nc.Block() as block:
            @block.vector
            def _(dve):
                links = [0]

                def link(ins):
                    links[0] += 1
                    ins.then_inc(chain, 1)
                    dve.wait_ge(chain, links[0])

                for n, (src, lo, hi, divisor, centre) in enumerate(groups):
                    width = hi - lo
                    spread = [P, BLOCKS, width]
                    if centre:
                        link(dve.tensor_reduce(mean[:, :], src[:, :, lo:hi], AX, ALU.add))
                        link(dve.tensor_scalar(mean1[:, :], mean[:, :], 1.0 / width, None, ALU.mult))
                        link(dve.tensor_tensor(out[:, :, lo:hi], src[:, :, lo:hi],
                                               mean1[:, :].unsqueeze(2).to_broadcast(spread), ALU.subtract))
                        src = out
                    link(dve.tensor_tensor(square[:, :, lo:hi], src[:, :, lo:hi], src[:, :, lo:hi], ALU.mult))
                    link(dve.tensor_reduce(var[:, :], square[:, :, lo:hi], AX, ALU.add))
                    link(dve.tensor_scalar(var1[:, :], var[:, :], 1.0 / divisor, EPS, ALU.mult, ALU.add))
                    dve.sem_inc(varied, 1)
                    dve.wait_ge(rooted, n + 1)
                    link(dve.reciprocal(inv[:, :], dev[:, :]))
                    link(dve.tensor_tensor(out[:, :, lo:hi], src[:, :, lo:hi],
                                           inv[:, :].unsqueeze(2).to_broadcast(spread), ALU.mult))

            @block.scalar
            def _(act):
                for n in range(len(groups)):
                    act.wait_ge(varied, n + 1)
                    act.activation(dev[:, :], var1[:, :], ACT.Sqrt).then_inc(rooted, 1)


def attention_input(nc, g):
    with ExitStack() as ctx:
        normed = ctx.enter_context(nc.sbuf_tensor("normed", [P, BLOCKS, C], F32))
        normalise(nc, g, "ln0", [(g["nodes"], 0, CS, CS, True), (g["nodes"], CS, C, CV, False)], normed)
        node_tables(nc, g, "tab0", normed, "ts0", "tv0", ("gamma_s", "beta_s", "gamma_v"),
                    [g["tab_src"], g["tab_dst"]], None)


def attention_edges(nc, g):
    w, psum, banks, io = g["w"], g["psum"], g["banks"], g["io"]
    with ExitStack() as ctx:
        def sb(name, shape, dt=F32):
            return ctx.enter_context(nc.sbuf_tensor(f"ae_{name}", shape, dt))

        def sem(name):
            return ctx.enter_context(nc.semaphore(f"ae_{name}"))
        idx = [sb(f"idx{u}", [P, 8], I32) for u in range(4)]
        y = [sb(f"y{u}", [P, 4, 5]) for u in range(4)]
        sigma = [sb(f"sigma{u}", [P, 4, P]) for u in range(4)]
        gsrc = [sb(f"gsrc{u}", [P, 4, C]) for u in range(2)]
        gdst = [sb(f"gdst{u}", [P, 4, C]) for u in range(2)]
        rbf = [sb(f"rbf{u}", [80, 512]) for u in range(2)]
        y16 = [sb(f"y16_{u}", [80, 512]) for u in range(2)]
        rbfy = [sb(f"rbfy{u}", [80, 512]) for u in range(2)]
        first = [sb(f"first{u}", [P, 4, 352]) for u in range(2)]
        mapped = [sb(f"mapped{u}", [P, 4, 288]) for u in range(2)]
        rest = [sb(f"rest{u}", [P, 4, 224]) for u in range(2)]
        logit = [sb(f"logit{u}", [P, 16]) for u in range(2)]
        values = [sb(f"values{u}", [P, 4, CV + C]) for u in range(2)]
        msg = sb("msg", [P, 4, C + CV])
        dotted, plus, minus = (sb(x, [P, 4, V3]) for x in ("dotted", "plus", "minus"))
        dotted2, plus2, minus2 = (sb(x, [P, 4, V3]) for x in ("dotted2", "plus2", "minus2"))
        partial, partial2 = sb("partial", [P, 4, CV]), sb("partial2", [P, 4, CV])
        leaky, scored = sb("leaky", [P, 4, CS]), sb("scored", [P, 4, CS])
        path, vsum, vval = sb("path", [P, 4, V3]), sb("vsum", [P, 4, V3]), sb("vval", [P, 4, C - CV])
        path2 = sb("path2", [P, 4, V3])
        first_t = [sb(f"first_t{b}", [P, 512]) for b in range(3)]
        second_t = [sb(f"second_t{b}", [P, 512]) for b in range(3)]
        idx_in, y_in = ([sem(f"{x}{u}") for u in range(4)] for x in ("idx_in", "y_in"))
        rbf_in, gathered, stored = ([sem(f"{x}{u}") for u in range(2)] for x in ("rbf_in", "gathered", "stored"))
        filled, may_gather = sem("filled"), sem("may_gather")
        summed, spread, weighted, dot_part, first_done = (sem(x) for x in (
            "summed", "spread", "weighted", "dot_part", "first_done"))
        leaky_done, path_done, scored_done, vsum_done, logit_done, vval_done, part2_done, dot2_part, rest_done, path2_done, \
            values_done = (sem(x) for x in ("leaky_done", "path_done", "scored_done", "vsum_done", "logit_done", "vval_done",
                                            "part2_done", "dot2_part", "rest_done", "path2_done", "values_done"))
        pe_weights, pe_turned, pe_mapped, pe_turned2, pe_values = (sem(x) for x in (
            "pe_weights", "pe_turned", "pe_mapped", "pe_turned2", "pe_values"))
        kept, mapped_kept, sigma_done, kept2, values_kept, vy_done, logit_kept = (sem(x) for x in (
            "kept", "mapped_kept", "sigma_done", "kept2", "values_kept", "vy_done", "logit_kept"))
        b_w, b_t, b_m = psum[:, 0:2, :], banks[2:4], psum[:, 4:6, :]
        b_h = psum[:, 6:8, :].rearrange("p b (k c) -> p (b k) c", c=256)

        def comps(x):
            return x.rearrange("p k (x c) -> p k x c", c=CV)

        def last(x, count):
            return min(x, count * SUPER) if isinstance(x, int) else x

        with nc.Block() as block:
            @block.sync
            def _(sp):
                def body(m):
                    t = m + 3
                    if t.inside(SUPER):
                        wait(sp, summed, t.n - 3)
                        sp.dma_start(idx[t.slot4][:, :], io["eidx"][t.n]).then_inc(idx_in[t.slot4], 16)
                    t = m + 2
                    if t.inside(SUPER):
                        wait(sp, spread, t.n - 1)
                        sp.dma_start(rbf[t.slot][:, :], io["rbf5"][t.n]).then_inc(rbf_in[t.slot], 16)
                        sp.dma_start(y16[t.slot][0:CS, :], io["y16"][t.n]).then_inc(rbf_in[t.slot], 16)
                    t = m + -4
                    if t.inside(SUPER):
                        sp.wait_ge(values_done, t.n + 1)
                        sp.dma_start(g["h_dram"][t.n].rearrange("p (k c) -> p k c", k=4), values[t.slot][:, :, CV:CV + C])\
                            .then_inc(stored[t.slot], 16)
                    t = m
                    if t.inside(SUPER):
                        wait(sp, path2_done, t.n - 3)
                        wait(sp, vy_done, t.n - 3)
                        sp.dma_start(y[t.slot4][:, :, :].rearrange("p k j -> p (k j)"), io["ey"][t.n]).then_inc(y_in[t.slot4], 16)
                loop(sp, body, -3, SUPER + 4, SUPER)
                for u in range(2):
                    sp.wait_ge(stored[u], 16 * (SUPER // 2))

            @block.gpsimd
            def _(pool):
                def body(t):
                    pool.wait_ge(idx_in[t.slot4], 16 * (t.quarter + 1))
                    wait(pool, summed, t.n - 1)
                    pool.sem_inc(may_gather, 1)
                    for k in range(4):
                        pool.indirect_dma_start(gsrc[t.slot][:, k, :], None, g["tab_src"],
                                                bass.IndirectOffsetOnAxis(ap=idx[t.slot4][:, k:k + 1], axis=0))\
                            .then_inc(gathered[t.slot], 16)
                        pool.indirect_dma_start(gdst[t.slot][:, k, :], None, g["tab_dst"],
                                                bass.IndirectOffsetOnAxis(ap=idx[t.slot4][:, 4 + k:5 + k], axis=0))\
                            .then_inc(gathered[t.slot], 16)
                loop(pool, body, 0, SUPER, SUPER)

            @block.vector
            def _(dve):
                dve.memset(y16[0][CS:80, :], 1.0)
                dve.memset(y16[1][CS:80, :], 1.0)
                dve.memset(g["alpha"][:, 4 * SUPER:SCANT, :], 0.0).then_inc(filled, 1)
                dve.wait_ge(filled, 1)

                def products(t, half):
                    ks = slice(2 * half, 2 * half + 2)
                    out, here = first[t.slot][:, ks, :], msg[:, ks, :]
                    dve.wait_ge(pe_weights, 2 * t.n + half + 1)
                    dve.tensor_tensor(out[:, :, 0:P].rearrange("p k (a c) -> p k a c", a=2),
                                      b_w[:, :, 0:P].rearrange("p k (a c) -> p k a c", a=2),
                                      here[:, :, 0:CS].unsqueeze(2).to_broadcast([P, 2, 2, CS]), ALU.mult)
                    dve.tensor_tensor(dotted[:, ks, :], b_w[:, :, P:224], here[:, :, CS:C], ALU.mult)
                    dve.tensor_tensor(comps(out[:, :, 256:352]), comps(here[:, :, CS:C]),
                                      b_w[:, :, 224:256].unsqueeze(2).to_broadcast([P, 2, 3, CV]), ALU.mult)
                    dve.tensor_tensor(plus[:, ks, 0:2 * CV], b_w[:, :, 288:352], here[:, :, CS:CS + 2 * CV], ALU.mult)
                    dve.tensor_tensor(plus[:, ks, 2 * CV:V3], b_w[:, :, 256:288], here[:, :, CS + 2 * CV:C], ALU.mult)
                    dve.tensor_tensor(minus[:, ks, :], b_w[:, :, 256:352], here[:, :, CS + CV:C + CV], ALU.mult)\
                        .then_inc(weighted, 1)

                def body(m):
                    t = m
                    if t.inside(SUPER):
                        dve.wait_ge(summed, t.n + 1)
                        wait(dve, pe_turned, 3 * t.n - 3)
                        wait(dve, first_done, t.n)
                        products(t, 0)
                    t = m + 1
                    if t.inside(SUPER):
                        dve.wait_ge(rbf_in[t.slot], 32 * (t.half + 1))
                        wait(dve, pe_weights, 2 * t.n - 2)
                        dve.tensor_tensor(rbfy[t.slot][:, :], rbf[t.slot][:, :], y16[t.slot][:, :], ALU.mult)\
                            .then_inc(spread, 1)
                    t = m + -2
                    if t.inside(SUPER):
                        here = mapped[t.slot]
                        yx = y[t.slot4][:, :, 1:4].unsqueeze(3).to_broadcast([P, 4, 3, CV])
                        dve.wait_ge(mapped_kept, 2 * t.n + 2)
                        dve.wait_ge(y_in[t.slot4], 16 * (t.quarter + 1))
                        wait(dve, scored_done, t.n)
                        dve.scalar_tensor_tensor(leaky[:, :, :], here[:, :, CV:96], 0.2, here[:, :, CV:96], ALU.mult, ALU.max)\
                            .then_inc(leaky_done, 1)
                        wait(dve, vsum_done, t.n)
                        dve.tensor_tensor(comps(path[:, :, :]), here[:, :, 0:CV].unsqueeze(2).to_broadcast([P, 4, 3, CV]), yx,
                                          ALU.mult).then_inc(path_done, 1)
                        dve.wait_ge(leaky_done, t.n + 1)
                        wait(dve, logit_done, t.n)
                        dve.tensor_tensor(scored[:, :, :], leaky[:, :, :], w("adot").unsqueeze(1).to_broadcast([P, 4, CS]),
                                          ALU.mult).then_inc(scored_done, 1)
                        dve.wait_ge(path_done, t.n + 1)
                        wait(dve, vval_done, t.n)
                        dve.tensor_tensor(vsum[:, :, :], path[:, :, :], here[:, :, 192:288], ALU.add).then_inc(vsum_done, 1)
                        dve.wait_ge(scored_done, t.n + 1)
                        wait(dve, logit_kept, t.n - 1)
                        dve.tensor_reduce(logit[t.slot][:, :], scored[:, :, :].rearrange("p k (h a) -> p (k h) a", a=AS), AX, ALU.add)\
                            .then_inc(logit_done, 1)
                        dve.wait_ge(vsum_done, t.n + 1)
                        wait(dve, part2_done, t.n)
                        wait(dve, vy_done, t.n)
                        dve.tensor_tensor(comps(vval[:, :, 0:V3]), comps(vsum[:, :, :]),
                                          here[:, :, 160:192].unsqueeze(2).to_broadcast([P, 4, 3, CV]), ALU.mult)
                        dve.tensor_tensor(vval[:, :, V3:P], vsum[:, :, 0:CV], here[:, :, 160:192], ALU.mult).then_inc(vval_done, 1)
                        dve.wait_ge(vval_done, t.n + 1)
                        wait(dve, rest_done, t.n)
                        vx = comps(vval[:, :, 0:V3])
                        for out, v, at in ((dotted2, vx, 1), (plus2, vx, 2), (minus2, comps(vval[:, :, CV:P]), 1)):
                            ins = dve.tensor_tensor(comps(out[:, :, :]), v,
                                                    y[t.slot4][:, :, at:at + 3].unsqueeze(3).to_broadcast([P, 4, 3, CV]), ALU.mult)
                        ins.then_inc(part2_done, 1)
                    t = m
                    if t.inside(SUPER):
                        products(t, 1)
                    t = m
                    if t.inside(SUPER):
                        dve.wait_ge(weighted, 2 * t.n + 2)
                        dve.tensor_tensor(partial[:, :, :], dotted[:, :, 0:CV], dotted[:, :, CV:2 * CV], ALU.add).then_inc(dot_part, 1)
                        dve.tensor_tensor(first[t.slot][:, :, P:224], plus[:, :, :], minus[:, :, :], ALU.subtract)
                        dve.wait_ge(dot_part, t.n + 1)
                        dve.tensor_tensor(first[t.slot][:, :, 224:256], partial[:, :, :], dotted[:, :, 2 * CV:V3], ALU.add)\
                            .then_inc(first_done, 1)
                    t = m + -2
                    if t.inside(SUPER):
                        dve.wait_ge(part2_done, t.n + 1)
                        wait(dve, pe_turned2, 3 * t.n - 3)
                        dve.tensor_tensor(partial2[:, :, :], dotted2[:, :, 0:CV], dotted2[:, :, CV:2 * CV], ALU.add).then_inc(dot2_part, 1)
                        dve.tensor_tensor(rest[t.slot][:, :, 0:V3], plus2[:, :, :], minus2[:, :, :], ALU.subtract)
                        dve.wait_ge(dot2_part, t.n + 1)
                        dve.tensor_tensor(rest[t.slot][:, :, V3:P], partial2[:, :, :], dotted2[:, :, 2 * CV:V3], ALU.add)\
                            .then_inc(rest_done, 1)
                    t = m + -4
                    if t.inside(SUPER):
                        dve.wait_ge(values_kept, t.n + 1)
                        wait(dve, values_done, t.n)
                        for x in range(3):
                            ins = dve.tensor_tensor(
                                path2[:, :, :].rearrange("p k (h x a) -> p k h x a", h=H, x=3)[:, :, :, x, :],
                                values[t.slot][:, :, 0:CV].rearrange("p k (h a) -> p k h a", h=H),
                                y[t.slot4][:, :, 1 + x:2 + x].unsqueeze(3).to_broadcast([P, 4, H, AV]), ALU.mult)
                        ins.then_inc(path2_done, 1)
                    t = m + 1
                    if t.inside(SUPER):
                        dve.wait_ge(gathered[t.slot], 128 * (t.half + 1))
                        wait(dve, weighted, 2 * t.n)
                        dve.tensor_tensor(msg[:, :, C:C + CV], gsrc[t.slot][:, :, CS:CS + CV], gdst[t.slot][:, :, CS:CS + CV], ALU.add)
                        dve.tensor_tensor(msg[:, :, 0:C], gsrc[t.slot][:, :, :], gdst[t.slot][:, :, :], ALU.add).then_inc(summed, 1)
                    t = m + -4
                    if t.inside(SUPER):
                        dve.wait_ge(path2_done, t.n + 1)
                        vectors = values[t.slot][:, :, 96:192]
                        dve.tensor_tensor(vectors, vectors, path2[:, :, :], ALU.add)\
                            .then_inc(values_done, 1)
                loop(dve, body, -1, SUPER + 4, SUPER)

            @block.tensor
            def _(pe):
                def weights(t, half, i):
                    e = P * (2 * half + i)
                    return pe.matmul(b_w[:, i, 0:352], rbfy[t.slot][:, e:e + P], w("wy"), start=True, stop=True)

                def turn(t, b):
                    lo, rows = P * b, V3 if b == 2 else P
                    for k in range(4):
                        ins = pe.transpose(b_t[b % 2][0:rows, P * k:P * k + P], first[t.slot][:, k, lo:lo + rows], w("ident"))
                    ins.then_inc(pe_turned, 1)

                def turn2(t, b):
                    what = sigma[t.slot4][:, :, :] if b == 0 else rest[t.slot][:, :, 0:P] if b == 1 else rest[t.slot][:, :, P:224]
                    rows = V3 if b == 2 else P
                    for k in range(4):
                        ins = pe.transpose(b_t[(b + 1) % 2][0:rows, P * k:P * k + P], what[:, k, :], w("ident"))
                    ins.then_inc(pe_turned2, 1)

                def maps(t, half):
                    wait(pe, mapped_kept, 2 * t.n + half)
                    for i in range(2):
                        e = slice(P * (2 * half + i), P * (2 * half + i) + P)
                        pe.matmul(b_m[:, i, 0:288], first_t[1][:, e], w("m1_1"), start=True, stop=False)
                        pe.matmul(b_m[:, i, 0:192], first_t[0][:, e], w("m1_0"), start=False, stop=False)
                        ins = pe.matmul(b_m[:, i, 192:288], first_t[2][0:V3, e], w("m1_2"), start=False, stop=True)
                    ins.then_inc(pe_mapped, 1)

                def body(m):
                    t = m + -1
                    if t.inside(SUPER):
                        pe.wait_ge(first_done, t.n + 1)
                        for b in range(2):
                            wait(pe, kept2, 3 * t.n - 7 + b)
                            turn(t, b)
                    t = m
                    if t.inside(SUPER):
                        pe.wait_ge(weighted, 2 * t.n + 1)
                        weights(t, 1, 0)
                    t = m + -1
                    if t.inside(SUPER):
                        pe.wait_ge(kept, 3 * t.n + 1)
                        turn(t, 2)
                    t = m
                    if t.inside(SUPER):
                        weights(t, 1, 1).then_inc(pe_weights, 1)
                    t = m + -1
                    if t.inside(SUPER):
                        pe.wait_ge(kept, 3 * t.n + 3)
                        maps(t, 0)
                    t = m + -3
                    if t.inside(SUPER):
                        for b, done in enumerate((sigma_done, rest_done)):
                            pe.wait_ge(done, t.n + 1)
                            pe.wait_ge(kept, last(3 * t.n + 8 + b, 3))
                            turn2(t, b)
                    t = m + 1
                    if t.inside(SUPER):
                        pe.wait_ge(spread, t.n + 1)
                        wait(pe, weighted, 2 * t.n)
                        weights(t, 0, 0)
                        weights(t, 0, 1).then_inc(pe_weights, 1)
                    t = m + -3
                    if t.inside(SUPER):
                        pe.wait_ge(vy_done, t.n + 1)
                        pe.wait_ge(kept2, 3 * t.n + 1)
                        turn2(t, 2)
                    t = m + -1
                    if t.inside(SUPER):
                        maps(t, 1)
                    t = m + -3
                    if t.inside(SUPER):
                        pe.wait_ge(kept2, 3 * t.n + 3)
                        wait(pe, values_kept, t.n)
                        for k in range(4):
                            out, e = b_h[:, k, :], slice(P * k, P * k + P)
                            pe.matmul(out[:, 0:192], second_t[1][:, e], w("m2_1"), start=True, stop=False)
                            pe.matmul(out[:, 0:96], second_t[0][:, e], w("m2_0"), start=False, stop=False)
                            ins = pe.matmul(out[:, 96:192], second_t[2][0:V3, e], w("m2_2"), start=False, stop=True)
                        ins.then_inc(pe_values, 1)
                loop(pe, body, -1, SUPER + 3, SUPER)

            @block.scalar
            def _(act):
                def keep_maps(t, half):
                    ks = slice(2 * half, 2 * half + 2)
                    act.wait_ge(pe_mapped, 2 * t.n + half + 1)
                    act.activation(mapped[t.slot][:, ks, 0:96], b_m[:, :, 0:96], ACT.Copy)
                    act.activation(mapped[t.slot][:, ks, 192:288], b_m[:, :, 192:288], ACT.Copy)
                    act.activation(sigma[t.slot4][:, ks, 0:CS], b_m[:, :, 96:160], ACT.Sigmoid)
                    act.activation(mapped[t.slot][:, ks, 160:192], b_m[:, :, 160:192], ACT.Sigmoid).then_inc(mapped_kept, 1)

                def keep1(t, b):
                    rows = V3 if b == 2 else P
                    act.wait_ge(pe_turned, 3 * t.n + b + 1)
                    act.activation(first_t[b][0:rows, :], b_t[b % 2][0:rows, :], ACT.Copy).then_inc(kept, 1)

                def keep2(t, b):
                    rows = V3 if b == 2 else P
                    act.wait_ge(pe_turned2, 3 * t.n + b + 1)
                    act.activation(second_t[b][0:rows, :], b_t[(b + 1) % 2][0:rows, :], ACT.Copy).then_inc(kept2, 1)

                def body(m):
                    t = m + -1
                    if t.inside(SUPER):
                        wait(act, pe_mapped, 2 * t.n)
                        for b in range(3):
                            keep1(t, b)
                    t = m + -4
                    if t.inside(SUPER):
                        act.wait_ge(pe_values, t.n + 1)
                        wait(act, stored[t.slot], 16 * t.half)
                        act.activation(values[t.slot][:, :, :], b_h[:, :, 0:192], ACT.Copy).then_inc(values_kept, 1)
                    t = m + -1
                    if t.inside(SUPER):
                        wait(act, vval_done, t.n - 1)
                        wait(act, leaky_done, t.n - 1)
                        wait(act, pe_turned2, 3 * t.n - 9)
                        keep_maps(t, 0)
                    t = m + -3
                    if t.inside(SUPER):
                        wait(act, pe_values, t.n)
                        for b in range(3):
                            keep2(t, b)
                    t = m + -1
                    if t.inside(SUPER):
                        keep_maps(t, 1)
                    t = m + -1
                    if t.inside(SUPER):
                        act.wait_ge(y_in[t.slot4], 16 * (t.quarter + 1))
                        act.wait_ge(mapped_kept, 2 * t.n + 2)
                        for k in range(4):
                            ins = act.activation(sigma[t.slot4][:, k, CS:P], sigma[t.slot4][:, k, 0:CS], ACT.Identity,
                                                 scale=y[t.slot4][:, k, 0:1])
                        ins.then_inc(sigma_done, 1)
                    t = m + -2
                    if t.inside(SUPER):
                        act.wait_ge(vval_done, t.n + 1)
                        act.wait_ge(y_in[t.slot4], 16 * (t.quarter + 1))
                        wait(act, pe_turned2, 3 * t.n - 3)
                        for k in range(4):
                            ins = act.activation(rest[t.slot][:, k, P:224], vval[:, k, 0:V3], ACT.Identity,
                                                 scale=y[t.slot4][:, k, 0:1])
                        ins.then_inc(vy_done, 1)
                        act.wait_ge(logit_done, t.n + 1)
                        act.activation(g["alpha"][:, bass.ds(4 * t.n, 4), :].rearrange("p k h -> p (k h)"),
                                       logit[t.slot][:, :], ACT.Copy).then_inc(logit_kept, 1)
                loop(act, body, 0, SUPER + 4, SUPER)


def segment_softmax(nc, g):
    w, banks, io, alpha = g["w"], g["banks"], g["io"], g["alpha"]
    with ExitStack() as ctx:
        def sb(name, shape, dt=F32):
            return ctx.enter_context(nc.sbuf_tensor(f"sm_{name}", shape, dt))

        def sem(name):
            return ctx.enter_context(nc.semaphore(f"sm_{name}"))
        logit = sb("logit", [P, H, SCANT])
        forward = sb("forward", [P, H, SCANT])
        backward = alpha[:, :, :].rearrange("p t h -> p (t h)").rearrange("p (h t) -> p h t", h=H)
        dst = [sb(f"dst{i}", [P, SCANT], I32) for i in range(3)]
        gate = sb("gate", [P, 2, SCANT])
        whole, whole4 = sb("whole", [P, 2]), sb("whole4", [P, 2, H])
        ends = sb("ends", [P, 2, H])
        rows = sb("rows", [H, 2, 2, P])
        carry = sb("carry", [H, 2, P + 2])
        first = sb("first", [P, 2, H])
        loaded, turned, kept, chain, ended, swapped, carried, returned, shifted, exped, back, back_kept = (
            sem(x) for x in ("loaded", "turned", "kept", "chain", "ended", "swapped", "carried", "returned",
                             "shifted", "exped", "back", "back_kept"))
        groups = [(h, j, min(4, SCANG - 4 * j)) for h in range(H) for j in range(-(-SCANG // 4))]
        by_group = alpha[:, :, :].rearrange("p (q g) h -> p h g q", g=SCANG)

        with nc.Block() as block:
            @block.sync
            def _(sp):
                for i in range(3):
                    sp.dma_start(dst[i][:, :], io["dst3"][i]).then_inc(loaded, 16)

            @block.tensor
            def _(pe):
                for n, (h, j, cnt) in enumerate(groups):
                    wait(pe, kept, n - 3)
                    for i in range(cnt):
                        ins = pe.transpose(banks[n % 4][:, P * i:P * i + P], by_group[:, h, 4 * j + i, :], w("ident"))
                    ins.then_inc(turned, 1)
                for d in range(2):
                    pe.wait_ge(ended, d + 1)
                    pe.transpose(banks[4][0:H, 0:P], ends[:, d, :], w("ident"))
                    pe.transpose(banks[4][0:H, P:2 * P], whole4[:, d, :], w("ident")).then_inc(swapped, 1)
                    pe.wait_ge(carried, d + 1)
                    pe.transpose(banks[5][:, 0:H], carry[0:H, d, 2 * d:2 * d + P], w("ident")[0:H, 0:H]).then_inc(returned, 1)
                for n, (h, j, cnt) in enumerate(groups):
                    pe.wait_ge(exped, h + 1)
                    wait(pe, back_kept, n - 3)
                    for i in range(cnt):
                        at = P * (4 * j + i)
                        ins = pe.transpose(banks[n % 4][:, P * i:P * i + P], logit[:, h, at:at + P], w("ident"))
                    ins.then_inc(back, 1)

            @block.scalar
            def _(act):
                for n, (h, j, cnt) in enumerate(groups):
                    act.wait_ge(turned, n + 1)
                    act.activation(logit[:, h, 512 * j:512 * j + P * cnt], banks[n % 4][:, 0:P * cnt], ACT.Copy).then_inc(kept, 1)
                act.wait_ge(shifted, 1)
                for h in range(H):
                    act.activation(logit[:, h, :], logit[:, h, :], ACT.Exp).then_inc(exped, 1)
                for n, (h, j, cnt) in enumerate(groups):
                    act.wait_ge(back, n + 1)
                    act.activation(by_group[:, h, 4 * j:4 * j + cnt, :],
                                   banks[n % 4][:, 0:P * cnt].rearrange("p (g q) -> p g q", q=P), ACT.Copy).then_inc(back_kept, 1)

            @block.vector
            def _(dve):
                links = [0]

                def link(ins):
                    links[0] += 1
                    ins.then_inc(chain, 1)
                    dve.wait_ge(chain, links[0])

                dve.memset(carry[:, :, :], -BIG)
                dve.wait_ge(loaded, 48)
                for d in range(2):
                    ins = dve.tensor_tensor(gate[:, d, :], dst[0][:, :], dst[1 + d][:, :], ALU.is_equal)
                link(ins)
                link(dve.tensor_scalar(gate[:, :, :], gate[:, :, :], 2 * BIG, -BIG, ALU.mult, ALU.add))
                link(dve.tensor_reduce(whole[:, :], gate[:, :, :], AX, ALU.min))
                link(dve.tensor_copy(whole4[:, :, :], whole[:, :].unsqueeze(2).to_broadcast([P, 2, H])))
                dve.wait_ge(kept, len(groups))
                for d, (out, data) in enumerate(((forward, logit), (backward, forward))):
                    def flip(x):
                        return x[:, ::-1] if d else x

                    def scans(initial):
                        for h in range(H):
                            ins = dve.tensor_tensor_scan(flip(out[:, h, :]), flip(gate[:, d, :]), flip(data[:, h, :]),
                                                         initial(h), ALU.min, ALU.max)
                        return ins
                    link(scans(lambda h: -BIG))
                    dve.tensor_copy(ends[:, d, :], out[:, :, 0 if d else SCANT - 1]).then_inc(ended, 1)
                    dve.wait_ge(swapped, d + 1)
                    link(dve.tensor_copy(rows[:, d, :, :], banks[4][0:H, 0:2 * P].rearrange("p (a q) -> p a q", a=2)))
                    dve.tensor_tensor_scan(flip(carry[:, d, 1:P + 1]), flip(rows[:, d, 1, :]), flip(rows[:, d, 0, :]),
                                           -BIG, ALU.min, ALU.max).then_inc(carried, 1)
                    dve.wait_ge(returned, d + 1)
                    link(dve.tensor_copy(first[:, d, :], banks[5][:, 0:H]))
                    link(scans(lambda h: first[:, d, h:h + 1]))
                dve.tensor_tensor(logit[:, :, :], logit[:, :, :], backward, ALU.subtract).then_inc(shifted, 1)


def step_loads(sp, at, table, free, loads):
    s = sp.value_load(table[0:1, bass.ds(at.n, 1)], min_val=0, max_val=SUPER - 1)
    for sem, value in free:
        wait(sp, sem, value)
    for out, src, sem in loads:
        sp.dma_start(out, src[bass.ds(s, 1)].rearrange("a p c -> (a p) c")).then_inc(sem, 16)


def attention_aggregate(nc, g):
    w, banks, io, agg = g["w"], g["banks"], g["io"], g["agg"]
    W = C + H
    with ExitStack() as ctx:
        def sb(name, shape, dt=F32):
            return ctx.enter_context(nc.sbuf_tensor(f"ag_{name}", shape, dt))

        def sem(name):
            return ctx.enter_context(nc.semaphore(f"ag_{name}"))
        dst, dst_f = sb("dst", [P, 4 * SUPER], I32), sb("dst_f", [P, 4 * SUPER])
        val = [sb(f"val{u}", [P, 4, C]) for u in range(4)]
        exval = [sb(f"exval{u}", [P, 4, W]) for u in range(2)]
        rel = [sb(f"rel{u}", [P, 4]) for u in range(2)]
        hot = [sb(f"hot{u}", [P, 4, P]) for u in range(2)]
        loaded = [sem(f"loaded{u}") for u in range(4)]
        dst_in, zeroed, rel_done, ready, weighted, summed, added = (sem(x) for x in (
            "dst_in", "zeroed", "rel_done", "ready", "weighted", "summed", "added"))
        with nc.Block() as block:
            @block.sync
            def _(sp):
                sp.dma_start(dst[:, :], io["dst"]).then_inc(dst_in, 16)

                def body(t):
                    step_loads(sp, t, g["step_s"], ((weighted, t.n - 3),),
                               ((val[t.slot4][:, :, :].rearrange("p k c -> p (k c)"), g["h_dram"], loaded[t.slot4]),))
                loop(sp, body, 0, STEPS, STEPS)

            @block.gpsimd
            def _(pool):
                pool.wait_ge(zeroed, 1)

                def body(t):
                    s = pool.value_load(g["step_s"][0:1, bass.ds(t.n, 1)], min_val=0, max_val=SUPER - 1)
                    ex = g["alpha"][:, bass.ds(4 * s, 4), :]
                    wait(pool, ready, t.n - 1)
                    pool.tensor_tensor(rel[t.slot][:, :], dst_f[:, bass.ds(4 * s, 4)],
                                       g["block128"][:, bass.ds(t.n, 1)].to_broadcast([P, 4]), ALU.subtract).then_inc(rel_done, 1)
                    pool.wait_ge(loaded[t.slot4], 16 * (t.quarter + 1))
                    wait(pool, summed, t.n - 1)
                    for lo, hi in ((0, CS), (CS, C)):
                        pool.tensor_tensor(exval[t.slot][:, :, lo:hi].rearrange("p k (h c) -> p k h c", h=H),
                                           val[t.slot4][:, :, lo:hi].rearrange("p k (h c) -> p k h c", h=H),
                                           ex.unsqueeze(3).to_broadcast([P, 4, H, (hi - lo) // H]), ALU.mult)
                    pool.tensor_copy(exval[t.slot][:, :, C:W], ex).then_inc(weighted, 1)
                loop(pool, body, 0, STEPS, STEPS)

            @block.vector
            def _(dve):
                dve.memset(agg[:, :, :], 0.0)
                dve.wait_ge(dst_in, 16)
                dve.tensor_copy(dst_f[:, :], dst[:, :]).then_inc(zeroed, 1)
                dve.wait_ge(zeroed, 1)

                def body(m):
                    t = m
                    if t.inside(STEPS):
                        dve.wait_ge(rel_done, t.n + 1)
                        wait(dve, summed, t.n - 1)
                        dve.tensor_tensor(hot[t.slot][:, :, :], w("iota").unsqueeze(1).to_broadcast([P, 4, P]),
                                          rel[t.slot][:, :].unsqueeze(2).to_broadcast([P, 4, P]), ALU.is_equal).then_inc(ready, 1)
                    t = m + -1
                    if t.inside(STEPS):
                        b = dve.value_load(g["step_b"][0:1, bass.ds(t.n, 1)], min_val=0, max_val=BLOCKS - 1)
                        there = agg[:, bass.ds(b, 1), :].rearrange("p a c -> p (a c)")
                        dve.wait_ge(summed, t.n + 1)
                        wait(dve, added, t.n)
                        dve.tensor_tensor(there, there, banks[t.slot][:, 0:W], ALU.add).then_inc(added, 1)
                loop(dve, body, 0, STEPS + 1, STEPS)

            @block.tensor
            def _(pe):
                def body(t):
                    pe.wait_ge(ready, t.n + 1)
                    pe.wait_ge(weighted, t.n + 1)
                    wait(pe, added, t.n - 1)
                    for k in range(4):
                        ins = pe.matmul(banks[t.slot][:, 0:W], hot[t.slot][:, k, :], exval[t.slot][:, k, :],
                                        start=(k == 0), stop=(k == 3))
                    ins.then_inc(summed, 1)
                loop(pe, body, 0, STEPS, STEPS)


def node_update(nc, g, tag, columns, pick, chunks, base, factor):
    w, banks = g["w"], g["banks"]
    with ExitStack() as ctx:
        row = [ctx.enter_context(nc.sbuf_tensor(f"{tag}_row{u}", [P, columns], F32)) for u in range(2)]
        feat = [ctx.enter_context(nc.sbuf_tensor(f"{tag}_feat{u}", [P, len(chunks), P], F32)) for u in range(2)]
        picked, turned, kept, mapped, added = (ctx.enter_context(nc.semaphore(f"{tag}_{x}")) for x in (
            "picked", "turned", "kept", "mapped", "added"))
        tall = max(cols for _, cols, *_ in chunks)
        b_t, b_o = banks[0:2], banks[2:4]
        with nc.Block() as block:
            @block.vector
            def _(dve):
                def body(m):
                    t = m + 1
                    if t.inside(BLOCKS):
                        wait(dve, turned, t.n - 1)
                        pick(dve, row[t.slot], t.n).then_inc(picked, 1)
                    t = m
                    if t.inside(BLOCKS):
                        there = base[:, bass.ds(t.n, 1), :].rearrange("p a c -> p (a c)")
                        dve.wait_ge(mapped, t.n + 1)
                        dve.scalar_tensor_tensor(there, there, factor, b_o[t.slot][:, 0:C], ALU.mult, ALU.add).then_inc(added, 1)
                loop(dve, body, -1, BLOCKS, BLOCKS)

            @block.tensor
            def _(pe):
                def body(m):
                    t = m + 1
                    if t.inside(BLOCKS):
                        pe.wait_ge(picked, t.n + 1)
                        wait(pe, kept, t.n - 1)
                        for i, (lo, *_) in enumerate(chunks):
                            ins = pe.transpose(b_t[t.slot][0:tall, P * i:P * i + P], row[t.slot][:, lo:lo + tall], w("ident"))
                        ins.then_inc(turned, 1)
                    t = m
                    if t.inside(BLOCKS):
                        pe.wait_ge(kept, t.n + 1)
                        wait(pe, added, t.n - 1)
                        for i, (_, cols, weights, lo, width) in enumerate(chunks):
                            ins = pe.matmul(b_o[t.slot][:, lo:lo + width], feat[t.slot][0:cols, i, :], w(weights),
                                            start=True, stop=True)
                        ins.then_inc(mapped, 1)
                loop(pe, body, -1, BLOCKS, BLOCKS)

            @block.scalar
            def _(act):
                def body(t):
                    act.wait_ge(turned, t.n + 1)
                    wait(act, mapped, t.n - 1)
                    act.activation(feat[t.slot][0:tall, :, :].rearrange("p i q -> p (i q)"), b_t[t.slot][0:tall, 0:P * len(chunks)],
                                   ACT.Copy).then_inc(kept, 1)
                loop(act, body, 0, BLOCKS, BLOCKS)


def attention_output(nc, g):
    agg, nodes = g["agg"], g["nodes"]
    with ExitStack() as ctx:
        den = ctx.enter_context(nc.sbuf_tensor("den", [P, BLOCKS, H], F32))
        rden = ctx.enter_context(nc.sbuf_tensor("rden", [P, BLOCKS, H], F32))
        chain = ctx.enter_context(nc.semaphore("den_chain"))
        with nc.Block() as block:
            @block.vector
            def _(dve):
                dve.tensor_scalar(den[:, :, :], agg[:, :, C:C + H], 1e-16, None, ALU.add).then_inc(chain, 1)
                dve.wait_ge(chain, 1)
                dve.reciprocal(rden[:, :, :], den[:, :, :]).then_inc(chain, 1)
                dve.wait_ge(chain, 2)
                for lo, hi in ((0, CS), (CS, C)):
                    heads = agg[:, :, lo:hi].rearrange("p b (h c) -> p b h c", h=H)
                    ins = dve.tensor_tensor(heads, heads, rden[:, :, :].unsqueeze(3).to_broadcast([P, BLOCKS, H, (hi - lo) // H]),
                                            ALU.mult)
                ins.then_inc(chain, 1)

    def pick(dve, row, b):
        return dve.tensor_copy(row[:, :], agg[:, bass.ds(b, 1), 0:C].rearrange("p a c -> p (a c)"))
    node_update(nc, g, "upd0", C, pick, [(0, CS, "wps", 0, CS), (CS, V3, "wpv", CS, V3)], nodes, 2.0)
    normalise(nc, g, "ln1", [(nodes, 0, C, C, True)], nodes)
    node_tables(nc, g, "tab1", nodes, "ts1", "tv1", None, [g["tab_conv"]], nodes)


def conv_edges(nc, g):
    w, psum, io, agg = g["w"], g["psum"], g["io"], g["agg"]
    WW = 224
    with ExitStack() as ctx:
        def sb(name, shape, dt=F32):
            return ctx.enter_context(nc.sbuf_tensor(f"ce_{name}", shape, dt))

        def sem(name):
            return ctx.enter_context(nc.semaphore(f"ce_{name}"))
        idx = [sb(f"idx{u}", [P, 8], I32) for u in range(4)]
        y = [sb(f"y{u}", [P, 20]) for u in range(4)]
        query = [sb(f"query{u}", [P, 512]) for u in range(4)]
        node = [sb(f"node{u}", [P, 4, C5]) for u in range(2)]
        rel = [sb(f"rel{u}", [P, 4]) for u in range(2)]
        prod = [sb(f"prod{u}", [P, 4, 4 * C]) for u in range(2)]
        plain = [sb(f"plain{u}", [P, 4, P]) for u in range(2)]
        hot = [sb(f"hot{j}", [P, 4, P]) for j in range(4)]
        idx_in, loaded = ([sem(f"{x}{u}") for u in range(4)] for x in ("idx_in", "loaded"))
        gathered = [sem(f"gathered{u}") for u in range(2)]
        may_gather, zeroed, rel_done, plain_done, hot_done, prod_done, weights, summed, added = (sem(x) for x in (
            "may_gather", "zeroed", "rel_done", "plain_done", "hot_done", "prod_done", "weights", "summed", "added"))
        b_w = [psum[:, 2 * u:2 * u + 2, :].rearrange("p b (k c) -> p (b k) c", k=2)[:, :, 0:WW] for u in range(2)]
        b_0 = [psum[:, 4 + 2 * u, 0:C] for u in range(2)]
        b_y = [psum[:, 5 + 2 * u, 0:3 * C].rearrange("p (x c) -> p x c", x=3) for u in range(2)]
        with nc.Block() as block:
            @block.sync
            def _(sp):
                def body(t):
                    step_loads(sp, t, g["step_s"], ((summed, 4 * t.n - 12),),
                               ((idx[t.slot4][:, :], io["eidx"], idx_in[t.slot4]), (y[t.slot4][:, :], io["ey"], loaded[t.slot4]),
                                (query[t.slot4][0:CS, :], io["query"], loaded[t.slot4])))
                loop(sp, body, 0, STEPS, STEPS)

            @block.gpsimd
            def _(pool):
                def body(t):
                    pool.wait_ge(idx_in[t.slot4], 16 * (t.quarter + 1))
                    wait(pool, prod_done, t.n - 1)
                    pool.sem_inc(may_gather, 1)
                    for k in range(4):
                        pool.indirect_dma_start(node[t.slot][:, k, :], None, g["tab_conv"],
                                                bass.IndirectOffsetOnAxis(ap=idx[t.slot4][:, k:k + 1], axis=0))\
                            .then_inc(gathered[t.slot], 16)
                loop(pool, body, 0, STEPS, STEPS)

            @block.vector
            def _(dve):
                dve.memset(agg[:, :, :], 0.0)
                for u in range(4):
                    ins = dve.memset(query[u][CS:P, :], 0.0)
                ins.then_inc(zeroed, 1)
                dve.wait_ge(zeroed, 1)

                def body(m):
                    t = m + 1
                    if t.inside(STEPS):
                        dve.wait_ge(idx_in[t.slot4], 16 * (t.quarter + 1))
                        wait(dve, plain_done, t.n - 1)
                        dve.tensor_scalar(rel[t.slot][:, :], idx[t.slot4][:, 4:8], g["block128"][:, bass.ds(t.n, 1)], None,
                                          ALU.subtract).then_inc(rel_done, 1)
                        dve.wait_ge(rel_done, t.n + 1)
                        wait(dve, hot_done, 4 * t.n - 4)
                        dve.tensor_tensor(plain[t.slot][:, :, :], w("iota").unsqueeze(1).to_broadcast([P, 4, P]),
                                          rel[t.slot][:, :].unsqueeze(2).to_broadcast([P, 4, P]), ALU.is_equal)\
                            .then_inc(plain_done, 1)
                    t = m
                    if t.inside(STEPS):
                        dve.wait_ge(gathered[t.slot], 64 * (t.half + 1))
                        dve.wait_ge(weights, t.n + 1)
                        wait(dve, summed, 4 * t.n - 4)
                        bank, here, there = b_w[t.slot], node[t.slot], prod[t.slot]
                        scalars, vectors = here[:, :, 0:CS], here[:, :, CS:C].rearrange("p k (x c) -> p k x c", x=3)
                        dve.tensor_tensor(there[:, :, 0:CS], bank[:, :, 0:CS], scalars, ALU.mult)
                        dve.tensor_tensor(there[:, :, CS:C].rearrange("p k (x c) -> p k x c", x=3), vectors,
                                          bank[:, :, 128:160].unsqueeze(2).to_broadcast([P, 4, 3, CV]), ALU.mult)
                        dve.tensor_tensor(there[:, :, C:4 * C].rearrange("p k (x c) -> p k x c", x=3)[:, :, :, 0:CS],
                                          bank[:, :, CS:128].unsqueeze(2).to_broadcast([P, 4, 3, CS]),
                                          scalars.unsqueeze(2).to_broadcast([P, 4, 3, CS]), ALU.mult)
                        for x in range(3):
                            dve.tensor_tensor(there[:, :, C * x + C + CS:C * x + C + 128], bank[:, :, 160:WW],
                                              here[:, :, CS + CV * x:CS + CV * x + 2 * CV], ALU.mult)
                        dve.tensor_tensor(there[:, :, C:4 * C].rearrange("p k (x c) -> p k x c", x=3)[:, :, :, 128:C],
                                          bank[:, :, 192:WW].unsqueeze(2).to_broadcast([P, 4, 3, CV]),
                                          here[:, :, 128:C5].rearrange("p k (x c) -> p k x c", x=3), ALU.mult).then_inc(prod_done, 1)
                    t = m + -1
                    if t.inside(STEPS):
                        b = dve.value_load(g["step_b"][0:1, bass.ds(t.n, 1)], min_val=0, max_val=BLOCKS - 1)
                        there = agg[:, bass.ds(b, 1), :].rearrange("p a c -> p (a c)")
                        dve.wait_ge(summed, 4 * t.n + 4)
                        wait(dve, added, 3 * t.n)
                        dve.tensor_tensor(there[:, 0:C], there[:, 0:C], b_0[t.slot], ALU.add).then_inc(added, 1)
                        a13 = there[:, C5:512].rearrange("p (x c) -> p x c", x=3)
                        dve.tensor_tensor(a13, a13, b_y[t.slot][:, :, 0:96], ALU.add)
                        dve.wait_ge(added, 3 * t.n + 1)
                        plus = there[:, 96:192].rearrange("p (x c) -> p x c", x=3)
                        dve.tensor_tensor(plus, plus, b_y[t.slot][:, :, 128:C], ALU.add).then_inc(added, 1)
                        dve.wait_ge(added, 3 * t.n + 2)
                        minus = there[:, 128:224].rearrange("p (x c) -> p x c", x=3)
                        dve.tensor_tensor(minus, minus, b_y[t.slot][:, :, 96:128], ALU.subtract).then_inc(added, 1)
                loop(dve, body, -1, STEPS + 1, STEPS)

            @block.scalar
            def _(act):
                def body(t):
                    act.wait_ge(plain_done, t.n + 1)
                    act.wait_ge(loaded[t.slot4], 32 * (t.quarter + 1))
                    for j in range(4):
                        wait(act, summed, 4 * t.n - 3 + j)
                        for k in range(4):
                            ins = act.activation(hot[j][:, k, :], plain[t.slot][:, k, :], ACT.Identity,
                                                 scale=y[t.slot4][:, 5 * k + j:5 * k + j + 1])
                        ins.then_inc(hot_done, 1)
                loop(act, body, 0, STEPS, STEPS)

            @block.tensor
            def _(pe):
                pe.wait_ge(zeroed, 1)

                def body(m):
                    t = m + 1
                    if t.inside(STEPS):
                        pe.wait_ge(loaded[t.slot4], 32 * (t.quarter + 1))
                        wait(pe, prod_done, t.n - 1)
                        for k in range(4):
                            ins = pe.matmul(b_w[t.slot][:, k, :], query[t.slot4][:, P * k:P * k + P], w("tp"),
                                            start=True, stop=True)
                        ins.then_inc(weights, 1)
                    t = m
                    if t.inside(STEPS):
                        pe.wait_ge(prod_done, t.n + 1)
                        wait(pe, added, 3 * t.n - 3)
                        for j in range(4):
                            pe.wait_ge(hot_done, 4 * t.n + j + 1)
                            for k in range(4):
                                ins = pe.matmul(b_y[t.slot][:, j - 1, :] if j else b_0[t.slot], hot[j][:, k, :],
                                                prod[t.slot][:, k, C * j:C * j + C], start=(k == 0), stop=(k == 3),
                                                skip_group_check=True)
                            ins.then_inc(summed, 1)
                loop(pe, body, -1, STEPS, STEPS)


def conv_output(nc, g):
    nodes, agg = g["nodes"], g["agg"]
    with nc.semaphore("folded") as folded:
        with nc.Block() as block:
            @block.vector
            def _(dve):
                dve.tensor_tensor(agg[:, :, 64:128], agg[:, :, 64:128], agg[:, :, 160:224], ALU.add)
                dve.tensor_tensor(agg[:, :, 288:320], agg[:, :, 288:320], agg[:, :, 384:416], ALU.add).then_inc(folded, 1)
                dve.wait_ge(folded, 1)
                dve.tensor_tensor(agg[:, :, 288:320], agg[:, :, 288:320], agg[:, :, 480:512], ALU.add).then_inc(folded, 1)
                dve.wait_ge(folded, 2)

    def pick(dve, row, b):
        there = agg[:, bass.ds(b, 1), :].rearrange("p a c -> p (a c)")
        vectors = row[:, 96:384].rearrange("p (x c) -> p x c", x=3)
        dve.tensor_copy(row[:, 0:CS], there[:, 0:CS])
        dve.tensor_copy(row[:, CS:96], there[:, 288:320])
        dve.tensor_copy(vectors[:, :, 0:CS], there[:, C5:512].rearrange("p (x c) -> p x c", x=3)[:, :, 0:CS])
        return dve.tensor_copy(vectors[:, :, CS:96], there[:, CS:C].rearrange("p (x c) -> p x c", x=3))
    node_update(nc, g, "upd1", 384, pick, [(0, 96, "l2s", 0, CS)] + [(96 + 96 * x, 96, "l2v", CS + CV * x, CV) for x in range(3)],
                nodes, 1.0)
    normalise(nc, g, "ln2", [(nodes, 0, C, C, True)], nodes)
    with nc.semaphore("out_stored") as stored:
        with nc.Block() as block:
            @block.sync
            def _(sp):
                sp.dma_start(g["io"]["out"], nodes[:, :, :]).then_inc(stored, 16)
                sp.wait_ge(stored, 16)


def component_major(a):
    return np.concatenate([a[..., :CS], a[..., CS:].reshape(*a.shape[:-1], CV, 3).swapaxes(-1, -2).reshape(*a.shape[:-1], V3)], -1)


def lay_pack(i):
    W = {name: np.zeros((rows, cols), np.float32) for name, rows, cols in PACK}
    L0 = {k[7:]: np.asarray(v) for k, v in i.items() if k.startswith("L0_gnn_")}
    L1 = {k[7:]: np.asarray(v) for k, v in i.items() if k.startswith("L1_gnn_")}
    W["ident"][:] = np.eye(P)
    W["ones"][:] = 1
    W["iota"][:] = np.arange(P)
    W["count"][:] = np.arange(STEPS)
    W["sidx"][:] = np.arange(4 * P).reshape(4, P).T
    W["ts0"][:, :CS], W["ts0"][:, CS:] = L0["Ws_src"], L0["Ws_dst"]
    W["ts1"][:, :CS], W["ts1"][:, CS:] = L1["lin1_w0"], L1["si_w0"]
    rbf = L0["W_rbf"]
    ss, sv, vs, vv0, vv1 = rbf[:, :64], rbf[:, 64:128], rbf[:, 128:160], rbf[:, 160:192], rbf[:, 192:224]
    for lo, part in ((0, ss), (224, vs)):
        W["wy"][0:16, lo:lo + part.shape[1]] = part
    W["wy"][64:80, 64:128] = sv
    for name in ("gamma_s", "beta_s"):
        W[name][:, 0] = L0[name]
    val, vval = L0["Ws_val"], L0["Wv_val"]
    W["m1_0"][64:128, 0:32], W["m1_0"][0:64, 32:96], W["m1_0"][0:64, 96:160] = vval[0:64], L0["W_alpha"][0:64], val[0:64]
    W["m1_1"][96:128, 32:96], W["m1_1"][96:128, 96:160] = L0["W_alpha"][64:96], val[64:96]
    W["val_0"][:, 0:64], W["val_1"][:, 96:128] = val[0:64].T, val[64:96].T
    W["wg"][:] = L0["Wg"]
    W["adot"][:] = L0["alpha_dot"].reshape(1, 64)
    Wsv, Wvv = L0["Ws_vlin"], L0["Wv_vlin"]
    W["m2_0"][0:64, 0:32], W["m2_0"][64:128, 32:96], W["m2_1"][96:128, 32:96] = Wvv[0:64], Wsv[0:64], Wsv[64:96]
    W["r2_0"][0:64, 0], W["r2_0"][64:128, 0], W["r2_1"][96:128, 0] = L0["w2_sv"], L0["w2_ss"], L0["w2_vv0"]
    heads = {n: W[n][:, -V3:].reshape(-1, H, 3, AV) for n in ("m2_1", "m2_2")}
    for x in range(3):
        r, before = slice(CV * x, CV * x + CV), (x + 2) % 3
        W["tv0"][r, CV * x:CV * x + CV], W["tv0"][r, V3 + CV * x:V3 + CV * x + CV] = L0["Wv_src"], L0["Wv_dst"]
        for at in (x, x + 3)[:2 if x < 2 else 1]:
            W["tv1"][r, CV * at:CV * at + CV] = L1["lin1_w1"]
        W["tv1"][r, 5 * CV + CV * x:5 * CV + CV * x + CV] = L1["si_w1"]
        W["gamma_v"][r, 0] = L0["gamma_v"]
        W["wy"][16 + 16 * x:32 + 16 * x, 128 + CV * x:160 + CV * x] = vv0
        W["wy"][16 + 16 * x:32 + 16 * x, 256 + CV * x:288 + CV * x] = vv1
        W["m1_1"][r, 192 + CV * before:224 + CV * before] = vval[96:128]
        W["m1_2"][r, r] = vval[64:96]
        heads["m2_1"][r, :, before] = Wvv[96:128].reshape(CV, H, AV)
        heads["m2_2"][r, :, x] = Wvv[64:96].reshape(CV, H, AV)
        W["r2_1"][r, 0], W["r2_2"][r, 0] = L0["w2_vv1"], L0["w2_vs"]
        for h in range(H):
            at = VH * h + AV * x
            W["wpv"][at:at + AV, CV * x:CV * x + CV] = L0["Wpv"][AV * h:AV * h + AV]
    for n, part in heads.items():
        W[n][:, -V3:] = part.reshape(-1, V3)
    W["wps"][:] = L0["Wps"]
    tp = L1["tp_weight"]
    W["tp"][0:64] = np.concatenate([tp[:, 0:160], tp[:, 192:224], tp[:, 160:192]], 1)
    W["l2s"][:], W["l2v"][:] = L1["lin2_w0"], L1["lin2_w1"]
    out = np.zeros((P, PACKW), np.float32)
    for name, (rows, at, cols) in PLACE.items():
        out[0:rows, at:at + cols] = W[name].reshape(rows, cols)
    return out


def lay_inputs(i):
    E = SUPER * 512
    x = component_major(np.asarray(i["x"]))
    x = np.pad(x, ((0, BLOCKS * P - NODES), (0, 0))).reshape(BLOCKS, P, C).transpose(1, 0, 2)
    src = np.pad(np.asarray(i["src"]), (0, E - EDGES))
    dst_all = np.pad(np.asarray(i["dst"]), (0, SCANT * P - EDGES), constant_values=NODES)
    dst = dst_all[:E]
    both = np.stack([src.reshape(SUPER, 4, P), dst.reshape(SUPER, 4, P)], 1)
    eidx = both.transpose(0, 3, 1, 2).reshape(SUPER, P, 8)
    far = np.array([FAR], dst.dtype)
    sdst = np.concatenate([far, dst[512::512], np.repeat(far, 512 - SUPER)]).reshape(4, P).T
    no = np.array([-1], dst.dtype)
    dst3 = np.stack([dst_all, np.concatenate([no, dst_all[:-1]]), np.concatenate([dst_all[1:], no])]).reshape(3, P, SCANT)
    y = np.pad(np.asarray(i["edge_attr_4"]), ((0, E - EDGES), (0, 0))).reshape(SUPER, 512, 4)
    ey = y.reshape(SUPER, 4, P, 4)[..., [0, 1, 2, 3, 1]].transpose(0, 2, 1, 3).reshape(SUPER, P, 20)
    yt = y.transpose(0, 2, 1)
    rbf = np.pad(np.asarray(i["edge_attr_16"]), ((0, E - EDGES), (0, 0))).reshape(SUPER, 512, 16).transpose(0, 2, 1)
    query = np.pad(np.asarray(i["edge_attr_64"]), ((0, E - EDGES), (0, 0))).reshape(SUPER, 512, 64).transpose(0, 2, 1)
    return dict(
        pack=lay_pack(i), x=x, eidx=eidx, dst=dst.reshape(4 * SUPER, P).T, sdst=sdst, dst3=dst3, ey=ey,
        rbf5=np.tile(rbf, (1, 5, 1)), y16=np.repeat(yt, 16, axis=1),
        query=query)


def kernel(**inputs):
    import numpy as _np
    import concourse.bacc as _bacc
    from concourse import mybir as _mybir
    from concourse.bass_utils import run_bass_kernel_spmd as _run

    nc = _bacc.Bacc("TRN2", target_bir_lowering=False, num_devices=1)
    arrays, io = {}, {}
    for name, a in lay_inputs(inputs).items():
        a = _np.ascontiguousarray(a)
        arrays[f"in_{name}"] = a
        io[name] = nc.dram_tensor(f"in_{name}", a.shape, _mybir.dt.from_np(a.dtype), kind="ExternalInput").ap()
    io["out"] = nc.dram_tensor("out_nodes", (P, BLOCKS, C), F32, kind="ExternalOutput").ap()
    gnn(nc, io)
    r = _run(nc, [arrays], core_ids=[0])
    got = r.results[0]["out_nodes"]
    got = got.transpose(1, 0, 2).reshape(BLOCKS * P, C)[:NODES]
    return _np.concatenate([got[:, :CS], got[:, CS:].reshape(NODES, 3, CV).swapaxes(1, 2).reshape(NODES, V3)], 1)
```
